# Optimizing a Trainium2 kernel written in Bass

```python
import numpy as np
import jax
import jax.numpy as jnp

def _softmax(x, axis=-1):
    return jax.nn.softmax(x, axis=axis)

def _gelu(x):
    return jax.nn.gelu(x, approximate=True)

def _silu(x):
    return jax.nn.silu(x)

def _sigmoid(x):
    return jax.nn.sigmoid(x)

def _layernorm(x, axis=-1, eps=1e-05):
    m = jnp.mean(x, axis=axis, keepdims=True)
    v = jnp.var(x, axis=axis, keepdims=True)
    return (x - m) / jnp.sqrt(v + eps)

def _scatter_add(tgt, idx, src, axis=0):
    return tgt.at[idx].add(src)

def _segment_sum(src, seg, n):
    return jax.ops.segment_sum(src, seg, n)
kernel_name = 'mk_perceiver_d4_seqx_r8_d2b90f'

def setup_inputs(seed: int=0):
    np.random.seed(seed)
    _w = jnp.asarray

    def _rec_inputs():
        import jax
        import jax.numpy as jnp
        _rk = jax.random.key(seed)
        x = -0.0002928 + 1 * jax.random.normal(jax.random.fold_in(_rk, 1), (4, 128, 128), jnp.float32)
        _lenS = 128 - jax.random.randint(jax.random.fold_in(_rk, 7), (4,), 0, max(1, 128 // 4) + 1, jnp.int32)
        _lenS2 = 2048 - jax.random.randint(jax.random.fold_in(_rk, 8), (4,), 0, max(1, 2048 // 4) + 1, jnp.int32)
        _ctx_1024P = jax.random.normal(jax.random.fold_in(_rk, 11), (4, 16, 128), jnp.float32)
        _ctx_1024c = jax.random.dirichlet(jax.random.fold_in(_rk, 511), 0.3 * jnp.ones((16,), jnp.float32), (4, 2048))
        _ctx_1024t = jnp.einsum('bsk,bkd->bsd', _ctx_1024c, _ctx_1024P)
        _ctx_1024t = _ctx_1024t * jax.lax.rsqrt(jnp.mean(jnp.square(_ctx_1024t)) + 1e-12) * 0.953939
        ctx_1024 = 4.13588e-05 + 0.999923 * (_ctx_1024t + 0.3 * jax.random.normal(jax.random.fold_in(_rk, 611), (4, 2048, 128), jnp.float32))
        itok_BxS_8_8191 = jax.random.randint(jax.random.fold_in(_rk, 12), (4, 128), 8, 1024, jnp.int32)
        itok_BxS2_1_8191 = jax.random.randint(jax.random.fold_in(_rk, 13), (4, 2048), 1, 1024, jnp.int32)
        _validS = jnp.arange(128)[None, :] < _lenS[:, None]
        _validS2 = jnp.arange(2048)[None, :] < _lenS2[:, None]
        _causal = jnp.tril(jnp.ones((128, 128), dtype=bool))
        mask_BxSxS2_if1 = jnp.where(jnp.ones((4, 128, 2048), dtype=bool), 1, 0).astype(jnp.int32)
        mask_BxS_ik0 = jnp.where(jnp.broadcast_to(_validS[:, :], (4, 128)), 0, 1).astype(jnp.int32)
        mask_BxS2_bf1 = jnp.ones((4, 2048), dtype=bool)
        return (x, ctx_1024, itok_BxS_8_8191, itok_BxS2_1_8191, mask_BxSxS2_if1, mask_BxS_ik0, mask_BxS2_bf1)
    x, ctx_1024, itok_BxS_8_8191, itok_BxS2_1_8191, mask_BxSxS2_if1, mask_BxS_ik0, mask_BxS2_bf1 = _rec_inputs()

    def _L0_xattn_setup():
        import jax, jax.numpy as jnp
        import numpy as np
        DIM = 128
        NUM_HEADS = 16
        HEAD_DIM = DIM // NUM_HEADS

        def _slopes(num_heads):
            ratio = 2.0 ** (-8.0 / num_heads)
            return jnp.asarray([ratio ** i for i in range(1, num_heads + 1)], dtype=jnp.float32)
        key = jax.random.key(seed)
        ks = jax.random.split(key, 10)
        b, q_len, k_len = (2, 256, 512)
        query = jax.random.normal(ks[0], (b, q_len, DIM), dtype=jnp.float32)
        keys = jax.random.normal(ks[1], (b, k_len, DIM), dtype=jnp.float32)
        values = jax.random.normal(ks[2], (b, k_len, DIM), dtype=jnp.float32)
        query_pos = jnp.sort(jax.random.randint(ks[3], (b, q_len), 0, 1024), axis=-1)
        key_pos = jnp.sort(jax.random.randint(ks[4], (b, k_len), 0, 1024), axis=-1)
        mask = jnp.ones((b, q_len, k_len), dtype=jnp.int32)
        lim = float(np.sqrt(6.0 / (DIM + DIM)))
        W_q = jax.random.uniform(ks[5], (DIM, DIM), minval=-lim, maxval=lim, dtype=jnp.float32)
        W_k = jax.random.uniform(ks[6], (DIM, DIM), minval=-lim, maxval=lim, dtype=jnp.float32)
        W_v = jax.random.uniform(ks[7], (DIM, DIM), minval=-lim, maxval=lim, dtype=jnp.float32)
        W_o = jax.random.uniform(ks[8], (DIM, DIM), minval=-lim, maxval=lim, dtype=jnp.float32)
        return {'query': query, 'keys': keys, 'values': values, 'W_q': W_q, 'W_k': W_k, 'W_v': W_v, 'W_o': W_o, 'query_pos': query_pos, 'key_pos': key_pos, 'mask': mask}
    _L0_xattn_all = _L0_xattn_setup()
    _L0_xattn_in = {k: v for k, v in _L0_xattn_all.items() if k in ('W_q', 'W_k', 'W_v', 'W_o')}
    del _L0_xattn_all

    def _L0_attn_setup():
        import jax, jax.numpy as jnp
        import numpy as np
        import math
        D_MODEL = 128
        N_HEAD = 16
        D_HEAD = D_MODEL // N_HEAD
        D_KMAP = 128
        D_INNER = 512

        def _layer_norm(x, g, b, eps=1e-05):
            mu = jnp.mean(x, axis=-1, keepdims=True)
            var = jnp.mean(jnp.square(x - mu), axis=-1, keepdims=True)
            return (x - mu) * jax.lax.rsqrt(var + eps) * g + b

        def _fourier_kernel(x, proj_mat):
            p = jnp.einsum('blhd,dm->blhm', x, proj_mat) / math.sqrt(D_HEAD)
            return jnp.concatenate([jnp.cos(p), jnp.sin(p)], axis=-1) / math.sqrt(D_KMAP)
        key = jax.random.key(seed)
        ks = jax.random.split(key, 12)
        s = 0.02
        return {'x': jax.random.normal(ks[0], (4, 512, D_MODEL), dtype=jnp.float32), 'proj_mat': jax.random.normal(ks[1], (D_HEAD, D_KMAP), dtype=jnp.float32), 'wq': jax.random.normal(ks[2], (D_MODEL, D_MODEL), dtype=jnp.float32) * s, 'bq': jnp.zeros((D_MODEL,), jnp.float32), 'wk': jax.random.normal(ks[3], (D_MODEL, D_MODEL), dtype=jnp.float32) * s, 'bk': jnp.zeros((D_MODEL,), jnp.float32), 'wv': jax.random.normal(ks[4], (D_MODEL, D_MODEL), dtype=jnp.float32) * s, 'bv': jnp.zeros((D_MODEL,), jnp.float32), 'wo': jax.random.normal(ks[5], (D_MODEL, D_MODEL), dtype=jnp.float32) * s, 'bo': jnp.zeros((D_MODEL,), jnp.float32), 'ln1_g': jnp.ones((D_MODEL,), jnp.float32), 'ln1_b': jnp.zeros((D_MODEL,), jnp.float32), 'w1': jax.random.normal(ks[6], (D_MODEL, D_INNER), dtype=jnp.float32) * s, 'b1': jnp.zeros((D_INNER,), jnp.float32), 'w2': jax.random.normal(ks[7], (D_INNER, D_MODEL), dtype=jnp.float32) * s, 'b2': jnp.zeros((D_MODEL,), jnp.float32), 'ln2_g': jnp.ones((D_MODEL,), jnp.float32), 'ln2_b': jnp.zeros((D_MODEL,), jnp.float32)}
    _L0_attn_all = _L0_attn_setup()
    _L0_attn_in = {k: v for k, v in _L0_attn_all.items() if k in ('proj_mat', 'wq', 'bq', 'wk', 'bk', 'wv', 'bv', 'wo', 'bo', 'ln1_g', 'ln1_b', 'w1', 'b1', 'w2', 'b2', 'ln2_g', 'ln2_b')}
    del _L0_attn_all

    def _L0_ffn_setup():
        import jax, jax.numpy as jnp
        import numpy as np
        B, T, D, H, E = (4, 256, 128, 512, 8)
        key = jax.random.key(seed)
        ks = jax.random.split(key, 7)
        x = jax.random.normal(ks[0], (B, T, D), dtype=jnp.float32)
        Wg = jax.random.normal(ks[1], (D, E), dtype=jnp.float32) / np.sqrt(D)
        bg = jax.random.normal(ks[2], (E,), dtype=jnp.float32) * 0.01
        W1 = jax.random.normal(ks[3], (E, D, H), dtype=jnp.float32) / np.sqrt(D)
        b1 = jax.random.normal(ks[4], (E, H), dtype=jnp.float32) * 0.01
        W2 = jax.random.normal(ks[5], (E, H, D), dtype=jnp.float32) / np.sqrt(H)
        b2 = jax.random.normal(ks[6], (E, D), dtype=jnp.float32) * 0.01
        return {'x': x, 'Wg': Wg, 'bg': bg, 'W1': W1, 'b1': b1, 'W2': W2, 'b2': b2}
    _L0_ffn_all = _L0_ffn_setup()
    _L0_ffn_in = {k: v for k, v in _L0_ffn_all.items() if k in ('Wg', 'bg', 'W1', 'b1', 'W2', 'b2')}
    del _L0_ffn_all

    def _L1_xattn_setup():
        import jax, jax.numpy as jnp
        import numpy as np
        HEADS = 16
        DIM_HEAD = 64
        SCALE = DIM_HEAD ** (-0.5)
        MASK_NEG = 1000000.0

        def _split_heads(t):
            b, n, _ = t.shape
            return t.reshape(b, n, HEADS, DIM_HEAD).transpose(0, 2, 1, 3)
        key = jax.random.key(seed)
        ks = jax.random.split(key, 6)
        B, N, M, D = (2, 256, 256, 128)
        inner = HEADS * DIM_HEAD
        x = jax.random.normal(ks[0], (B, N, D), dtype=jnp.float32)
        context = jax.random.normal(ks[1], (B, M, D), dtype=jnp.float32)
        mask = jax.random.randint(ks[2], (B, N), 0, 2, dtype=jnp.int32)
        Wq = jax.random.normal(ks[3], (D, inner), dtype=jnp.float32) * D ** (-0.5)
        Wkv = jax.random.normal(ks[4], (D, 2 * inner), dtype=jnp.float32) * D ** (-0.5)
        Wout = jax.random.normal(ks[5], (inner, D), dtype=jnp.float32) * inner ** (-0.5)
        bout = jnp.zeros((D,), dtype=jnp.float32)
        return {'x': x, 'context': context, 'mask': mask, 'Wq': Wq, 'Wkv': Wkv, 'Wout': Wout, 'bout': bout}
    _L1_xattn_all = _L1_xattn_setup()
    _L1_xattn_in = {k: v for k, v in _L1_xattn_all.items() if k in ('Wq', 'Wkv', 'Wout', 'bout')}
    del _L1_xattn_all

    def _L1_attn_setup():
        import jax, jax.numpy as jnp
        from jax import lax
        import numpy as np
        B, L, D_MODEL = (4, 256, 128)
        D_STATE, D_CONV, EXPAND = (16, 4, 2)
        D_INNER = EXPAND * D_MODEL
        DT_RANK = D_MODEL // 16
        LN_EPS = 1e-05

        def _layer_norm(x, g, b):
            mu = jnp.mean(x, -1, keepdims=True)
            var = jnp.mean((x - mu) ** 2, -1, keepdims=True)
            return (x - mu) * lax.rsqrt(var + LN_EPS) * g + b

        def _mamba_block(x, ln_g, ln_b, W_in, conv_w, conv_b, W_x, W_dt, b_dt, A_log, Dskip, W_out):
            b, l, _ = x.shape
            xn = _layer_norm(x, ln_g, ln_b)
            xz = xn @ W_in
            u, z = jnp.split(xz, 2, axis=-1)
            u_t = u.transpose(0, 2, 1)
            k = conv_w[:, None, :]
            uc = lax.conv_general_dilated(u_t, k, (1,), [(D_CONV - 1, 0)], dimension_numbers=('NCH', 'OIH', 'NCH'), feature_group_count=D_INNER) + conv_b[None, :, None]
            uc = jax.nn.silu(uc).transpose(0, 2, 1)
            dbc = uc @ W_x
            dt_r = dbc[..., :DT_RANK]
            Bs = dbc[..., DT_RANK:DT_RANK + D_STATE]
            Cs = dbc[..., DT_RANK + D_STATE:]
            dt = jax.nn.softplus(dt_r @ W_dt + b_dt)
            A = -jnp.exp(A_log)

            def step(h, ins):
                dt_t, B_t, C_t, u_t = ins
                dA = jnp.exp(dt_t[..., None] * A)
                h = h * dA + (dt_t * u_t)[..., None] * B_t[:, None, :]
                y = jnp.einsum('bds,bs->bd', h, C_t)
                return (h, y)
            h0 = jnp.zeros((b, D_INNER, D_STATE), x.dtype)
            xs = (dt.transpose(1, 0, 2), Bs.transpose(1, 0, 2), Cs.transpose(1, 0, 2), uc.transpose(1, 0, 2))
            _, ys = lax.scan(step, h0, xs)
            y = ys.transpose(1, 0, 2) + uc * Dskip
            y = y * jax.nn.silu(z)
            return x + y @ W_out
        key = jax.random.key(seed)
        ks = jax.random.split(key, 8)
        s = 0.02
        A_init = jnp.tile(jnp.arange(1, D_STATE + 1, dtype=jnp.float32), (D_INNER, 1))
        return {'x': jax.random.normal(ks[0], (B, L, D_MODEL), jnp.float32), 'ln_g': jnp.ones((D_MODEL,), jnp.float32), 'ln_b': jnp.zeros((D_MODEL,), jnp.float32), 'W_in': jax.random.normal(ks[1], (D_MODEL, 2 * D_INNER), jnp.float32) * s, 'conv_w': jax.random.normal(ks[2], (D_INNER, D_CONV), jnp.float32) * s, 'conv_b': jnp.zeros((D_INNER,), jnp.float32), 'W_x': jax.random.normal(ks[3], (D_INNER, DT_RANK + 2 * D_STATE), jnp.float32) * s, 'W_dt': jax.random.normal(ks[4], (DT_RANK, D_INNER), jnp.float32) * s, 'b_dt': jnp.full((D_INNER,), -4.6, jnp.float32), 'A_log': jnp.log(A_init), 'Dskip': jnp.ones((D_INNER,), jnp.float32), 'W_out': jax.random.normal(ks[5], (D_INNER, D_MODEL), jnp.float32) * s}
    _L1_attn_all = _L1_attn_setup()
    _L1_attn_in = {k: v for k, v in _L1_attn_all.items() if k in ('ln_g', 'ln_b', 'W_in', 'conv_w', 'conv_b', 'W_x', 'W_dt', 'b_dt', 'A_log', 'Dskip', 'W_out')}
    del _L1_attn_all

    def _L1_ffn_setup():
        import jax, jax.numpy as jnp
        import numpy as np
        B, S, D, M, E, K = (2, 256, 128, 176, 8, 2)
        key = jax.random.key(seed)
        k0, k1, k2, k3, k4 = jax.random.split(key, 5)
        scale = 0.02
        return {'x': jax.random.normal(k0, (B, S, D), dtype=jnp.float32), 'w_gate': jax.random.normal(k1, (D, E), dtype=jnp.float32) * scale, 'w_g': jax.random.normal(k2, (E, D, M), dtype=jnp.float32) * scale, 'w_u': jax.random.normal(k3, (E, D, M), dtype=jnp.float32) * scale, 'w_d': jax.random.normal(k4, (E, M, D), dtype=jnp.float32) * scale}
    _L1_ffn_all = _L1_ffn_setup()
    _L1_ffn_in = {k: v for k, v in _L1_ffn_all.items() if k in ('w_gate', 'w_g', 'w_u', 'w_d')}
    del _L1_ffn_all

    def _L2_xattn_setup():
        import jax, jax.numpy as jnp
        import numpy as np
        DIM = 128
        DIM_LATENT = 128
        DIM_HEAD = 64
        HEADS = 16
        INNER = HEADS * DIM_HEAD

        def layernorm(x, g, b, eps=1e-05):
            m = jnp.mean(x, axis=-1, keepdims=True)
            v = jnp.mean((x - m) ** 2, axis=-1, keepdims=True)
            return (x - m) / jnp.sqrt(v + eps) * g + b

        def rmsnorm(x, gamma, eps=1e-08):
            n = jnp.linalg.norm(x, axis=-1, keepdims=True) * x.shape[-1] ** (-0.5)
            return x / jnp.maximum(n, eps) * gamma
        key = jax.random.key(seed)
        ks = jax.random.split(key, 8)
        b, n, m = (4, 512, 64)
        x = jax.random.normal(ks[0], (b, n, DIM), dtype=jnp.float32)
        latents = jax.random.normal(ks[1], (b, m, DIM_LATENT), dtype=jnp.float32)
        mask = jnp.ones((b, n), dtype=bool)
        s = 0.02
        return {'x': x, 'latents': latents, 'mask': mask, 'ln_x_g': jnp.ones((DIM,), jnp.float32), 'ln_x_b': jnp.zeros((DIM,), jnp.float32), 'ln_l_g': jnp.ones((DIM_LATENT,), jnp.float32), 'ln_l_b': jnp.zeros((DIM_LATENT,), jnp.float32), 'qn_g': jnp.ones((DIM_HEAD,), jnp.float32), 'kn_g': jnp.ones((DIM_HEAD,), jnp.float32), 'Wq': jax.random.normal(ks[2], (DIM_LATENT, INNER), jnp.float32) * s, 'Wkv': jax.random.normal(ks[3], (DIM, 2 * INNER), jnp.float32) * s, 'Wout': jax.random.normal(ks[4], (INNER, DIM_LATENT), jnp.float32) * s, 'bout': jnp.zeros((DIM_LATENT,), jnp.float32)}
    _L2_xattn_all = _L2_xattn_setup()
    _L2_xattn_in = {k: v for k, v in _L2_xattn_all.items() if k in ('ln_x_g', 'ln_x_b', 'ln_l_g', 'ln_l_b', 'qn_g', 'kn_g', 'Wq', 'Wkv', 'Wout', 'bout')}
    del _L2_xattn_all

    def _L2_attn_setup():
        import jax, jax.numpy as jnp
        import numpy as np
        DIM = 128
        DEPTH = 6
        LN_EPS = 1e-05

        def _layernorm(x, gamma, beta):
            mu = jnp.mean(x, axis=-1, keepdims=True)
            var = jnp.mean(jnp.square(x - mu), axis=-1, keepdims=True)
            return (x - mu) * jax.lax.rsqrt(var + LN_EPS) * gamma + beta
        key = jax.random.key(seed)
        ks = jax.random.split(key, 6)
        b, n, d = (4, 256, DIM)
        x = jax.random.normal(ks[0], (b, n, d), dtype=jnp.float32)
        w_qkv = jax.random.normal(ks[1], (DEPTH, d, 3 * d), dtype=jnp.float32) * 0.02
        w_out = jax.random.normal(ks[2], (DEPTH, d, d), dtype=jnp.float32) * 0.02
        b_out = jnp.zeros((DEPTH, d), dtype=jnp.float32)
        gamma = jnp.ones((DEPTH, d), dtype=jnp.float32)
        beta = jnp.zeros((DEPTH, d), dtype=jnp.float32)
        return {'x': x, 'w_qkv': w_qkv, 'w_out': w_out, 'b_out': b_out, 'gamma': gamma, 'beta': beta}
    _L2_attn_all = _L2_attn_setup()
    _L2_attn_in = {k: v for k, v in _L2_attn_all.items() if k in ('w_qkv', 'w_out', 'b_out', 'gamma', 'beta')}
    del _L2_attn_all

    def _L2_ffn_setup():
        import jax, jax.numpy as jnp
        import numpy as np
        TOP_K = 2
        CAPACITY_FACTOR = 1.25

        def _moe_forward(x, gate_w, wi_gate, wi_up, wo):
            B, S, D = x.shape
            E = wi_gate.shape[0]
            N = B * S
            capacity = max(int(N / E * CAPACITY_FACTOR), 1)
            x_flat = x.reshape(N, D)
            router_logits = x_flat @ gate_w.T
            router_probs = jax.nn.softmax(router_logits, axis=-1)
            top_k_probs, top_k_idx = jax.lax.top_k(router_probs, TOP_K)
            top_k_probs = top_k_probs / jnp.sum(top_k_probs, axis=-1, keepdims=True)
            out = jnp.zeros_like(x_flat)
            experts = jnp.arange(E, dtype=jnp.int32)
            for k in range(TOP_K):
                eid = top_k_idx[:, k]
                ew = top_k_probs[:, k]
                onehot = (eid[:, None] == experts[None, :]).astype(jnp.int32)
                pos_all = jnp.cumsum(onehot, axis=0) - 1
                pos = jnp.take_along_axis(pos_all, eid[:, None].astype(jnp.int32), axis=1)[:, 0]
                valid = pos < capacity
                pos_c = jnp.where(valid, pos, 0)
                disp = jnp.zeros((E, capacity, D), x_flat.dtype).at[eid, pos_c].add(jnp.where(valid[:, None], x_flat, 0.0))
                gate = jax.nn.silu(jnp.einsum('ecd,efd->ecf', disp, wi_gate))
                up = jnp.einsum('ecd,efd->ecf', disp, wi_up)
                expert_out = jnp.einsum('ecf,edf->ecd', gate * up, wo)
                tok_out = expert_out[eid, pos_c]
                out = out + jnp.where(valid[:, None], ew[:, None] * tok_out, 0.0)
            return out.reshape(B, S, D)
        key = jax.random.key(seed)
        k1, k2, k3, k4, k5 = jax.random.split(key, 5)
        B, S, D, F, E = (4, 256, 128, 512, 8)
        return {'x': jax.random.normal(k1, (B, S, D), dtype=jnp.float32), 'gate_w': jax.random.normal(k2, (E, D), dtype=jnp.float32) * 0.02, 'wi_gate': jax.random.normal(k3, (E, F, D), dtype=jnp.float32) * 0.02, 'wi_up': jax.random.normal(k4, (E, F, D), dtype=jnp.float32) * 0.02, 'wo': jax.random.normal(k5, (E, D, F), dtype=jnp.float32) * 0.02}
    _L2_ffn_all = _L2_ffn_setup()
    _L2_ffn_in = {k: v for k, v in _L2_ffn_all.items() if k in ('gate_w', 'wi_gate', 'wi_up', 'wo')}
    del _L2_ffn_all

    def _L3_xattn_setup():
        import jax, jax.numpy as jnp
        import numpy as np
        DIM = 128
        NUM_HEADS = 8
        HEAD_DIM = 64
        INNER = NUM_HEADS * HEAD_DIM
        key = jax.random.key(seed)
        ks = jax.random.split(key, 7)
        B, N, M = (8, 64, 512)
        x = jax.random.normal(ks[0], (B, N, DIM), dtype=jnp.float32)
        context = jax.random.normal(ks[1], (B, M, DIM), dtype=jnp.float32)
        s_in = 1.0 / np.sqrt(DIM)
        s_inner = 1.0 / np.sqrt(INNER)
        Wq = jax.random.normal(ks[2], (DIM, INNER), dtype=jnp.float32) * s_in
        Wk = jax.random.normal(ks[3], (DIM, INNER), dtype=jnp.float32) * s_in
        Wv = jax.random.normal(ks[4], (DIM, INNER), dtype=jnp.float32) * s_in
        Wo = jax.random.normal(ks[5], (INNER, DIM), dtype=jnp.float32) * s_inner
        bo = jax.random.normal(ks[6], (DIM,), dtype=jnp.float32) * 0.01
        return {'x': x, 'context': context, 'Wq': Wq, 'Wk': Wk, 'Wv': Wv, 'Wo': Wo, 'bo': bo}
    _L3_xattn_all = _L3_xattn_setup()
    _L3_xattn_in = {k: v for k, v in _L3_xattn_all.items() if k in ('Wq', 'Wk', 'Wv', 'Wo', 'bo')}
    del _L3_xattn_all

    def _L3_attn_setup():
        import jax, jax.numpy as jnp
        import numpy as np
        import math
        B, T, E, H, DQ, NB, MAXLEN = (4, 128, 128, 16, 64, 10, 128)
        NEG = -1000000000.0

        def _attn_forward(X, Wq, bq, Wk, Wv, Wproj, bproj, Wr, br, b_nd):
            b, t, e = X.shape
            maxlen = b_nd.shape[1]
            nb = b_nd.shape[0]
            h = H
            dq = Wq.shape[1] // h
            Q = (X @ Wq + bq).reshape(b, t, h, dq).transpose(0, 2, 1, 3)
            K = (X @ Wk).reshape(b, t, h, dq).transpose(0, 2, 1, 3)
            V = (X @ Wv).reshape(b, t, h, dq).transpose(0, 2, 1, 3)
            R = (X @ Wr + br).reshape(b, t, h, nb).transpose(0, 2, 1, 3)
            d = jnp.arange(t)[:, None] - jnp.arange(t)[None, :]
            valid = (d >= 0) & (d < maxlen)
            bias = jnp.where(valid, 0.0, NEG).astype(jnp.float32)
            D_ntT = jnp.where(valid[None, :, :], b_nd[:, jnp.clip(d, 0, maxlen - 1)], 0.0)
            extra = jnp.einsum('bhtn,ntp->bhtp', R, D_ntT)
            logits = jnp.einsum('bhtd,bhpd->bhtp', Q, K) / math.sqrt(dq) + bias + extra
            W = jax.nn.softmax(logits, axis=-1)
            A = jnp.einsum('bhtp,bhpd->bhtd', W, V)
            A = A.transpose(0, 2, 1, 3).reshape(b, t, h * dq)
            return A @ Wproj + bproj
        key = jax.random.key(seed)
        k = jax.random.split(key, 10)
        X = jax.random.normal(k[0], (B, T, E), jnp.float32)
        Wq = jax.random.normal(k[1], (E, H * DQ), jnp.float32) * (0.1 / math.sqrt(E))
        bq = jnp.zeros((H * DQ,), jnp.float32)
        Wk = jax.random.normal(k[2], (E, H * DQ), jnp.float32) * (0.2 / math.sqrt(E))
        Wv = jax.random.normal(k[3], (E, H * DQ), jnp.float32) * (1.0 / math.sqrt(E))
        Wproj = jax.random.normal(k[4], (H * DQ, E), jnp.float32) * (1.0 / math.sqrt(H * DQ))
        bproj = jnp.zeros((E,), jnp.float32)
        Wr = jax.random.normal(k[5], (E, H * NB), jnp.float32) * (0.1 / math.sqrt(E))
        br = jnp.zeros((H * NB,), jnp.float32)
        b_nd = jax.random.normal(k[6], (NB, MAXLEN), jnp.float32) * 0.2
        return dict(X=X, Wq=Wq, bq=bq, Wk=Wk, Wv=Wv, Wproj=Wproj, bproj=bproj, Wr=Wr, br=br, b_nd=b_nd)
    _L3_attn_all = _L3_attn_setup()
    _L3_attn_in = {k: v for k, v in _L3_attn_all.items() if k in ('Wq', 'bq', 'Wk', 'Wv', 'Wproj', 'bproj', 'Wr', 'br', 'b_nd')}
    del _L3_attn_all

    def _L3_ffn_setup():
        import jax, jax.numpy as jnp
        import numpy as np
        D_MODEL = 128
        EXPANSION = 4
        D_HIDDEN = D_MODEL * EXPANSION
        NUM_STAGES = int(np.log2(D_HIDDEN))

        def butterfly(y, weights, dim):
            lead = y.shape[:-1]
            for stage in range(weights.shape[0]):
                s = 2 ** stage
                nb = dim // (2 * s)
                yr = y.reshape(*lead, nb, 2, s)
                a = yr[..., 0, :]
                b = yr[..., 1, :]
                w = weights[stage].reshape(nb, s, 2, 2)
                na = w[..., 0, 0] * a + w[..., 0, 1] * b
                nb2 = w[..., 1, 0] * a + w[..., 1, 1] * b
                y = jnp.stack([na, nb2], axis=-2).reshape(*lead, dim)
            return y
        key = jax.random.key(seed)
        ks = jax.random.split(key, 6)
        B, S = (4, 256)
        x = jax.random.normal(ks[0], (B, S, D_MODEL), jnp.float32)
        W_exp = jax.random.normal(ks[1], (D_MODEL, D_HIDDEN), jnp.float32) * 0.02
        b_exp = jnp.zeros((D_HIDDEN,), jnp.float32)
        up_weights = jax.random.normal(ks[2], (NUM_STAGES, D_HIDDEN // 2, 2, 2), jnp.float32) * 0.02
        up_bias = jnp.zeros((D_HIDDEN,), jnp.float32)
        down_weights = jax.random.normal(ks[3], (NUM_STAGES, D_HIDDEN // 2, 2, 2), jnp.float32) * 0.02
        W_con = jax.random.normal(ks[4], (D_HIDDEN, D_MODEL), jnp.float32) * 0.02
        b_con = jnp.zeros((D_MODEL,), jnp.float32)
        down_bias = jnp.zeros((D_MODEL,), jnp.float32)
        return dict(x=x, W_exp=W_exp, b_exp=b_exp, up_weights=up_weights, up_bias=up_bias, down_weights=down_weights, W_con=W_con, b_con=b_con, down_bias=down_bias)
    _L3_ffn_all = _L3_ffn_setup()
    _L3_ffn_in = {k: v for k, v in _L3_ffn_all.items() if k in ('W_exp', 'b_exp', 'up_weights', 'up_bias', 'down_weights', 'W_con', 'b_con', 'down_bias')}
    del _L3_ffn_all
    return {'x': x, 'ctx_1024': ctx_1024, 'itok_BxS_8_8191': itok_BxS_8_8191, 'itok_BxS2_1_8191': itok_BxS2_1_8191, 'mask_BxSxS2_if1': mask_BxSxS2_if1, 'mask_BxS_ik0': mask_BxS_ik0, 'mask_BxS2_bf1': mask_BxS2_bf1, 'L0_xattn_W_q': _L0_xattn_in['W_q'], 'L0_xattn_W_k': _L0_xattn_in['W_k'], 'L0_xattn_W_v': _L0_xattn_in['W_v'], 'L0_xattn_W_o': _L0_xattn_in['W_o'], 'L0_attn_proj_mat': _L0_attn_in['proj_mat'], 'L0_attn_wq': _L0_attn_in['wq'], 'L0_attn_bq': _L0_attn_in['bq'], 'L0_attn_wk': _L0_attn_in['wk'], 'L0_attn_bk': _L0_attn_in['bk'], 'L0_attn_wv': _L0_attn_in['wv'], 'L0_attn_bv': _L0_attn_in['bv'], 'L0_attn_wo': _L0_attn_in['wo'], 'L0_attn_bo': _L0_attn_in['bo'], 'L0_attn_ln1_g': _L0_attn_in['ln1_g'], 'L0_attn_ln1_b': _L0_attn_in['ln1_b'], 'L0_attn_w1': _L0_attn_in['w1'], 'L0_attn_b1': _L0_attn_in['b1'], 'L0_attn_w2': _L0_attn_in['w2'], 'L0_attn_b2': _L0_attn_in['b2'], 'L0_attn_ln2_g': _L0_attn_in['ln2_g'], 'L0_attn_ln2_b': _L0_attn_in['ln2_b'], 'L0_ffn_Wg': _L0_ffn_in['Wg'], 'L0_ffn_bg': _L0_ffn_in['bg'], 'L0_ffn_W1': _L0_ffn_in['W1'], 'L0_ffn_b1': _L0_ffn_in['b1'], 'L0_ffn_W2': _L0_ffn_in['W2'], 'L0_ffn_b2': _L0_ffn_in['b2'], 'L1_xattn_Wq': _L1_xattn_in['Wq'], 'L1_xattn_Wkv': _L1_xattn_in['Wkv'], 'L1_xattn_Wout': _L1_xattn_in['Wout'], 'L1_xattn_bout': _L1_xattn_in['bout'], 'L1_attn_ln_g': _L1_attn_in['ln_g'], 'L1_attn_ln_b': _L1_attn_in['ln_b'], 'L1_attn_W_in': _L1_attn_in['W_in'], 'L1_attn_conv_w': _L1_attn_in['conv_w'], 'L1_attn_conv_b': _L1_attn_in['conv_b'], 'L1_attn_W_x': _L1_attn_in['W_x'], 'L1_attn_W_dt': _L1_attn_in['W_dt'], 'L1_attn_b_dt': _L1_attn_in['b_dt'], 'L1_attn_A_log': _L1_attn_in['A_log'], 'L1_attn_Dskip': _L1_attn_in['Dskip'], 'L1_attn_W_out': _L1_attn_in['W_out'], 'L1_ffn_w_gate': _L1_ffn_in['w_gate'], 'L1_ffn_w_g': _L1_ffn_in['w_g'], 'L1_ffn_w_u': _L1_ffn_in['w_u'], 'L1_ffn_w_d': _L1_ffn_in['w_d'], 'L2_xattn_ln_x_g': _L2_xattn_in['ln_x_g'], 'L2_xattn_ln_x_b': _L2_xattn_in['ln_x_b'], 'L2_xattn_ln_l_g': _L2_xattn_in['ln_l_g'], 'L2_xattn_ln_l_b': _L2_xattn_in['ln_l_b'], 'L2_xattn_qn_g': _L2_xattn_in['qn_g'], 'L2_xattn_kn_g': _L2_xattn_in['kn_g'], 'L2_xattn_Wq': _L2_xattn_in['Wq'], 'L2_xattn_Wkv': _L2_xattn_in['Wkv'], 'L2_xattn_Wout': _L2_xattn_in['Wout'], 'L2_xattn_bout': _L2_xattn_in['bout'], 'L2_attn_w_qkv': _L2_attn_in['w_qkv'], 'L2_attn_w_out': _L2_attn_in['w_out'], 'L2_attn_b_out': _L2_attn_in['b_out'], 'L2_attn_gamma': _L2_attn_in['gamma'], 'L2_attn_beta': _L2_attn_in['beta'], 'L2_ffn_gate_w': _L2_ffn_in['gate_w'], 'L2_ffn_wi_gate': _L2_ffn_in['wi_gate'], 'L2_ffn_wi_up': _L2_ffn_in['wi_up'], 'L2_ffn_wo': _L2_ffn_in['wo'], 'L3_xattn_Wq': _L3_xattn_in['Wq'], 'L3_xattn_Wk': _L3_xattn_in['Wk'], 'L3_xattn_Wv': _L3_xattn_in['Wv'], 'L3_xattn_Wo': _L3_xattn_in['Wo'], 'L3_xattn_bo': _L3_xattn_in['bo'], 'L3_attn_Wq': _L3_attn_in['Wq'], 'L3_attn_bq': _L3_attn_in['bq'], 'L3_attn_Wk': _L3_attn_in['Wk'], 'L3_attn_Wv': _L3_attn_in['Wv'], 'L3_attn_Wproj': _L3_attn_in['Wproj'], 'L3_attn_bproj': _L3_attn_in['bproj'], 'L3_attn_Wr': _L3_attn_in['Wr'], 'L3_attn_br': _L3_attn_in['br'], 'L3_attn_b_nd': _L3_attn_in['b_nd'], 'L3_ffn_W_exp': _L3_ffn_in['W_exp'], 'L3_ffn_b_exp': _L3_ffn_in['b_exp'], 'L3_ffn_up_weights': _L3_ffn_in['up_weights'], 'L3_ffn_up_bias': _L3_ffn_in['up_bias'], 'L3_ffn_down_weights': _L3_ffn_in['down_weights'], 'L3_ffn_W_con': _L3_ffn_in['W_con'], 'L3_ffn_b_con': _L3_ffn_in['b_con'], 'L3_ffn_down_bias': _L3_ffn_in['down_bias']}

def reference(x, ctx_1024, itok_BxS_8_8191, itok_BxS2_1_8191, mask_BxSxS2_if1, mask_BxS_ik0, mask_BxS2_bf1, L0_xattn_W_q, L0_xattn_W_k, L0_xattn_W_v, L0_xattn_W_o, L0_attn_proj_mat, L0_attn_wq, L0_attn_bq, L0_attn_wk, L0_attn_bk, L0_attn_wv, L0_attn_bv, L0_attn_wo, L0_attn_bo, L0_attn_ln1_g, L0_attn_ln1_b, L0_attn_w1, L0_attn_b1, L0_attn_w2, L0_attn_b2, L0_attn_ln2_g, L0_attn_ln2_b, L0_ffn_Wg, L0_ffn_bg, L0_ffn_W1, L0_ffn_b1, L0_ffn_W2, L0_ffn_b2, L1_xattn_Wq, L1_xattn_Wkv, L1_xattn_Wout, L1_xattn_bout, L1_attn_ln_g, L1_attn_ln_b, L1_attn_W_in, L1_attn_conv_w, L1_attn_conv_b, L1_attn_W_x, L1_attn_W_dt, L1_attn_b_dt, L1_attn_A_log, L1_attn_Dskip, L1_attn_W_out, L1_ffn_w_gate, L1_ffn_w_g, L1_ffn_w_u, L1_ffn_w_d, L2_xattn_ln_x_g, L2_xattn_ln_x_b, L2_xattn_ln_l_g, L2_xattn_ln_l_b, L2_xattn_qn_g, L2_xattn_kn_g, L2_xattn_Wq, L2_xattn_Wkv, L2_xattn_Wout, L2_xattn_bout, L2_attn_w_qkv, L2_attn_w_out, L2_attn_b_out, L2_attn_gamma, L2_attn_beta, L2_ffn_gate_w, L2_ffn_wi_gate, L2_ffn_wi_up, L2_ffn_wo, L3_xattn_Wq, L3_xattn_Wk, L3_xattn_Wv, L3_xattn_Wo, L3_xattn_bo, L3_attn_Wq, L3_attn_bq, L3_attn_Wk, L3_attn_Wv, L3_attn_Wproj, L3_attn_bproj, L3_attn_Wr, L3_attn_br, L3_attn_b_nd, L3_ffn_W_exp, L3_ffn_b_exp, L3_ffn_up_weights, L3_ffn_up_bias, L3_ffn_down_weights, L3_ffn_W_con, L3_ffn_b_con, L3_ffn_down_bias):
    import jax
    import jax.numpy as jnp

    def _L0_xattn_ref(query, keys, values, W_q, W_k, W_v, W_o, query_pos, key_pos, mask):
        import jax, jax.numpy as jnp
        import numpy as np
        DIM = 128
        NUM_HEADS = 16
        HEAD_DIM = DIM // NUM_HEADS

        def _slopes(num_heads):
            ratio = 2.0 ** (-8.0 / num_heads)
            return jnp.asarray([ratio ** i for i in range(1, num_heads + 1)], dtype=jnp.float32)
        b, q_len, _ = query.shape
        k_len = keys.shape[1]
        scale = 1.0 / np.sqrt(HEAD_DIM)
        Q = (query @ W_q.T).reshape(b, q_len, NUM_HEADS, HEAD_DIM).transpose(0, 2, 1, 3)
        K = (keys @ W_k.T).reshape(b, k_len, NUM_HEADS, HEAD_DIM).transpose(0, 2, 1, 3)
        V = (values @ W_v.T).reshape(b, k_len, NUM_HEADS, HEAD_DIM).transpose(0, 2, 1, 3)
        scores = jnp.einsum('bhqd,bhkd->bhqk', Q, K) * scale
        dist = (query_pos[:, :, None] - key_pos[:, None, :]).astype(scores.dtype)
        bias = -_slopes(NUM_HEADS)[None, :, None, None] * dist[:, None, :, :]
        scores = scores + bias
        scores = jnp.where(mask[:, None, :, :] == 0, -jnp.inf, scores)
        m = jnp.max(scores, axis=-1, keepdims=True)
        e = jnp.exp(scores - m)
        attn = e / (1.0 + jnp.sum(e, axis=-1, keepdims=True))
        out = jnp.einsum('bhqk,bhkd->bhqd', attn, V)
        out = out.transpose(0, 2, 1, 3).reshape(b, q_len, DIM)
        return out @ W_o.T

    def _L0_attn_ref(x, proj_mat, wq, bq, wk, bk, wv, bv, wo, bo, ln1_g, ln1_b, w1, b1, w2, b2, ln2_g, ln2_b):
        import jax, jax.numpy as jnp
        import numpy as np
        import math
        D_MODEL = 128
        N_HEAD = 16
        D_HEAD = D_MODEL // N_HEAD
        D_KMAP = 128
        D_INNER = 512

        def _layer_norm(x, g, b, eps=1e-05):
            mu = jnp.mean(x, axis=-1, keepdims=True)
            var = jnp.mean(jnp.square(x - mu), axis=-1, keepdims=True)
            return (x - mu) * jax.lax.rsqrt(var + eps) * g + b

        def _fourier_kernel(x, proj_mat):
            p = jnp.einsum('blhd,dm->blhm', x, proj_mat) / math.sqrt(D_HEAD)
            return jnp.concatenate([jnp.cos(p), jnp.sin(p)], axis=-1) / math.sqrt(D_KMAP)
        B, L, _ = x.shape
        x2 = _layer_norm(x, ln1_g, ln1_b)
        q = (x2 @ wq + bq).reshape(B, L, N_HEAD, D_HEAD)
        k = (x2 @ wk + bk).reshape(B, L, N_HEAD, D_HEAD)
        v = (x2 @ wv + bv).reshape(B, L, N_HEAD, D_HEAD)
        qp = _fourier_kernel(q, proj_mat)
        kp = _fourier_kernel(k, proj_mat)
        kv = jnp.einsum('blhm,blhd->bhmd', kp, v)
        attn = jnp.einsum('blhm,bhmd->blhd', qp, kv)
        attn = attn.reshape(B, L, D_MODEL) @ wo + bo
        x = x + attn
        x2 = _layer_norm(x, ln2_g, ln2_b)
        h = jax.nn.relu(x2 @ w1 + b1)
        x = x + (h @ w2 + b2)
        return x

    def _L0_ffn_ref(x, Wg, bg, W1, b1, W2, b2):
        import jax, jax.numpy as jnp
        import numpy as np
        B, T, D, H, E = (4, 256, 128, 512, 8)
        gate_scores = x @ Wg + bg
        top1 = jnp.argmax(gate_scores, axis=-1)
        onehot = jax.nn.one_hot(top1, Wg.shape[-1], dtype=x.dtype)
        h = jax.nn.relu(jnp.einsum('btd,edh->beth', x, W1) + b1[None, :, None, :])
        y = jnp.einsum('beth,ehd->betd', h, W2) + b2[None, :, None, :]
        out = jnp.einsum('betd,bte->btd', y, onehot)
        return out

    def _L1_xattn_ref(x, context, mask, Wq, Wkv, Wout, bout):
        import jax, jax.numpy as jnp
        import numpy as np
        HEADS = 16
        DIM_HEAD = 64
        SCALE = DIM_HEAD ** (-0.5)
        MASK_NEG = 1000000.0

        def _split_heads(t):
            b, n, _ = t.shape
            return t.reshape(b, n, HEADS, DIM_HEAD).transpose(0, 2, 1, 3)
        kv = context @ Wkv
        k, v = jnp.split(kv, 2, axis=-1)
        q = x @ Wq
        q, k, v = (_split_heads(q), _split_heads(k), _split_heads(v))
        dots = jnp.einsum('bhnd,bhmd->bhnm', q, k) * SCALE
        dots = dots - (1.0 - mask.astype(jnp.float32))[:, None, :, None] * MASK_NEG
        attn = jax.nn.softmax(dots, axis=-1)
        out = jnp.einsum('bhnm,bhmd->bhnd', attn, v)
        b, h, n, d = out.shape
        out = out.transpose(0, 2, 1, 3).reshape(b, n, h * d)
        return out @ Wout + bout

    def _L1_attn_ref(x, ln_g, ln_b, W_in, conv_w, conv_b, W_x, W_dt, b_dt, A_log, Dskip, W_out):
        import jax, jax.numpy as jnp
        from jax import lax
        import numpy as np
        B, L, D_MODEL = (4, 256, 128)
        D_STATE, D_CONV, EXPAND = (16, 4, 2)
        D_INNER = EXPAND * D_MODEL
        DT_RANK = D_MODEL // 16
        LN_EPS = 1e-05

        def _layer_norm(x, g, b):
            mu = jnp.mean(x, -1, keepdims=True)
            var = jnp.mean((x - mu) ** 2, -1, keepdims=True)
            return (x - mu) * lax.rsqrt(var + LN_EPS) * g + b

        def _mamba_block(x, ln_g, ln_b, W_in, conv_w, conv_b, W_x, W_dt, b_dt, A_log, Dskip, W_out):
            b, l, _ = x.shape
            xn = _layer_norm(x, ln_g, ln_b)
            xz = xn @ W_in
            u, z = jnp.split(xz, 2, axis=-1)
            u_t = u.transpose(0, 2, 1)
            k = conv_w[:, None, :]
            uc = lax.conv_general_dilated(u_t, k, (1,), [(D_CONV - 1, 0)], dimension_numbers=('NCH', 'OIH', 'NCH'), feature_group_count=D_INNER) + conv_b[None, :, None]
            uc = jax.nn.silu(uc).transpose(0, 2, 1)
            dbc = uc @ W_x
            dt_r = dbc[..., :DT_RANK]
            Bs = dbc[..., DT_RANK:DT_RANK + D_STATE]
            Cs = dbc[..., DT_RANK + D_STATE:]
            dt = jax.nn.softplus(dt_r @ W_dt + b_dt)
            A = -jnp.exp(A_log)

            def step(h, ins):
                dt_t, B_t, C_t, u_t = ins
                dA = jnp.exp(dt_t[..., None] * A)
                h = h * dA + (dt_t * u_t)[..., None] * B_t[:, None, :]
                y = jnp.einsum('bds,bs->bd', h, C_t)
                return (h, y)
            h0 = jnp.zeros((b, D_INNER, D_STATE), x.dtype)
            xs = (dt.transpose(1, 0, 2), Bs.transpose(1, 0, 2), Cs.transpose(1, 0, 2), uc.transpose(1, 0, 2))
            _, ys = lax.scan(step, h0, xs)
            y = ys.transpose(1, 0, 2) + uc * Dskip
            y = y * jax.nn.silu(z)
            return x + y @ W_out
        return _mamba_block(x, ln_g, ln_b, W_in, conv_w, conv_b, W_x, W_dt, b_dt, A_log, Dskip, W_out)

    def _L1_ffn_ref(x, w_gate, w_g, w_u, w_d):
        import jax, jax.numpy as jnp
        import numpy as np
        B, S, D, M, E, K = (2, 256, 128, 176, 8, 2)
        scores = x @ w_gate
        topk_scores, topk_idx = jax.lax.top_k(scores, K)
        topk_probs = jax.nn.softmax(topk_scores, axis=-1)
        gating = jnp.sum(jax.nn.one_hot(topk_idx, E, dtype=topk_probs.dtype) * topk_probs[..., None], axis=-2)
        hidden = jax.nn.silu(jnp.einsum('bsd,edm->ebsm', x, w_g)) * jnp.einsum('bsd,edm->ebsm', x, w_u)
        expert_out = jnp.einsum('ebsm,emd->ebsd', hidden, w_d)
        y = jnp.einsum('bse,ebsd->bsd', gating, expert_out)
        return y

    def _L2_xattn_ref(x, latents, mask, ln_x_g, ln_x_b, ln_l_g, ln_l_b, qn_g, kn_g, Wq, Wkv, Wout, bout):
        import jax, jax.numpy as jnp
        import numpy as np
        DIM = 128
        DIM_LATENT = 128
        DIM_HEAD = 64
        HEADS = 16
        INNER = HEADS * DIM_HEAD

        def layernorm(x, g, b, eps=1e-05):
            m = jnp.mean(x, axis=-1, keepdims=True)
            v = jnp.mean((x - m) ** 2, axis=-1, keepdims=True)
            return (x - m) / jnp.sqrt(v + eps) * g + b

        def rmsnorm(x, gamma, eps=1e-08):
            n = jnp.linalg.norm(x, axis=-1, keepdims=True) * x.shape[-1] ** (-0.5)
            return x / jnp.maximum(n, eps) * gamma
        b, n, _ = x.shape
        m = latents.shape[1]
        h, d = (HEADS, DIM_HEAD)
        scale = d ** (-0.5)
        xn = layernorm(x, ln_x_g, ln_x_b)
        ln = layernorm(latents, ln_l_g, ln_l_b)
        q = (ln @ Wq).reshape(b, m, h, d).transpose(0, 2, 1, 3)
        kv = jnp.concatenate([xn @ Wkv, ln @ Wkv], axis=1)
        kv = kv.reshape(b, n + m, 2, h, d)
        k = kv[:, :, 0].transpose(0, 2, 1, 3)
        v = kv[:, :, 1].transpose(0, 2, 1, 3)
        qn = rmsnorm(q, qn_g) * scale
        kn = rmsnorm(k, kn_g)
        sim = jnp.einsum('bhid,bhjd->bhij', qn, kn)
        max_neg = -jnp.finfo(sim.dtype).max
        padded_mask = jnp.concatenate([mask, jnp.ones((b, m), bool)], axis=1)
        sim = jnp.where(padded_mask[:, None, None, :], sim, max_neg)
        attn = jax.nn.softmax(sim.astype(jnp.float32), axis=-1).astype(sim.dtype)
        out = jnp.einsum('bhij,bhjd->bhid', attn, v)
        out = out.transpose(0, 2, 1, 3).reshape(b, m, h * d)
        return out @ Wout + bout

    def _L2_attn_ref(x, w_qkv, w_out, b_out, gamma, beta):
        import jax, jax.numpy as jnp
        import numpy as np
        DIM = 128
        DEPTH = 6
        LN_EPS = 1e-05

        def _layernorm(x, gamma, beta):
            mu = jnp.mean(x, axis=-1, keepdims=True)
            var = jnp.mean(jnp.square(x - mu), axis=-1, keepdims=True)
            return (x - mu) * jax.lax.rsqrt(var + LN_EPS) * gamma + beta
        depth = w_qkv.shape[0]
        for l in range(depth):
            residual = x
            h = _layernorm(x, gamma[l], beta[l])
            qkv = h @ w_qkv[l]
            q, k, v = jnp.split(qkv, 3, axis=-1)
            q = jax.nn.softmax(q, axis=1)
            k = jax.nn.softmax(k, axis=2)
            context = jnp.einsum('bic,bjc->bij', k, v)
            out = jnp.einsum('bic,bij->bjc', q, context)
            out = out @ w_out[l] + b_out[l]
            x = out + residual
        return x

    def _L2_ffn_ref(x, gate_w, wi_gate, wi_up, wo):
        import jax, jax.numpy as jnp
        import numpy as np
        TOP_K = 2
        CAPACITY_FACTOR = 1.25

        def _moe_forward(x, gate_w, wi_gate, wi_up, wo):
            B, S, D = x.shape
            E = wi_gate.shape[0]
            N = B * S
            capacity = max(int(N / E * CAPACITY_FACTOR), 1)
            x_flat = x.reshape(N, D)
            router_logits = x_flat @ gate_w.T
            router_probs = jax.nn.softmax(router_logits, axis=-1)
            top_k_probs, top_k_idx = jax.lax.top_k(router_probs, TOP_K)
            top_k_probs = top_k_probs / jnp.sum(top_k_probs, axis=-1, keepdims=True)
            out = jnp.zeros_like(x_flat)
            experts = jnp.arange(E, dtype=jnp.int32)
            for k in range(TOP_K):
                eid = top_k_idx[:, k]
                ew = top_k_probs[:, k]
                onehot = (eid[:, None] == experts[None, :]).astype(jnp.int32)
                pos_all = jnp.cumsum(onehot, axis=0) - 1
                pos = jnp.take_along_axis(pos_all, eid[:, None].astype(jnp.int32), axis=1)[:, 0]
                valid = pos < capacity
                pos_c = jnp.where(valid, pos, 0)
                disp = jnp.zeros((E, capacity, D), x_flat.dtype).at[eid, pos_c].add(jnp.where(valid[:, None], x_flat, 0.0))
                gate = jax.nn.silu(jnp.einsum('ecd,efd->ecf', disp, wi_gate))
                up = jnp.einsum('ecd,efd->ecf', disp, wi_up)
                expert_out = jnp.einsum('ecf,edf->ecd', gate * up, wo)
                tok_out = expert_out[eid, pos_c]
                out = out + jnp.where(valid[:, None], ew[:, None] * tok_out, 0.0)
            return out.reshape(B, S, D)
        return _moe_forward(x, gate_w, wi_gate, wi_up, wo)

    def _L3_xattn_ref(x, context, Wq, Wk, Wv, Wo, bo):
        import jax, jax.numpy as jnp
        import numpy as np
        DIM = 128
        NUM_HEADS = 8
        HEAD_DIM = 64
        INNER = NUM_HEADS * HEAD_DIM
        B, N, _ = x.shape
        M = context.shape[1]
        scale = HEAD_DIM ** (-0.5)
        q = (x @ Wq).reshape(B, N, NUM_HEADS, HEAD_DIM).transpose(0, 2, 1, 3)
        k = (context @ Wk).reshape(B, M, NUM_HEADS, HEAD_DIM).transpose(0, 2, 1, 3)
        v = (context @ Wv).reshape(B, M, NUM_HEADS, HEAD_DIM).transpose(0, 2, 1, 3)
        attn = jax.nn.softmax(jnp.einsum('bhnd,bhmd->bhnm', q, k) * scale, axis=-1)
        out = jnp.einsum('bhnm,bhmd->bhnd', attn, v)
        out = out.transpose(0, 2, 1, 3).reshape(B, N, INNER)
        return out @ Wo + bo

    def _L3_attn_ref(X, Wq, bq, Wk, Wv, Wproj, bproj, Wr, br, b_nd):
        import jax, jax.numpy as jnp
        import numpy as np
        import math
        B, T, E, H, DQ, NB, MAXLEN = (4, 128, 128, 16, 64, 10, 128)
        NEG = -1000000000.0

        def _attn_forward(X, Wq, bq, Wk, Wv, Wproj, bproj, Wr, br, b_nd):
            b, t, e = X.shape
            maxlen = b_nd.shape[1]
            nb = b_nd.shape[0]
            h = H
            dq = Wq.shape[1] // h
            Q = (X @ Wq + bq).reshape(b, t, h, dq).transpose(0, 2, 1, 3)
            K = (X @ Wk).reshape(b, t, h, dq).transpose(0, 2, 1, 3)
            V = (X @ Wv).reshape(b, t, h, dq).transpose(0, 2, 1, 3)
            R = (X @ Wr + br).reshape(b, t, h, nb).transpose(0, 2, 1, 3)
            d = jnp.arange(t)[:, None] - jnp.arange(t)[None, :]
            valid = (d >= 0) & (d < maxlen)
            bias = jnp.where(valid, 0.0, NEG).astype(jnp.float32)
            D_ntT = jnp.where(valid[None, :, :], b_nd[:, jnp.clip(d, 0, maxlen - 1)], 0.0)
            extra = jnp.einsum('bhtn,ntp->bhtp', R, D_ntT)
            logits = jnp.einsum('bhtd,bhpd->bhtp', Q, K) / math.sqrt(dq) + bias + extra
            W = jax.nn.softmax(logits, axis=-1)
            A = jnp.einsum('bhtp,bhpd->bhtd', W, V)
            A = A.transpose(0, 2, 1, 3).reshape(b, t, h * dq)
            return A @ Wproj + bproj
        return _attn_forward(X, Wq, bq, Wk, Wv, Wproj, bproj, Wr, br, b_nd)

    def _L3_ffn_ref(x, W_exp, b_exp, up_weights, up_bias, down_weights, W_con, b_con, down_bias):
        import jax, jax.numpy as jnp
        import numpy as np
        D_MODEL = 128
        EXPANSION = 4
        D_HIDDEN = D_MODEL * EXPANSION
        NUM_STAGES = int(np.log2(D_HIDDEN))

        def butterfly(y, weights, dim):
            lead = y.shape[:-1]
            for stage in range(weights.shape[0]):
                s = 2 ** stage
                nb = dim // (2 * s)
                yr = y.reshape(*lead, nb, 2, s)
                a = yr[..., 0, :]
                b = yr[..., 1, :]
                w = weights[stage].reshape(nb, s, 2, 2)
                na = w[..., 0, 0] * a + w[..., 0, 1] * b
                nb2 = w[..., 1, 0] * a + w[..., 1, 1] * b
                y = jnp.stack([na, nb2], axis=-2).reshape(*lead, dim)
            return y
        h = jnp.einsum('bsd,dh->bsh', x, W_exp) + b_exp
        h = butterfly(h, up_weights, D_HIDDEN)
        h = jax.nn.gelu(h + up_bias, approximate=False)
        h = butterfly(h, down_weights, D_HIDDEN)
        y = jnp.einsum('bsh,hd->bsd', h, W_con) + b_con
        return y + down_bias
    x = x + _L0_xattn_ref(_layernorm(x, axis=-1), ctx_1024, ctx_1024, L0_xattn_W_q, L0_xattn_W_k, L0_xattn_W_v, L0_xattn_W_o, itok_BxS_8_8191, itok_BxS2_1_8191, mask_BxSxS2_if1)
    x = x + _L0_attn_ref(_layernorm(x, axis=-1), L0_attn_proj_mat, L0_attn_wq, L0_attn_bq, L0_attn_wk, L0_attn_bk, L0_attn_wv, L0_attn_bv, L0_attn_wo, L0_attn_bo, L0_attn_ln1_g, L0_attn_ln1_b, L0_attn_w1, L0_attn_b1, L0_attn_w2, L0_attn_b2, L0_attn_ln2_g, L0_attn_ln2_b)
    x = x + _L0_ffn_ref(_layernorm(x, axis=-1), L0_ffn_Wg, L0_ffn_bg, L0_ffn_W1, L0_ffn_b1, L0_ffn_W2, L0_ffn_b2)
    x = x + _L1_xattn_ref(_layernorm(x, axis=-1), ctx_1024, mask_BxS_ik0, L1_xattn_Wq, L1_xattn_Wkv, L1_xattn_Wout, L1_xattn_bout)
    x = x + _L1_attn_ref(_layernorm(x, axis=-1), L1_attn_ln_g, L1_attn_ln_b, L1_attn_W_in, L1_attn_conv_w, L1_attn_conv_b, L1_attn_W_x, L1_attn_W_dt, L1_attn_b_dt, L1_attn_A_log, L1_attn_Dskip, L1_attn_W_out)
    x = x + _L1_ffn_ref(_layernorm(x, axis=-1), L1_ffn_w_gate, L1_ffn_w_g, L1_ffn_w_u, L1_ffn_w_d)
    x = x + _L2_xattn_ref(ctx_1024, _layernorm(x, axis=-1), mask_BxS2_bf1, L2_xattn_ln_x_g, L2_xattn_ln_x_b, L2_xattn_ln_l_g, L2_xattn_ln_l_b, L2_xattn_qn_g, L2_xattn_kn_g, L2_xattn_Wq, L2_xattn_Wkv, L2_xattn_Wout, L2_xattn_bout)
    x = x + _L2_attn_ref(_layernorm(x, axis=-1), L2_attn_w_qkv, L2_attn_w_out, L2_attn_b_out, L2_attn_gamma, L2_attn_beta)
    x = x + _L2_ffn_ref(_layernorm(x, axis=-1), L2_ffn_gate_w, L2_ffn_wi_gate, L2_ffn_wi_up, L2_ffn_wo)
    x = x + _L3_xattn_ref(_layernorm(x, axis=-1), ctx_1024, L3_xattn_Wq, L3_xattn_Wk, L3_xattn_Wv, L3_xattn_Wo, L3_xattn_bo)
    x = x + _L3_attn_ref(_layernorm(x, axis=-1), L3_attn_Wq, L3_attn_bq, L3_attn_Wk, L3_attn_Wv, L3_attn_Wproj, L3_attn_bproj, L3_attn_Wr, L3_attn_br, L3_attn_b_nd)
    x = x + _L3_ffn_ref(_layernorm(x, axis=-1), L3_ffn_W_exp, L3_ffn_b_exp, L3_ffn_up_weights, L3_ffn_up_bias, L3_ffn_down_weights, L3_ffn_W_con, L3_ffn_b_con, L3_ffn_down_bias)
    return x

_drawn_inputs = setup_inputs


def setup_inputs(seed=0):
    import zlib

    import numpy as np

    out = dict(_drawn_inputs(seed))
    spreads = {'L0_attn_bq': (0.0, 0.383),
     'L0_attn_bk': (0.0, 0.1),
     'L0_attn_bv': (0.0, 0.1),
     'L0_attn_bo': (0.0, 0.1),
     'L0_attn_ln1_g': (1.0, 0.2),
     'L0_attn_ln1_b': (0.0, 0.1),
     'L0_attn_b1': (0.0, 0.347),
     'L0_attn_b2': (0.0, 0.1),
     'L0_attn_ln2_g': (1.0, 0.6),
     'L0_attn_ln2_b': (0.0, 0.8),
     'L1_xattn_bout': (0.0, 0.371),
     'L1_attn_ln_g': (1.0, 0.6),
     'L1_attn_ln_b': (0.0, 0.8),
     'L1_attn_conv_b': (0.0, 0.8),
     'L1_attn_b_dt': (-4.599999904632568, 0.6),
     'L1_attn_Dskip': (1.0, 0.6),
     'L2_xattn_ln_x_g': (1.0, 0.6),
     'L2_xattn_ln_x_b': (0.0, 0.8),
     'L2_xattn_ln_l_g': (1.0, 0.6),
     'L2_xattn_ln_l_b': (0.0, 0.8),
     'L2_xattn_qn_g': (1.0, 0.6),
     'L2_xattn_kn_g': (1.0, 0.6),
     'L2_xattn_bout': (0.0, 0.5),
     'L2_attn_b_out': (0.0, 0.1),
     'L2_attn_gamma': (1.0, 0.6),
     'L2_attn_beta': (0.0, 0.8),
     'L3_attn_bq': (0.0, 2.0),
     'L3_attn_bproj': (0.0, 0.5),
     'L3_attn_br': (0.0, 0.8),
     'L3_ffn_b_exp': (0.0, 0.1),
     'L3_ffn_up_bias': (0.0, 0.1),
     'L3_ffn_b_con': (0.0, 0.544),
     'L3_ffn_down_bias': (0.0, 0.568)}
    factors = {'L0_attn_proj_mat': 3.233,
     'L0_attn_wk': 3.763,
     'L0_ffn_bg': 3.25,
     'L0_ffn_b1': 8.0,
     'L0_ffn_b2': 8.0,
     'L1_attn_W_in': 8.0,
     'L1_attn_conv_w': 8.0,
     'L1_attn_W_x': 8.0,
     'L1_attn_W_dt': 8.0,
     'L1_attn_A_log': 8.0,
     'L1_attn_W_out': 8.0,
     'L1_ffn_w_gate': 8.0,
     'L1_ffn_w_g': 8.0,
     'L1_ffn_w_u': 8.0,
     'L1_ffn_w_d': 8.0,
     'L2_xattn_Wq': 8.0,
     'L2_xattn_Wkv': 4.261,
     'L2_xattn_Wout': 4.219,
     'L2_attn_w_qkv': 8.0,
     'L2_attn_w_out': 8.0,
     'L2_ffn_gate_w': 8.0,
     'L2_ffn_wi_gate': 8.0,
     'L2_ffn_wi_up': 8.0,
     'L2_ffn_wo': 8.0,
     'L3_xattn_bo': 64.0,
     'L3_attn_Wq': 23.489,
     'L3_attn_Wk': 8.0,
     'L3_attn_Wr': 8.0,
     'L3_attn_b_nd': 8.0,
     'L3_xattn_Wq': 3.647,
     'L3_xattn_Wk': 3.624}
    for name, (base, spread) in spreads.items():
        noise = np.random.default_rng([zlib.crc32(name.encode()), seed]).standard_normal(out[name].shape)
        drawn = base * np.exp(spread * noise) if base else spread * noise
        out[name] = jnp.asarray(drawn.astype(out[name].dtype))
    for name, factor in factors.items():
        out[name] = (out[name] * factor).astype(out[name].dtype)
    return out
```

```python
from collections import namedtuple
from contextlib import ExitStack, contextmanager

import numpy as np

import concourse.bass as bass
from concourse import mybir

SUBLAYERS = range(12)

ALU = mybir.AluOpType
ACT = mybir.ActivationFunctionType
F32 = mybir.dt.float32
BF16 = mybir.dt.bfloat16
I32 = mybir.dt.int32
U8 = mybir.dt.uint8
X = mybir.AxisListType.X

P = 128
B = 4
T = B * P
KEYS = 2048
CH = KEYS // P
HB = 4
E = 8
LN_EPS = 1e-5
MASKED = -1e30


@contextmanager
def stage(nc, prefix, names):
    fields, sems, every = [], [], []
    for entry in names.split():
        field, _, count = entry.partition("*")
        mine = [nc.alloc_semaphore(f"{prefix}_{field}{i}" if count else f"{prefix}_{field}") for i in range(int(count or 1))]
        fields.append(field)
        sems.append(mine if count else mine[0])
        every += mine
    with nc.Block() as block:
        yield block, namedtuple("Semaphores", fields)(*sems)
    for s in every:
        nc.gpsimd.sem_clear(s)
    for s in every:
        nc.release_semaphore(s)


class Chip:

    def __init__(self, nc, d):
        self.nc, self.d = nc, d
        self.x = nc.alloc_sbuf_tensor("x", [P, T], F32)
        self.xn = nc.alloc_sbuf_tensor("xn", [P, T], F32)
        self.ident = nc.alloc_sbuf_tensor("ident", [P, P], F32)
        self.ident_bf = nc.alloc_sbuf_tensor("ident_bf", [P, P], BF16)
        self.ones = nc.alloc_sbuf_tensor("ones", [P, P], F32)
        self.ones_bf = nc.alloc_sbuf_tensor("ones_bf", [P, P], BF16)
        self.mean = nc.alloc_sbuf_tensor("mean", [P, P], F32)
        self.eps = nc.alloc_sbuf_tensor("eps", [P, 1], F32)
        self.half_pi = nc.alloc_sbuf_tensor("half_pi", [P, 1], F32)
        self.select = nc.alloc_sbuf_tensor("select", [16, 16, P], F32)
        self.rank = nc.alloc_sbuf_tensor("rank", [P, B, E], F32)
        self.bank = [nc.alloc_psum_tensor(f"bank{i}", [P, T], F32) for i in range(8)]


class Queries:

    def __init__(self, qp):
        self.qp, self.latents, self.gains, self.key_norm = qp, None, None, None


def scratch(nc, frees, name, shape, dt):
    return frees.enter_context(nc.sbuf_tensor(name, shape, dt))


def setup(c):
    nc = c.nc
    with stage(nc, "setup", "loaded zeroed made") as (block, s):
        @block.sync
        def _(sp):
            sp.dma_start(c.x[:, :], c.d.xT).then_inc(s.loaded, 16)
            sp.dma_start(c.select[:, :, :], c.d.select).then_inc(s.loaded, 16)
            sp.dma_start(c.rank[:, :, :], c.d.rank).then_inc(s.loaded, 16)
            sp.wait_ge(s.loaded, 48)

        @block.gpsimd
        def _(pool):
            nc.gpsimd.memset(c.ident[:, :], 0.0).then_inc(s.zeroed, 1)
            nc.gpsimd.memset(c.ones[:, :], 1.0)
            nc.gpsimd.memset(c.ones_bf[:, :], 1.0)
            nc.gpsimd.memset(c.mean[:, :], 1.0 / P)
            nc.gpsimd.memset(c.eps[:, :], LN_EPS)
            nc.gpsimd.memset(c.half_pi[:, :], float(np.float32(np.pi / 2)))
            pool.wait_ge(s.zeroed, 1)
            nc.gpsimd.affine_select(out=c.ident[:, :], in_=c.ident[:, :], compare_op=ALU.not_equal, fill=1.0,
                                    base=0, pattern=[[-1, P]], channel_multiplier=1).then_inc(s.made, 1)
            pool.wait_ge(s.made, 1)
            nc.gpsimd.tensor_copy(c.ident_bf[:, :], c.ident[:, :])


def store(c):
    nc = c.nc
    with stage(nc, "store", "stored") as (block, s):
        @block.sync
        def _(sp):
            sp.dma_start(c.d.outT, c.x[:, :]).then_inc(s.stored, 16)
            sp.wait_ge(s.stored, 16)


def layernorm(c, name, src, out, gain=None, shift=None, also=None):
    nc = c.nc
    n = src.shape[-1]
    with nc.sbuf_tensor(f"{name}_xc", [P, n], F32) as xc, nc.sbuf_tensor(f"{name}_sq", [P, n], F32) as sq, \
            nc.sbuf_tensor(f"{name}_std", [P, n], F32) as std, \
            stage(nc, name, "mean_done centred squared var_done std_done inverted normed") as (block, s):
        mean_ps, var_ps = c.bank[0][:, 0:n], c.bank[1][:, 0:n]

        @block.tensor
        def _(pe):
            nc.tensor.matmul(mean_ps, c.mean[:, :], src, start=True, stop=True).then_inc(s.mean_done, 1)
            pe.wait_ge(s.squared, 1)
            nc.tensor.matmul(var_ps, c.mean[:, :], sq[:, :], start=True, stop=True).then_inc(s.var_done, 1)

        @block.scalar
        def _(act):
            act.wait_ge(s.centred, 1)
            nc.scalar.activation(sq[:, :], xc[:, :], ACT.Square).then_inc(s.squared, 1)
            act.wait_ge(s.var_done, 1)
            nc.scalar.activation(std[:, :], var_ps, ACT.Sqrt, bias=c.eps[:, 0:1]).then_inc(s.std_done, 1)

        @block.vector
        def _(dve):
            dve.wait_ge(s.mean_done, 1)
            nc.vector.tensor_tensor(xc[:, :], src, mean_ps, ALU.subtract).then_inc(s.centred, 1)
            dve.wait_ge(s.std_done, 1)
            nc.vector.reciprocal(std[:, :], std[:, :]).then_inc(s.inverted, 1)
            dve.wait_ge(s.inverted, 1)
            nc.vector.tensor_tensor(out, xc[:, :], std[:, :], ALU.mult).then_inc(s.normed, 1)
            if gain is not None:
                dve.wait_ge(s.normed, 1)
                nc.vector.tensor_scalar(out, out, gain, shift, ALU.mult, ALU.add)



def query_side(c, z, name, heads, scale, dq, wq, wk_t, gains=None):
    nc = c.nc
    with nc.sbuf_tensor(f"{name}_q", [dq, 2, T], F32) as q, nc.sbuf_tensor(f"{name}_sq", [dq, 2, T], F32) as sq, \
            nc.sbuf_tensor(f"{name}_rms", [dq, 2, T], F32) as rms, \
            stage(nc, name, "q_ready q_copied carried carried_copied squared sum_ready rms_ready rms_kept inverted scaled") as (block, s):
        q_ps, carried_ps, sum_ps = c.bank[0:2], c.bank[2:4], c.bank[4:6]

        @block.tensor
        def _(pe):
            def project(h):
                if h >= 2:
                    pe.wait_ge(s.q_copied, h - 1)
                nc.tensor.matmul(q_ps[h % 2][0:dq, :], wq[:, h, :], c.xn[:, :], start=True, stop=True).then_inc(s.q_ready, 1)

            def norm(h):
                pe.wait_ge(s.squared, h + 1)
                if h >= 2:
                    pe.wait_ge(s.rms_ready, h - 1)
                nc.tensor.matmul(sum_ps[h % 2][0:dq, :], c.ones[0:dq, 0:dq], sq[:, h % 2, :], start=True, stop=True).then_inc(s.sum_ready, 1)

            def carry(h):
                pe.wait_ge(s.scaled if gains is not None else s.q_copied, h + 1)
                if h >= 2:
                    pe.wait_ge(s.carried_copied, h - 1)
                nc.tensor.matmul(carried_ps[h % 2][:, :], wk_t[:, h, :], q[:, h % 2, :], start=True, stop=True).then_inc(s.carried, 1)

            project(0)
            for h in range(heads):
                if gains is not None:
                    norm(h)
                if h + 1 < heads:
                    project(h + 1)
                carry(h)

        @block.scalar
        def _(act):
            for h in range(heads):
                act.wait_ge(s.q_ready, h + 1)
                if h >= 2:
                    act.wait_ge(s.carried, h - 1)
                nc.scalar.activation(q[:, h % 2, :], q_ps[h % 2][0:dq, :], ACT.Copy, scale=scale).then_inc(s.q_copied, 1)
                if gains is not None:
                    act.wait_ge(s.q_copied, h + 1)
                    nc.scalar.activation(sq[:, h % 2, :], q[:, h % 2, :], ACT.Square).then_inc(s.squared, 1)
                    act.wait_ge(s.sum_ready, h + 1)
                    if h >= 2:
                        act.wait_ge(s.scaled, h - 1)
                    nc.scalar.activation(rms[:, h % 2, :], sum_ps[h % 2][0:dq, :], ACT.Sqrt, scale=1.0 / dq).then_inc(s.rms_ready, 1)

        @block.vector
        def _(dve):
            for h in range(heads):
                if gains is not None:
                    dve.wait_ge(s.rms_ready, h + 1)
                    nc.vector.tensor_scalar(rms[:, h % 2, :], rms[:, h % 2, :], 1e-8, None, ALU.max).then_inc(s.rms_kept, 1)
                    dve.wait_ge(s.rms_kept, h + 1)
                    nc.vector.reciprocal(rms[:, h % 2, :], rms[:, h % 2, :]).then_inc(s.inverted, 1)
                    dve.wait_ge(s.inverted, h + 1)
                    nc.vector.scalar_tensor_tensor(out=q[:, h % 2, :], in0=q[:, h % 2, :], scalar=gains, in1=rms[:, h % 2, :],
                                                   op0=ALU.mult, op1=ALU.mult).then_inc(s.scaled, 1)
                dve.wait_ge(s.carried, h + 1)
                nc.vector.tensor_copy(z.qp[:, :, h, :], carried_ps[h % 2][:, :].rearrange("p (b q) -> p b q", b=B)).then_inc(s.carried_copied, 1)


def attend_context(c, z, name, heads, ctx_t, ctx, chunks, one_more, rows=None, row_bias=None, mask=None, key_scale=None):
    nc = c.nc
    groups = heads // HB
    steps = B * groups
    PIECE = 4
    pieces = [(a, min(a + PIECE, chunks)) for a in range(0, chunks, PIECE)]
    NP = len(pieces)
    R = rows[1] if rows is not None else 0
    with ExitStack() as st:
        kt = scratch(nc, st, f"{name}_kt", [P, chunks, P], F32)
        kn = scratch(nc, st, f"{name}_kn", [P, chunks, P], F32)
        sc = scratch(nc, st, f"{name}_scores", [P, 2, chunks, HB * P], F32)
        part = scratch(nc, st, f"{name}_part", [P, NP, HB * P], F32)
        cmax = scratch(nc, st, f"{name}_cmax", [P, HB * P], F32)
        m = scratch(nc, st, f"{name}_m", [P, HB], F32)
        diag = scratch(nc, st, f"{name}_diag", [P, HB, P], F32)
        psum_rows = scratch(nc, st, f"{name}_rowsum", [P, HB * P], F32)
        den = scratch(nc, st, f"{name}_den", [P, HB * P], F32)
        rec = scratch(nc, st, f"{name}_rec", [P, HB * P], F32)
        if rows is not None:
            rt = scratch(nc, st, f"{name}_rows", [R, chunks, P], BF16)
        if mask is not None:
            mi = scratch(nc, st, f"{name}_mask", [P, chunks, P], I32)
            mb = scratch(nc, st, f"{name}_maskbias", [P, chunks, P], BF16)
        names = "scores_ready copied part_max col_max turned row_max diag_ready max_ready " \
                "shifted exps sum_step den_ready den_copied inverted mean_ready stored mask_in mask_ready mask_used rows_in rows_used kt_used kn_used"
        names += f" kt_in*{NP} kn_in*{NP}"
        block, s = st.enter_context(stage(nc, name, names))
        score_ps, turn_ps, max_ps, out_ps, den_ps = c.bank[0:4], c.bank[4], c.bank[5], c.bank[6], c.bank[7]
        order = [(ci, pi) for pi, (a, b_) in enumerate(pieces) for ci in range(a, b_)]

        def over_batches(eng, body):
            with eng.Fori(0, B - 1) as b:
                body(b, False)
            body(B - 1, True)

        def successor(b, g):
            return (b, g + 1) if g + 1 < groups else (b + 1, 0)

        @block.sync
        def _(sp):
            def load(b):
                sp.wait_ge(s.kt_used, b)
                for p, (a, e) in enumerate(pieces):
                    sp.dma_start(kt[:, a:e, :], ctx_t(b, a, e)).then_inc(s.kt_in[p], 16)
                if rows is not None:
                    sp.dma_start(rt[:, :, :], rows[0](b)).then_inc(s.rows_in, 16)
                if mask is not None:
                    sp.wait_ge(s.mask_ready, b)
                    sp.dma_start(mi[:, :, :], mask(b)).then_inc(s.mask_in, 16)
                sp.wait_ge(s.kn_used, b)
                for p, (a, e) in enumerate(pieces):
                    sp.dma_start(kn[:, a:e, :], ctx(b, a, e)).then_inc(s.kn_in[p], 16)

            with sp.Fori(0, B) as b:
                load(b)

        @block.tensor
        def _(pe):
            def scores(b, g):
                for ci, p in order:
                    n = (b * groups + g) * chunks + ci
                    if g == 0 and ci == pieces[p][0]:
                        pe.wait_ge(s.kt_in[p], 16 * b + 16)
                    if g == 0 and ci == 0:
                        if rows is not None:
                            pe.wait_ge(s.rows_in, 16 * b + 16)
                        if mask is not None:
                            pe.wait_ge(s.mask_ready, b + 1)
                    pe.wait_ge(s.copied, n + 1)
                    ps = score_ps[(g * chunks + ci) % 4]
                    more = (rows is not None) + (mask is not None)
                    mm = nc.tensor.matmul(ps[:, :].rearrange("p (h q) -> p h q", h=HB), kt[:, ci, :], z.qp[:, b, g * HB:(g + 1) * HB, :],
                                          start=True, stop=not more)
                    if mask is not None:
                        more -= 1
                        mm = nc.tensor.matmul(ps[:, :].rearrange("p (h q) -> p h q", h=HB), c.ident_bf[:, :],
                                              mb[:, ci, :].unsqueeze(1).to_broadcast([P, HB, P]), start=False, stop=not more)
                    if rows is not None:
                        mm = nc.tensor.matmul(ps[:, :].rearrange("p (h q) -> p h q", h=HB), rt[:, ci, :], row_bias(b, g), start=False, stop=True)
                    mm.then_inc(s.scores_ready, 1)
                if g == groups - 1:
                    pe.wait_ge(s.scores_ready, (b * groups + g + 1) * chunks)
                    pe.sem_inc(s.kt_used, 1)

            def weighted_sum(b, g):
                n = b * groups + g
                pe.wait_ge(s.stored, n + 2)
                for ci, p in order:
                    if ci == pieces[p][0]:
                        pe.wait_ge(s.exps, n * NP + p + 1)
                        if g == 0:
                            pe.wait_ge(s.kn_in[p], 16 * b + 16)
                    mm = nc.tensor.matmul(out_ps[:, :], kn[:, ci, :], sc[:, g % 2, ci, :], start=(ci == 0), stop=(ci == chunks - 1))
                mm.then_inc(s.mean_ready, 1)

            def turn(b, g):
                n = b * groups + g
                pe.wait_ge(s.col_max, n + 1)
                pe.wait_ge(s.row_max, n + 1)
                for h in range(HB):
                    mm = nc.tensor.transpose(turn_ps[:, h * P:(h + 1) * P], cmax[:, h * P:(h + 1) * P], c.ident[:, :])
                mm.then_inc(s.turned, 1)

            def denominators(b, g):
                n = b * groups + g
                pe.wait_ge(s.sum_step, (n + 1) * (chunks - 1))
                pe.wait_ge(s.den_copied, n + 1)
                nc.tensor.matmul(den_ps[:, :], c.ones[:, :], psum_rows[:, :], start=True, stop=True).then_inc(s.den_ready, 1)

            def spread_max(b, g):
                n = b * groups + g
                pe.wait_ge(s.diag_ready, n + 1)
                pe.wait_ge(s.shifted, n * NP + 1)
                nc.tensor.matmul(max_ps[:, :].rearrange("p (h q) -> p h q", h=HB), c.ones[:, :], diag[:, :, :],
                                 start=True, stop=True).then_inc(s.max_ready, 1)

            scores(0, 0)
            turn(0, 0)
            spread_max(0, 0)

            def body(b, last):
                for g in range(groups):
                    end = last and g == groups - 1
                    if not end:
                        scores(*successor(b, g))
                    weighted_sum(b, g)
                    if g == groups - 1:
                        pe.wait_ge(s.mean_ready, (b + 1) * groups)
                        pe.sem_inc(s.kn_used, 1)
                    if not end:
                        turn(*successor(b, g))
                    denominators(b, g)
                    if not end:
                        spread_max(*successor(b, g))

            over_batches(pe, body)

        @block.scalar
        def _(act):
            def copy(b, g, ci):
                n = (b * groups + g) * chunks + ci
                act.wait_ge(s.scores_ready, n + 1)
                nc.scalar.activation(sc[:, g % 2, ci, :], score_ps[(g * chunks + ci) % 4][:, :], ACT.Copy).then_inc(s.copied, 1)

            def exps(b, g, p):
                n = b * groups + g
                a, e = pieces[p]
                act.wait_ge(s.shifted, n * NP + p + 2)
                nc.scalar.activation(sc[:, g % 2, a:e, :], sc[:, g % 2, a:e, :], ACT.Exp).then_inc(s.exps, 1)

            def copies(b, g, lo, hi):
                if key_scale is None:
                    for ci in range(lo, hi):
                        if ci == 0:
                            act.wait_ge(s.stored, b * groups + g + 1)
                        copy(b, g, ci)

            copies(0, 0, 0, chunks)

            def body(b, last):
                for g in range(groups):
                    more = not (last and g == groups - 1)
                    cut = [0] + [chunks // 2 + (chunks // 2) * p // NP for p in range(NP)] + [chunks]
                    for p in range(NP):
                        if more:
                            copies(*successor(b, g), cut[p], cut[p + 1])
                        exps(b, g, p)
                    if more:
                        copies(*successor(b, g), cut[NP], cut[NP + 1])

            over_batches(act, body)

        @block.vector
        def _(dve):
            def scale_keys(b, g, ci):
                n = (b * groups + g) * chunks + ci
                if ci == 0:
                    dve.wait_ge(s.stored, b * groups + g + 1)
                dve.wait_ge(s.scores_ready, n + 1)
                add, factor = key_scale
                nc.vector.scalar_tensor_tensor(
                    out=sc[:, g % 2, ci, :].rearrange("p (h q) -> p h q", h=HB),
                    in0=score_ps[(g * chunks + ci) % 4][:, :].rearrange("p (h q) -> p h q", h=HB), scalar=add(b, ci),
                    in1=factor(b, g, ci).unsqueeze(2).to_broadcast([P, HB, P]),
                    op0=ALU.add, op1=ALU.mult).then_inc(s.copied, 1)

            def part_max(b, g, p):
                n = b * groups + g
                a, e = pieces[p]
                if key_scale is not None:
                    for ci in range(a, e):
                        scale_keys(b, g, ci)
                dve.wait_ge(s.copied, n * chunks + e + 4)
                if p == 0:
                    dve.wait_ge(s.col_max, n)
                nc.vector.tensor_reduce(part[:, p, :], sc[:, g % 2, a:e, :].rearrange("p c f -> p f c"), X, ALU.max).then_inc(s.part_max, 1)

            def col_max(b, g):
                n = b * groups + g
                dve.wait_ge(s.part_max, (n + 1) * NP)
                dve.wait_ge(s.turned, n)
                nc.vector.tensor_reduce(cmax[:, :], part[:, :, :].rearrange("p c f -> p f c"), X, ALU.max).then_inc(s.col_max, 1)

            def row_max(b, g):
                n = b * groups + g
                dve.wait_ge(s.turned, n + 1)
                nc.vector.tensor_reduce(m[:, :], turn_ps[:, :].rearrange("p (h k) -> p h k", h=HB), X, ALU.max).then_inc(s.row_max, 1)
                dve.wait_ge(s.row_max, n + 2)
                dve.wait_ge(s.max_ready, n)
                nc.vector.tensor_tensor(diag[:, :, :], c.ident[:, :].unsqueeze(1).to_broadcast([P, HB, P]),
                                        m[:, :].unsqueeze(2).to_broadcast([P, HB, P]), ALU.mult).then_inc(s.diag_ready, 1)

            def shift(b, g, p):
                n = b * groups + g
                a, e = pieces[p]
                dve.wait_ge(s.max_ready, n + 1)
                if p == 0:
                    dve.wait_ge(s.part_max, (n + 1) * NP)
                nc.vector.tensor_tensor(sc[:, g % 2, a:e, :], sc[:, g % 2, a:e, :], max_ps[:, :].unsqueeze(1).to_broadcast([P, e - a, HB * P]),
                                        ALU.subtract).then_inc(s.shifted, 1)

            def divide(b, g):
                n = b * groups + g
                dve.wait_ge(s.den_ready, n + 1)
                nc.vector.tensor_scalar(den[:, :], den_ps[:, :], 1.0 if one_more else 0.0, None, ALU.add).then_inc(s.den_copied, 1)
                dve.wait_ge(s.den_copied, n + 2)
                nc.vector.reciprocal(rec[:, :], den[:, :]).then_inc(s.inverted, 1)
                dve.wait_ge(s.inverted, n + 1)
                dve.wait_ge(s.mean_ready, n + 1)
                nc.vector.tensor_tensor(z.qp[:, b, g * HB:(g + 1) * HB, :], out_ps[:, :].rearrange("p (h q) -> p h q", h=HB),
                                        rec[:, :].rearrange("p (h q) -> p h q", h=HB), ALU.mult).then_inc(s.stored, 1)

            def convert_mask(b):
                dve.wait_ge(s.mask_in, 16 * b + 16)
                dve.wait_ge(s.kt_used, b)
                nc.vector.tensor_scalar(mb[:, :, :], mi[:, :, :], 0.0, MASKED, ALU.is_equal, ALU.mult).then_inc(s.mask_ready, 1)

            dve.sem_inc(s.copied, 4)
            dve.sem_inc(s.stored, 2)
            dve.sem_inc(s.row_max, 1)
            dve.sem_inc(s.den_copied, 1)
            dve.sem_inc(s.shifted, 1)
            if mask is not None:
                convert_mask(0)
            for p in range(NP):
                part_max(0, 0, p)
            col_max(0, 0)
            row_max(0, 0)

            def body(b, last):
                for g in range(groups):
                    more = not (last and g == groups - 1)
                    for p in range(NP):
                        shift(b, g, p)
                    if more:
                        for p in range(NP):
                            part_max(*successor(b, g), p)
                        col_max(*successor(b, g))
                        row_max(*successor(b, g))
                    if mask is not None and g == groups - 2 and not last:
                        convert_mask(b + 1)
                    divide(b, g)

            over_batches(dve, body)

        @block.gpsimd
        def _(pool):
            def sums(b, g):
                n = b * groups + g
                pool.wait_ge(s.den_ready, n)
                for k, (ci, p) in enumerate(order):
                    if ci == pieces[p][0] and ci:
                        pool.wait_ge(s.exps, n * NP + p + 1)
                    if ci == 1:
                        pool.wait_ge(s.exps, n * NP + 1)
                        nc.gpsimd.tensor_tensor(psum_rows[:, :], sc[:, g % 2, 0, :], sc[:, g % 2, 1, :], ALU.add).then_inc(s.sum_step, 1)
                    elif ci > 1:
                        pool.wait_ge(s.sum_step, n * (chunks - 1) + ci - 1)
                        nc.gpsimd.tensor_tensor(psum_rows[:, :], psum_rows[:, :], sc[:, g % 2, ci, :], ALU.add).then_inc(s.sum_step, 1)

            def body(b, last):
                for g in range(groups):
                    sums(b, g)

            over_batches(pool, body)


def output_side(c, z, name, heads, dq, wv, wout, bout=None):
    nc = c.nc
    pairs = heads // 2
    with nc.sbuf_tensor(f"{name}_o", [P, 2, T], F32) as o, stage(nc, name, "values_ready values_copied projected") as (block, s):
        @block.tensor
        def _(pe):
            def values(j):
                if j >= 2:
                    pe.wait_ge(s.values_copied, j - 1)
                for k in range(2):
                    mm = nc.tensor.matmul(c.bank[j % 2][k * dq:(k + 1) * dq, :].rearrange("p (b q) -> p b q", b=B), wv[:, 2 * j + k, :],
                                          z.qp[:, :, 2 * j + k, :], start=True, stop=True)
                mm.then_inc(s.values_ready, 1)

            values(0)
            for j in range(pairs):
                if j + 1 < pairs:
                    values(j + 1)
                pe.wait_ge(s.values_copied, j + 1)
                mm = nc.tensor.matmul(c.bank[2][:, :], wout[:, j, :], o[:, j % 2, :], start=(j == 0), stop=(j == pairs - 1))
                mm.then_inc(s.projected, 1)

        @block.scalar
        def _(act):
            for j in range(pairs):
                act.wait_ge(s.values_ready, j + 1)
                if j >= 2:
                    act.wait_ge(s.projected, j - 1)
                nc.scalar.activation(o[:, j % 2, :], c.bank[j % 2][:, :], ACT.Copy).then_inc(s.values_copied, 1)

        @block.vector
        def _(dve):
            dve.wait_ge(s.projected, pairs)
            nc.vector.scalar_tensor_tensor(out=c.x[:, :], in0=c.bank[2][:, :], scalar=bout if bout is not None else 0.0, in1=c.x[:, :],
                                           op0=ALU.add, op1=ALU.add)


def load(c, name, pairs):
    nc = c.nc
    with stage(nc, name, "loaded") as (block, s):
        @block.sync
        def _(sp):
            for dst, src in pairs:
                sp.dma_start(dst, src).then_inc(s.loaded, 16)
            sp.wait_ge(s.loaded, 16 * len(pairs))


def split_to_dram(c, name, src, dst):
    nc = c.nc
    m, n = src.shape
    with nc.sbuf_tensor(f"{name}_parts", [m, 3, n], BF16) as parts, nc.sbuf_tensor(f"{name}_rest", [m, 2, n], F32) as rest, \
            stage(nc, name, "step stored") as (block, s):
        @block.vector
        def _(dve):
            left = src
            for i in range(3):
                nc.vector.tensor_copy(parts[:, i, :], left).then_inc(s.step, 1)
                dve.wait_ge(s.step, 2 * i + 1)
                if i < 2:
                    nc.vector.tensor_tensor(rest[:, i, :], left, parts[:, i, :], ALU.subtract).then_inc(s.step, 1)
                    dve.wait_ge(s.step, 2 * i + 2)
                    left = rest[:, i, :]

        @block.sync
        def _(sp):
            sp.wait_ge(s.step, 5)
            for i in range(3):
                sp.dma_start(dst[i], parts[:, i, :]).then_inc(s.stored, 16)
            sp.wait_ge(s.stored, 48)


def context_views(d):
    def ctx_t(b, a, e):
        return d.ctxT[:, bass.ds(b * CH + a, e - a) if not isinstance(b, int) else slice(b * CH + a, b * CH + e), :]

    def ctx(b, a, e):
        return d.ctx[:, bass.ds(b * CH + a, e - a) if not isinstance(b, int) else slice(b * CH + a, b * CH + e), :]

    return ctx_t, ctx


def l0_xattn(c):
    nc, d = c.nc, c.d
    with ExitStack() as st:
        heads, dh = 16, 8
        z = Queries(scratch(nc, st, "qp0", [P, B, heads, P], F32))
        rb = scratch(nc, st, "l0_slopes", [9, heads, P], BF16)
        layernorm(c, "l0x_ln", c.x[:, :], c.xn[:, :])
        with ExitStack() as st2:
            wq = scratch(nc, st2, "l0_wq", [P, P], F32)
            wk = scratch(nc, st2, "l0_wk", [P, P], F32)
            hm = scratch(nc, st2, "l0_headmask", [P, heads], F32)
            pos_i = scratch(nc, st2, "l0_pos_i", [P, B * CH], I32)
            pos = scratch(nc, st2, "l0_pos", [P, B * CH], F32)
            q = scratch(nc, st2, "l0_q", [P, T], F32)
            qm = scratch(nc, st2, "l0_qm", [P, 2, T], F32)
            load(c, "l0x_load", [(wq[:, :], d.L0_xattn_W_qT), (wk[:, :], d.L0_xattn_W_k), (hm[:, :], d.headmask),
                                 (pos_i[:, :], d.key_pos), (rb[:, :, :], d.slope_rows)])
            with stage(nc, "l0x_q", "q_ready q_scaled masked carried copied cast") as (block, s):
                @block.tensor
                def _(pe):
                    nc.tensor.matmul(c.bank[0][:, :], wq[:, :], c.xn[:, :], start=True, stop=True).then_inc(s.q_ready, 1)
                    for h in range(heads):
                        pe.wait_ge(s.masked, h + 1)
                        if h >= 2:
                            pe.wait_ge(s.copied, h - 1)
                        nc.tensor.matmul(c.bank[1 + h % 2][:, :], wk[:, :], qm[:, h % 2, :], start=True, stop=True).then_inc(s.carried, 1)

                @block.scalar
                def _(act):
                    act.wait_ge(s.q_ready, 1)
                    nc.scalar.activation(q[:, :], c.bank[0][:, :], ACT.Copy, scale=dh ** -0.5).then_inc(s.q_scaled, 1)
                    act.wait_ge(s.q_scaled, 1)
                    for h in range(heads):
                        if h >= 2:
                            act.wait_ge(s.carried, h - 1)
                        nc.scalar.activation(qm[:, h % 2, :], q[:, :], ACT.Copy, scale=hm[:, h:h + 1]).then_inc(s.masked, 1)

                @block.vector
                def _(dve):
                    nc.vector.tensor_copy(pos[:, :], pos_i[:, :]).then_inc(s.cast, 1)
                    for h in range(heads):
                        dve.wait_ge(s.carried, h + 1)
                        nc.vector.tensor_copy(z.qp[:, :, h, :], c.bank[1 + h % 2][:, :].rearrange("p (b q) -> p b q", b=B)).then_inc(s.copied, 1)

            split_to_dram(c, "l0x_pos", pos[:, :], [d.pos_parts[i] for i in range(3)])

        rows_dram = d.pos_parts.rearrange("i p n -> i (p n)").rearrange("i (b c k) -> i b c k", b=B, k=P)
        with stage(nc, "l0x_rows", "spread") as (block, s):
            @block.sync
            def _(sp):
                for i in range(3):
                    sp.dma_start(d.pos_rows[3 * i:3 * i + 3], rows_dram[i:i + 1].to_broadcast([3, B, CH, P])).then_inc(s.spread, 16)
                sp.wait_ge(s.spread, 48)
        ctx_t, ctx = context_views(d)
        attend_context(c, z, "l0x", heads, ctx_t, ctx, CH, True,
                       rows=(lambda b: d.pos_rows[:, bass.ds(b, 1), :, :].rearrange("r b c k -> r (b c) k"), 9),
                       row_bias=lambda b, g: rb[:, g * HB:(g + 1) * HB, :],
                       mask=lambda b: d.mask_t[:, bass.ds(b * CH, CH), :])
        with ExitStack() as st2:
            wv = scratch(nc, st2, "l0_wv", [P, heads, P], F32)
            wo = scratch(nc, st2, "l0_wo", [P, P], F32)
            o = scratch(nc, st2, "l0_o", [P, T], F32)
            load(c, "l0x_load2", [(wv[:, :, :], d.L0_xattn_W_v_blocks), (wo[:, :], d.L0_xattn_W_oT)])
            with stage(nc, "l0x_out", "values_ready values_copied projected") as (block, s):
                @block.tensor
                def _(pe):
                    for h in range(heads):
                        mm = nc.tensor.matmul(c.bank[0][:, :].rearrange("p (b q) -> p b q", b=B), wv[:, h, :], z.qp[:, :, h, :],
                                              start=(h == 0), stop=(h == heads - 1))
                    mm.then_inc(s.values_ready, 1)
                    pe.wait_ge(s.values_copied, 1)
                    nc.tensor.matmul(c.bank[1][:, :], wo[:, :], o[:, :], start=True, stop=True).then_inc(s.projected, 1)

                @block.scalar
                def _(act):
                    act.wait_ge(s.values_ready, 1)
                    nc.scalar.activation(o[:, :], c.bank[0][:, :], ACT.Copy).then_inc(s.values_copied, 1)

                @block.vector
                def _(dve):
                    dve.wait_ge(s.projected, 1)
                    nc.vector.tensor_tensor(c.x[:, :], c.x[:, :], c.bank[1][:, :], ALU.add)


def l3_xattn(c):
    nc, d = c.nc, c.d
    with ExitStack() as st:
        heads, dq = 8, 64
        z = Queries(scratch(nc, st, "qp9", [P, B, heads, P], F32))
        layernorm(c, "l3x_ln", c.x[:, :], c.xn[:, :])
        with ExitStack() as st2:
            wq = scratch(nc, st2, "l3_wq", [P, heads, dq], F32)
            wk = scratch(nc, st2, "l3_wk", [dq, heads, P], F32)
            load(c, "l3x_load", [(wq[:, :, :], d.L3_xattn_Wq), (wk[:, :, :], d.L3_xattn_WkT)])
            query_side(c, z, "l3x_q", heads, dq ** -0.5, dq, wq, wk)
        ctx_t, ctx = context_views(d)
        attend_context(c, z, "l3x", heads, ctx_t, ctx, CH, False)
        with ExitStack() as st2:
            wv = scratch(nc, st2, "l3_wv", [P, heads, dq], F32)
            wo = scratch(nc, st2, "l3_wo", [P, heads // 2, P], F32)
            bo = scratch(nc, st2, "l3_bo", [P, 1], F32)
            load(c, "l3x_load2", [(wv[:, :, :], d.L3_xattn_Wv), (wo[:, :, :], d.L3_xattn_Wo), (bo[:, :], d.L3_xattn_bo)])
            output_side(c, z, "l3x_out", heads, dq, wv, wo, bo[:, 0:1])


def l1_xattn(c):
    nc, d = c.nc, c.d
    with ExitStack() as st:
        heads, dq = 16, 64
        z = Queries(scratch(nc, st, "qp3", [P, B, heads, P], F32))
        mrows = scratch(nc, st, "l1_mask_rows", [3, B, P], BF16)
        layernorm(c, "l1x_ln", c.x[:, :], c.xn[:, :])
        with ExitStack() as st2:
            wq = scratch(nc, st2, "l1_wq", [P, heads, dq], F32)
            wk = scratch(nc, st2, "l1_wk", [dq, heads, P], F32)
            mi = scratch(nc, st2, "l1_mi", [B, P], I32)
            mf = scratch(nc, st2, "l1_mf", [B, P], F32)
            load(c, "l1x_load", [(wq[:, :, :], d.L1_xattn_Wq), (wk[:, :, :], d.L1_xattn_WkT), (mi[:, :], d.query_mask)])
            query_side(c, z, "l1x_q", heads, dq ** -0.5, dq, wq, wk)
            with stage(nc, "l1x_mask", "made") as (block, s):
                @block.vector
                def _(dve):
                    nc.vector.tensor_scalar(mf[:, :], mi[:, :], 1.0, 1e6, ALU.subtract, ALU.mult).then_inc(s.made, 1)
            split_to_dram(c, "l1x_parts", mf[:, :], [d.mask_parts[i] for i in range(3)])
            load(c, "l1x_load_rows", [(mrows[:, :, :], d.mask_parts)])
        ctx_t, ctx = context_views(d)
        attend_context(c, z, "l1x", heads, ctx_t, ctx, CH, False,
                       rows=(lambda b: d.ones_rows, 3),
                       row_bias=lambda b, g: mrows[:, bass.ds(b, 1), :].to_broadcast([3, HB, P]))
        with ExitStack() as st2:
            wv = scratch(nc, st2, "l1_wv", [P, heads, dq], F32)
            wo = scratch(nc, st2, "l1_wo", [P, heads // 2, P], F32)
            bo = scratch(nc, st2, "l1_bo", [P, 1], F32)
            load(c, "l1x_load2", [(wv[:, :, :], d.L1_xattn_Wv), (wo[:, :, :], d.L1_xattn_Wout), (bo[:, :], d.L1_xattn_bout)])
            output_side(c, z, "l1x_out", heads, dq, wv, wo, bo[:, 0:1])



class Steps:

    def __init__(self, eng, sem):
        self.eng, self.sem, self.n = eng, sem, 0

    def __call__(self, instruction):
        self.n += 1
        instruction.then_inc(self.sem, 1)
        self.eng.wait_ge(self.sem, self.n)


def route(c, name, wg, bg, w_t, top, capacity=None):
    nc = c.nc
    with ExitStack() as st:
        def t3(n):
            return scratch(nc, st, f"{name}_{n}", [P, B, E], F32)

        def t2(n):
            return scratch(nc, st, f"{name}_{n}", [P, B], F32)

        score, eq, second, expd = t3("score"), t3("eq"), t3("second"), t3("expd")
        chosen = [t3("chosen0"), t3("chosen1")]
        weighed = [t3("weighed0"), t3("weighed1")]
        top_v = [t2("top0"), t2("top1")]
        rank_top, total, e2 = t2("rank_top"), t2("total"), t2("e2")
        turned_sb = scratch(nc, st, f"{name}_turned", [E, 4, T], F32)
        count = scratch(nc, st, f"{name}_count", [E, 2, T], F32)
        ones_row = scratch(nc, st, f"{name}_ones", [E, T], F32)
        block, s = st.enter_context(stage(nc, name, "scored step to_exp exp_done ready turned out_step"))

        def over_e(v):
            return v[:, :].unsqueeze(2).to_broadcast([P, B, E])

        sources = [weighed[0]] if capacity is None else [chosen[0], chosen[1], weighed[0], weighed[1]]

        @block.tensor
        def _(pe):
            for b in range(B):
                mm = nc.tensor.matmul(c.bank[0][:, b * E:(b + 1) * E], c.xn[:, b * P:(b + 1) * P], wg, start=True, stop=True)
            mm.then_inc(s.scored, 1)
            pe.wait_ge(s.ready, 1)
            for k, src in enumerate(sources):
                for b in range(B):
                    mm = nc.tensor.transpose(c.bank[1 + k][0:E, b * P:(b + 1) * P], src[:, b, :], c.ident[:, :])
            mm.then_inc(s.turned, 1)

        @block.scalar
        def _(act):
            if top == 1:
                return
            act.wait_ge(s.to_exp, 1)
            if capacity is None:
                nc.scalar.activation(e2[:, :], e2[:, :], ACT.Exp).then_inc(s.exp_done, 1)
            else:
                nc.scalar.activation(expd[:, :, :], expd[:, :, :], ACT.Exp).then_inc(s.exp_done, 1)

        @block.vector
        def _(dve):
            step = Steps(dve, s.step)
            v = nc.vector

            def choose(src, k):
                step(v.tensor_reduce(top_v[k][:, :], src[:, :, :], X, ALU.max))
                step(v.tensor_tensor(eq[:, :, :], src[:, :, :], over_e(top_v[k]), ALU.is_equal))
                step(v.tensor_tensor(eq[:, :, :], eq[:, :, :], c.rank[:, :, :], ALU.mult))
                step(v.tensor_reduce(rank_top[:, :], eq[:, :, :], X, ALU.max))
                step(v.tensor_tensor(chosen[k][:, :, :], eq[:, :, :], over_e(rank_top), ALU.is_equal))

            def without_first(src):
                step(v.scalar_tensor_tensor(out=second[:, :, :], in0=chosen[0][:, :, :], scalar=MASKED, in1=src[:, :, :],
                                            op0=ALU.mult, op1=ALU.add))

            dve.wait_ge(s.scored, 1)
            ps = c.bank[0][:, 0:B * E].rearrange("p (b e) -> p b e", b=B)
            if bg is not None:
                step(v.tensor_tensor(score[:, :, :], ps, bg.unsqueeze(1).to_broadcast([P, B, E]), ALU.add))
            else:
                step(v.tensor_copy(score[:, :, :], ps))
            if capacity is not None:
                step(v.tensor_reduce(total[:, :], score[:, :, :], X, ALU.max))
                v.tensor_tensor(expd[:, :, :], score[:, :, :], over_e(total), ALU.subtract).then_inc(s.to_exp, 1)
                dve.wait_ge(s.exp_done, 1)
                step(v.tensor_reduce(total[:, :], expd[:, :, :], X, ALU.add))
                step(v.reciprocal(total[:, :], total[:, :]))
                step(v.tensor_tensor(score[:, :, :], expd[:, :, :], over_e(total), ALU.mult))
            choose(score, 0)
            if top == 2:
                without_first(score)
                choose(second, 1)
                if capacity is None:
                    v.tensor_tensor(e2[:, :], top_v[1][:, :], top_v[0][:, :], ALU.subtract).then_inc(s.to_exp, 1)
                    dve.wait_ge(s.exp_done, 1)
                    step(v.tensor_scalar(total[:, :], e2[:, :], 1.0, None, ALU.add))
                    step(v.reciprocal(top_v[0][:, :], total[:, :]))
                    step(v.tensor_tensor(top_v[1][:, :], e2[:, :], top_v[0][:, :], ALU.mult))
                else:
                    step(v.tensor_tensor(total[:, :], top_v[0][:, :], top_v[1][:, :], ALU.add))
                    step(v.reciprocal(total[:, :], total[:, :]))
                    step(v.tensor_tensor(top_v[0][:, :], top_v[0][:, :], total[:, :], ALU.mult))
                    step(v.tensor_tensor(top_v[1][:, :], top_v[1][:, :], total[:, :], ALU.mult))
                step(v.tensor_tensor(weighed[0][:, :, :], chosen[0][:, :, :], over_e(top_v[0]), ALU.mult))
                if capacity is None:
                    step(v.tensor_tensor(weighed[1][:, :, :], chosen[1][:, :, :], over_e(top_v[1]), ALU.mult))
                    v.tensor_tensor(weighed[0][:, :, :], weighed[0][:, :, :], weighed[1][:, :, :], ALU.add).then_inc(s.ready, 1)
                else:
                    v.tensor_tensor(weighed[1][:, :, :], chosen[1][:, :, :], over_e(top_v[1]), ALU.mult).then_inc(s.ready, 1)
            else:
                v.tensor_copy(weighed[0][:, :, :], chosen[0][:, :, :]).then_inc(s.ready, 1)
            if capacity is None:
                dve.wait_ge(s.turned, 1)
                step(v.tensor_copy(w_t[:, :], c.bank[1][0:E, :]))
                return
            step(v.memset(ones_row[:, :], 1.0))
            dve.wait_ge(s.turned, 1)
            for k in range(4):
                step(v.tensor_copy(turned_sb[:, k, :], c.bank[1 + k][0:E, :]))
            for k in range(2):
                step(v.tensor_tensor_scan(count[:, k, :], ones_row[:, :], turned_sb[:, k, :], 0.0, ALU.mult, ALU.add))
                step(v.scalar_tensor_tensor(out=turned_sb[:, 2 + k, :], in0=count[:, k, :], scalar=float(capacity), in1=turned_sb[:, 2 + k, :],
                                            op0=ALU.is_le, op1=ALU.mult))
            step(v.tensor_tensor(w_t[:, :], turned_sb[:, 2, :], turned_sb[:, 3, :], ALU.add))


def experts(c, name, w_t, up, gate, down, blocks, width, b1=None, b2=None):
    nc = c.nc
    F = blocks * width
    glu = gate is not None
    RING = 4
    with ExitStack() as st:
        wu = scratch(nc, st, f"{name}_wu", [P, 2, F], F32)
        wg = scratch(nc, st, f"{name}_wg", [P, 2, F], F32) if glu else None
        wd = scratch(nc, st, f"{name}_wd", [width, 2, blocks, P], F32)
        spread = scratch(nc, st, f"{name}_spread", [P, E, T], F32)
        act_out = scratch(nc, st, f"{name}_act", [width, RING, T], F32)
        prod = scratch(nc, st, f"{name}_prod", [width, RING, T], F32) if glu else None
        hidden = scratch(nc, st, f"{name}_hidden", [width, RING, T], F32)
        block, s = st.enter_context(stage(nc, name, "w_in0 w_in1 up_used down_used spread_ready spread_copied "
                                                    "up_ready activated multiplied weighed accumulated"))
        w_in = [s.w_in0, s.w_in1]
        acc = c.bank[7]
        banks = 2 if glu else RING
        up_ps, gate_ps = c.bank[0:banks], c.bank[2:4]
        spread_ps = c.bank[5:7]
        per = 2 * blocks
        LAG = 2
        loads = 48 if glu else 32

        @block.sync
        def _(sp):
            with sp.Fori(0, E // 2) as i:
                for k in range(2):
                    sp.wait_ge(s.up_used, 2 * i + k + 1)
                    sp.dma_start(wu[:, k, :], up[:, bass.ds(2 * i + k, 1), :].rearrange("p o f -> p (o f)")).then_inc(w_in[k], 16)
                    if glu:
                        sp.dma_start(wg[:, k, :], gate[:, bass.ds(2 * i + k, 1), :].rearrange("p o f -> p (o f)")).then_inc(w_in[k], 16)
                    sp.wait_ge(s.down_used, 2 * i + k + 1)
                    sp.dma_start(wd[:, k, :, :], down[:, bass.ds(2 * i + k, 1), :, :].rearrange("p o j d -> p (o j) d")).then_inc(w_in[k], 16)

        @block.tensor
        def _(pe):
            pe.sem_inc(s.up_used, 2)
            pe.sem_inc(s.down_used, 2)
            pe.sem_inc(s.accumulated, RING)
            for e in range(E):
                if e >= 2:
                    pe.wait_ge(s.spread_copied, e - 1)
                nc.tensor.matmul(spread_ps[e % 2][:, :], c.select[0:E, e, :], w_t[:, :], start=True, stop=True).then_inc(s.spread_ready, 1)
            nc.tensor.matmul(acc[:, :], c.ident[:, :], c.x[:, :], start=True, stop=False, skip_group_check=True)
            if b2 is not None:
                nc.tensor.matmul(acc[:, :], b2, w_t[:, :], start=False, stop=False, skip_group_check=True)

            def first(i, k):
                slot, j = divmod(k, blocks)
                n = i * per + k
                if j == 0:
                    pe.wait_ge(w_in[slot], loads * i + loads)
                pe.wait_ge(s.multiplied if glu else s.activated, n + 1 + RING - banks)
                if glu:
                    nc.tensor.matmul(gate_ps[k % banks][0:width, :], wg[:, slot, j * width:(j + 1) * width], c.xn[:, :], start=True, stop=True)
                nc.tensor.matmul(up_ps[k % banks][0:width, :], wu[:, slot, j * width:(j + 1) * width], c.xn[:, :],
                                 start=True, stop=True).then_inc(s.up_ready, 1)
                if j == blocks - 1:
                    pe.wait_ge(s.up_ready, n + 1)
                    pe.sem_inc(s.up_used, 1)

            def second(i, k, end):
                slot, j = divmod(k, blocks)
                n = i * per + k
                pe.wait_ge(s.weighed, n + 1 + RING)
                nc.tensor.matmul(acc[:, :], wd[:, slot, j, :], hidden[:, k % RING, :], start=False, stop=end,
                                 skip_group_check=True).then_inc(s.accumulated, 1)
                if j == blocks - 1:
                    pe.wait_ge(s.accumulated, n + 1 + RING)
                    pe.sem_inc(s.down_used, 1)

            for k in range(LAG):
                first(0, k)
            with pe.Fori(0, E // 2 - 1) as i:
                for k in range(per):
                    first(*((i, k + LAG) if k + LAG < per else (i + 1, k + LAG - per)))
                    second(i, k, False)
            for k in range(per):
                if k + LAG < per:
                    first(E // 2 - 1, k + LAG)
                second(E // 2 - 1, k, k == per - 1)

        @block.scalar
        def _(act):
            if not glu:
                act.sem_inc(s.activated, RING)
            for e in range(E):
                act.wait_ge(s.spread_ready, e + 1)
                nc.scalar.activation(spread[:, e, :], spread_ps[e % 2][:, :], ACT.Copy).then_inc(s.spread_copied, 1)
            with act.Fori(0, E // 2) as i:
                for k in range(per):
                    slot, j = divmod(k, blocks)
                    n = i * per + k
                    act.wait_ge(s.up_ready, n + 1)
                    act.wait_ge(s.multiplied if glu else s.weighed, n + 1)
                    if glu:
                        nc.scalar.activation(act_out[:, k % RING, :], gate_ps[k % banks][0:width, :], ACT.Silu).then_inc(s.activated, 1)
                    else:
                        nc.scalar.activation(act_out[:, k % RING, :], up_ps[k % banks][0:width, :], ACT.Relu,
                                             bias=b1[:, bass.ds((2 * i + slot) * blocks + j, 1)]).then_inc(s.activated, 1)

        @block.vector
        def _(dve):
            dve.sem_inc(s.weighed, RING)
            if glu:
                dve.sem_inc(s.multiplied, RING)
            dve.wait_ge(s.spread_copied, E)
            with dve.Fori(0, E // 2) as i:
                for k in range(per):
                    slot = k // blocks
                    n = i * per + k
                    src = act_out
                    if glu:
                        dve.wait_ge(s.activated, n + 1)
                        dve.wait_ge(s.weighed, n + 1)
                        nc.vector.tensor_tensor(prod[:, k % RING, :], act_out[:, k % RING, :], up_ps[k % banks][0:width, :],
                                                ALU.mult).then_inc(s.multiplied, 1)
                        src = prod
                        dve.wait_ge(s.multiplied, n + 1 + RING)
                    else:
                        dve.wait_ge(s.activated, n + 1 + RING)
                    dve.wait_ge(s.accumulated, n + 1)
                    nc.vector.tensor_tensor(hidden[:, k % RING, :], src[:, k % RING, :],
                                            spread[0:width, bass.ds(2 * i + slot, 1), :].rearrange("p o t -> p (o t)"),
                                            ALU.mult).then_inc(s.weighed, 1)
            dve.wait_ge(s.accumulated, E * blocks + RING)
            nc.vector.tensor_copy(c.x[:, :], acc[:, :])


def l0_ffn(c):
    nc, d = c.nc, c.d
    layernorm(c, "l0f_ln", c.x[:, :], c.xn[:, :])
    with ExitStack() as st:
        w_t = scratch(nc, st, "l0f_w_t", [E, T], F32)
        wg = scratch(nc, st, "l0f_router", [P, E], F32)
        bg = scratch(nc, st, "l0f_bg", [P, E], F32)
        b1 = scratch(nc, st, "l0f_b1", [P, E * 4], F32)
        b2 = scratch(nc, st, "l0f_b2", [E, P], F32)
        load(c, "l0f_load", [(wg[:, :], d.L0_ffn_Wg), (bg[:, :], d.L0_ffn_bg.to_broadcast([P, E])), (b1[:, :], d.L0_ffn_b1), (b2[:, :], d.L0_ffn_b2)])
        route(c, "l0f_route", wg[:, :], bg[:, :], w_t, 1)
        experts(c, "l0f", w_t, d.L0_ffn_W1, None, d.L0_ffn_W2, 4, P, b1, b2[:, :])


def l1_ffn(c):
    nc, d = c.nc, c.d
    layernorm(c, "l1f_ln", c.x[:, :], c.xn[:, :])
    with ExitStack() as st:
        w_t = scratch(nc, st, "l1f_w_t", [E, T], F32)
        wg = scratch(nc, st, "l1f_router", [P, E], F32)
        load(c, "l1f_load", [(wg[:, :], d.L1_ffn_w_gate)])
        route(c, "l1f_route", wg[:, :], None, w_t, 2)
        experts(c, "l1f", w_t, d.L1_ffn_w_u, d.L1_ffn_w_g, d.L1_ffn_w_d, 2, 88)


def l2_ffn(c):
    nc, d = c.nc, c.d
    layernorm(c, "l2f_ln", c.x[:, :], c.xn[:, :])
    with ExitStack() as st:
        w_t = scratch(nc, st, "l2f_w_t", [E, T], F32)
        wg = scratch(nc, st, "l2f_router", [P, E], F32)
        load(c, "l2f_load", [(wg[:, :], d.L2_ffn_gate_w)])
        route(c, "l2f_route", wg[:, :], None, w_t, 2, capacity=max(int(T / E * 1.25), 1))
        experts(c, "l2f", w_t, d.L2_ffn_wi_up, d.L2_ffn_wi_gate, d.L2_ffn_wo, 4, P)




def l0_attn(c):
    nc, d = c.nc, c.d
    heads, dh = 16, 8
    ROUND = 1.5 * 2.0 ** 23
    TURN = -6.283185
    layernorm(c, "l0a_ln", c.x[:, :], c.xn[:, :])
    with ExitStack() as st:
        def t(name, shape):
            return scratch(nc, st, f"l0a_{name}", shape, F32)

        x2, x1, q, k, v = t("x2", [P, T]), t("x1", [P, T]), t("q", [P, T]), t("k", [P, T]), t("v", [P, B, P])
        bias, bv = t("bias", [P, 13]), t("bv", [P, P])
        w4 = t("w4", [P, 4, P])
        load(c, "l0a_load", [(w4[:, :, :], d.L0_attn_w4), (bias[:, :], d.L0_attn_bias), (bv[:, :], d.L0_attn_bv.to_broadcast([P, P]))])
        BQ, BK, BO, G1, S1, G2, S2, B2, B1 = range(9)

        def col(i):
            return bias[:, i:i + 1]

        layernorm(c, "l0a_ln1", c.xn[:, :], x2[:, :], col(G1), col(S1))
        with stage(nc, "l0a_qkv", "projected") as (block, s):
            @block.tensor
            def _(pe):
                nc.tensor.matmul(c.bank[0][:, :], w4[:, 0, :], x2[:, :], start=True, stop=True).then_inc(s.projected, 1)
                nc.tensor.matmul(c.bank[1][:, :], w4[:, 1, :], x2[:, :], start=True, stop=True).then_inc(s.projected, 1)
                for b in range(B):
                    mm = nc.tensor.matmul(c.bank[2][:, b * P:(b + 1) * P], x2[:, b * P:(b + 1) * P], w4[:, 2, :], start=True, stop=True)
                mm.then_inc(s.projected, 1)

            @block.scalar
            def _(act):
                act.wait_ge(s.projected, 1)
                nc.scalar.activation(q[:, :], c.bank[0][:, :], ACT.Identity, bias=col(BQ))
                act.wait_ge(s.projected, 2)
                nc.scalar.activation(k[:, :], c.bank[1][:, :], ACT.Identity, bias=col(BK))

            @block.vector
            def _(dve):
                dve.wait_ge(s.projected, 3)
                nc.vector.tensor_tensor(v[:, :, :], c.bank[2][:, :].rearrange("p (b j) -> p b j", b=B),
                                        bv[:, :].unsqueeze(1).to_broadcast([P, B, P]), ALU.add)

        with ExitStack() as st2:
            def t2(name, shape):
                return scratch(nc, st2, f"l0a_{name}", shape, F32)

            proj = t2("proj", [P, heads, P])
            fq = t2("fq", [P, 2, heads, T])
            fk = t2("fk", [P, 2, B, heads * P])
            turns, whole, fold = t2("turns", [P, 3, T]), t2("whole", [P, 3, 2, T]), t2("fold", [P, 3, 2, T])
            kv, out, out_t = t2("kv", [P, 2, T]), t2("out", [P, B, P]), t2("out_t", [P, T])
            load(c, "l0a_load2", [(proj[:, :, :], d.L0_attn_proj)])
            n_items = heads + B * heads // HB
            with stage(nc, "l0a_feat", "angle_ready turns_ready whole_ready folded waved kv_ready kv_copied out_ready out_copied "
                                       "turned turned_copied") as (block, s):
                @block.tensor
                def _(pe):
                    for i in range(n_items):
                        if i >= 3:
                            pe.wait_ge(s.turns_ready, i - 2)
                        if i < heads:
                            mm = nc.tensor.matmul(c.bank[i % 3][:, :], proj[:, i, :], q[:, :], start=True, stop=True)
                        else:
                            b, g = divmod(i - heads, heads // HB)
                            mm = nc.tensor.matmul(c.bank[i % 3][:, :].rearrange("p (h m) -> p h m", h=HB), k[:, b * P:(b + 1) * P],
                                                  proj[:, g * HB:(g + 1) * HB, :], start=True, stop=True)
                        mm.then_inc(s.angle_ready, 1)
                    pe.wait_ge(s.waved, n_items)
                    for f in range(2):
                        for b in range(B):
                            for h in range(heads):
                                at = slice(b * P + h * dh, b * P + (h + 1) * dh)
                                mm = nc.tensor.matmul(c.bank[3 + f][:, at], fk[:, f, b, h * P:(h + 1) * P], v[:, b, h * dh:(h + 1) * dh],
                                                      start=True, stop=True)
                        mm.then_inc(s.kv_ready, 1)
                    pe.wait_ge(s.kv_copied, 2)
                    for b in range(B):
                        for h in range(heads):
                            at = slice(b * P + h * dh, b * P + (h + 1) * dh)
                            for f in range(2):
                                mm = nc.tensor.matmul(c.bank[5][:, at], fq[:, f, h, b * P:(b + 1) * P], kv[:, f, at], start=(f == 0), stop=(f == 1))
                    mm.then_inc(s.out_ready, 1)
                    pe.wait_ge(s.out_copied, 1)
                    for b in range(B):
                        mm = nc.tensor.transpose(c.bank[6][:, b * P:(b + 1) * P], out[:, b, :], c.ident[:, :])
                    mm.then_inc(s.turned, 1)
                    pe.wait_ge(s.turned_copied, 1)
                    nc.tensor.matmul(c.bank[7][:, :], w4[:, 3, :], out_t[:, :], start=True, stop=True).then_inc(s.out_ready, 1)

                @block.scalar
                def _(act):
                    def waves(i):
                        act.wait_ge(s.folded, i + 1)
                        if i < heads:
                            cos, sin = fq[:, 0, i, :], fq[:, 1, i, :]
                        else:
                            b, g = divmod(i - heads, heads // HB)
                            cos, sin = fk[:, 0, b, g * T:(g + 1) * T], fk[:, 1, b, g * T:(g + 1) * T]
                        nc.scalar.activation(sin, fold[:, i % 3, 0, :], ACT.Sin, scale=TURN)
                        nc.scalar.activation(cos, fold[:, i % 3, 1, :], ACT.Sin, scale=TURN, bias=c.half_pi[:, 0:1]).then_inc(s.waved, 1)

                    for i in range(n_items):
                        act.wait_ge(s.angle_ready, i + 1)
                        if i >= 3:
                            act.wait_ge(s.folded, i - 2)
                        nc.scalar.activation(turns[:, i % 3, :], c.bank[i % 3][:, :], ACT.Copy,
                                             scale=float(dh ** -0.5 / (2 * np.pi))).then_inc(s.turns_ready, 1)
                        if i >= 2:
                            waves(i - 2)
                    waves(n_items - 2)
                    waves(n_items - 1)
                    for f in range(2):
                        act.wait_ge(s.kv_ready, f + 1)
                        nc.scalar.activation(kv[:, f, :], c.bank[3 + f][:, :], ACT.Copy).then_inc(s.kv_copied, 1)
                    act.wait_ge(s.out_ready, 1)
                    nc.scalar.activation(out[:, :, :], c.bank[5][:, :].rearrange("p (b j) -> p b j", b=B), ACT.Copy, scale=1.0 / P).then_inc(s.out_copied, 1)
                    act.wait_ge(s.turned, 1)
                    nc.scalar.activation(out_t[:, :], c.bank[6][:, :], ACT.Copy).then_inc(s.turned_copied, 1)

                @block.gpsimd
                def _(pool):
                    for i in range(n_items):
                        pool.wait_ge(s.turns_ready, i + 1)
                        if i >= 3:
                            pool.wait_ge(s.folded, i - 2)
                        nc.gpsimd.tensor_scalar(whole[:, i % 3, 0, :], turns[:, i % 3, :], ROUND, None, ALU.add)
                        nc.gpsimd.tensor_scalar(whole[:, i % 3, 1, :], turns[:, i % 3, :], 0.25, ROUND, ALU.add, ALU.add).then_inc(s.whole_ready, 1)

                @block.vector
                def _(dve):
                    for i in range(n_items):
                        dve.wait_ge(s.whole_ready, i + 1)
                        if i >= 3:
                            dve.wait_ge(s.waved, i - 2)
                        for f in range(2):
                            mm = nc.vector.scalar_tensor_tensor(out=fold[:, i % 3, f, :], in0=whole[:, i % 3, f, :], scalar=ROUND,
                                                                in1=turns[:, i % 3, :], op0=ALU.subtract, op1=ALU.subtract)
                        mm.then_inc(s.folded, 1)
                    dve.wait_ge(s.out_ready, 2)
                    nc.vector.scalar_tensor_tensor(out=x1[:, :], in0=c.bank[7][:, :], scalar=col(BO), in1=c.xn[:, :], op0=ALU.add, op1=ALU.add)
        layernorm(c, "l0a_ln2", x1[:, :], x2[:, :], col(G2), col(S2))
        w1, w2, hid = t("w1", [P, T]), t("w2", [P, 4, P]), t("hid", [P, 4, T])
        load(c, "l0a_load3", [(w1[:, :], d.L0_attn_w1), (w2[:, :, :], d.L0_attn_w2)])
        with stage(nc, "l0a_ffn", "up_ready relued down_ready added") as (block, s):
            @block.tensor
            def _(pe):
                for j in range(4):
                    nc.tensor.matmul(c.bank[j][:, :], w1[:, j * P:(j + 1) * P], x2[:, :], start=True, stop=True).then_inc(s.up_ready, 1)
                for j in range(4):
                    pe.wait_ge(s.relued, j + 1)
                    mm = nc.tensor.matmul(c.bank[4][:, :], w2[:, j, :], hid[:, j, :], start=(j == 0), stop=(j == 3))
                mm.then_inc(s.down_ready, 1)

            @block.scalar
            def _(act):
                for j in range(4):
                    act.wait_ge(s.up_ready, j + 1)
                    nc.scalar.activation(hid[:, j, :], c.bank[j][:, :], ACT.Relu, bias=col(B1 + j)).then_inc(s.relued, 1)

            @block.vector
            def _(dve):
                nc.vector.tensor_tensor(c.x[:, :], c.x[:, :], x1[:, :], ALU.add).then_inc(s.added, 1)
                dve.wait_ge(s.down_ready, 1)
                dve.wait_ge(s.added, 1)
                nc.vector.scalar_tensor_tensor(out=c.x[:, :], in0=c.bank[4][:, :], scalar=col(B2), in1=c.x[:, :], op0=ALU.add, op1=ALU.add)


def l1_attn(c):
    nc, d = c.nc, c.d
    N, DR, CONV = 16, 8, 4
    layernorm(c, "l1a_ln", c.x[:, :], c.xn[:, :])
    with ExitStack() as st:
        def t(name, shape):
            return scratch(nc, st, f"l1a_{name}", shape, F32)

        x2 = t("x2", [P, T])
        gs = t("gs", [P, 2])
        w_in, conv, w_x, w_dt = t("w_in", [P, 4, P]), t("conv", [P, 2, CONV]), t("w_x", [P, 2, DR + 2 * N]), t("w_dt", [DR, 2, P])
        cols, a_log, w_out = t("cols", [P, 2, 3]), t("a_log", [P, 2, N]), t("w_out", [P, 2, P])
        load(c, "l1a_load", [(gs[:, :], d.L1_attn_ln), (w_in[:, :, :], d.L1_attn_W_in), (conv[:, :, :], d.L1_attn_conv_w),
                             (w_x[:, :, :], d.L1_attn_W_x), (w_dt[:, :, :], d.L1_attn_W_dt), (cols[:, :, :], d.L1_attn_cols),
                             (a_log[:, :, :], d.L1_attn_A_log), (w_out[:, :, :], d.L1_attn_W_out)])
        CB, BDT, DS = range(3)
        layernorm(c, "l1a_ln1", c.xn[:, :], x2[:, :], gs[:, 0:1], gs[:, 1:2])
        PAD = CONV - 1
        u = t("u", [P, 2, B, PAD + P])
        conved, uc, z = t("conved", [P, 2, B, P]), t("uc", [P, 2, T]), t("z", [P, 2, T])
        dt_r, bs, cs = t("dt_r", [DR, T]), t("bs", [N, T]), t("cs", [N, T])
        pre, neg, dt, dtu = t("pre", [P, 2, T]), t("neg", [P, 2, T]), t("dt", [P, 2, T]), t("dtu", [P, 2, T])
        with stage(nc, "l1a_conv", "padded in_ready in_copied conv_step uc_ready x_ready x_copied dt_ready pre_ready folded "
                                   "expd logd step a_ready") as (block, s):
            @block.tensor
            def _(pe):
                for j in range(4):
                    nc.tensor.matmul(c.bank[j][:, :], w_in[:, j, :], x2[:, :], start=True, stop=True).then_inc(s.in_ready, 1)
                pe.wait_ge(s.uc_ready, 2)
                for k, (lo, hi) in enumerate(((0, DR), (DR, DR + N), (DR + N, DR + 2 * N))):
                    for j in range(2):
                        mm = nc.tensor.matmul(c.bank[4 + k][0:hi - lo, :], w_x[:, j, lo:hi], uc[:, j, :], start=(j == 0), stop=(j == 1))
                    mm.then_inc(s.x_ready, 1)
                pe.wait_ge(s.x_copied, 1)
                pe.wait_ge(s.in_copied, 4)
                for j in range(2):
                    nc.tensor.matmul(c.bank[j][:, :], w_dt[:, j, :], dt_r[:, :], start=True, stop=True).then_inc(s.dt_ready, 1)

            @block.gpsimd
            def _(pool):
                nc.gpsimd.memset(u[:, :, :, 0:PAD], 0.0).then_inc(s.padded, 1)

            @block.scalar
            def _(act):
                for j in range(2):
                    act.wait_ge(s.in_ready, j + 1)
                    nc.scalar.activation(u[:, j, :, PAD:], c.bank[j][:, :].rearrange("p (b l) -> p b l", b=B), ACT.Copy).then_inc(s.in_copied, 1)
                for j in range(2):
                    act.wait_ge(s.in_ready, j + 3)
                    nc.scalar.activation(z[:, j, :], c.bank[2 + j][:, :], ACT.Silu).then_inc(s.in_copied, 1)
                for j in range(2):
                    act.wait_ge(s.conv_step, CONV * (j + 1))
                    nc.scalar.activation(uc[:, j, :], conved[:, j, :, :].rearrange("p b l -> p (b l)"), ACT.Silu,
                                         bias=cols[:, j, CB:CB + 1]).then_inc(s.uc_ready, 1)
                for k, dst in enumerate((dt_r, bs, cs)):
                    act.wait_ge(s.x_ready, k + 1)
                    nc.scalar.activation(dst[:, :], c.bank[4 + k][0:dst.shape[0], :], ACT.Copy).then_inc(s.x_copied, 1)
                act.wait_ge(s.folded, 2)
                nc.scalar.activation(neg[:, :, :], neg[:, :, :], ACT.Exp, scale=-1.0).then_inc(s.expd, 1)
                nc.scalar.activation(a_log[:, :, :], a_log[:, :, :], ACT.Exp).then_inc(s.a_ready, 1)
                act.wait_ge(s.expd, 1)
                nc.scalar.activation(neg[:, :, :], neg[:, :, :], ACT.Ln, bias=1.0).then_inc(s.logd, 1)

            @block.vector
            def _(dve):
                v = nc.vector
                dve.wait_ge(s.padded, 1)
                for j in range(2):
                    dve.wait_ge(s.in_copied, j + 1)
                    for k in range(CONV):
                        src = u[:, j, :, k:k + P]
                        if k == 0:
                            v.tensor_scalar(conved[:, j, :, :], src, conv[:, j, 0:1], None, ALU.mult).then_inc(s.conv_step, 1)
                        else:
                            dve.wait_ge(s.conv_step, CONV * j + k)
                            v.scalar_tensor_tensor(out=conved[:, j, :, :], in0=src, scalar=conv[:, j, k:k + 1], in1=conved[:, j, :, :],
                                                   op0=ALU.mult, op1=ALU.add).then_inc(s.conv_step, 1)
                for j in range(2):
                    dve.wait_ge(s.dt_ready, j + 1)
                    v.tensor_scalar(pre[:, j, :], c.bank[j][:, :], cols[:, j, BDT:BDT + 1], None, ALU.add).then_inc(s.pre_ready, 1)
                    dve.wait_ge(s.pre_ready, j + 1)
                    v.scalar_tensor_tensor(out=neg[:, j, :], in0=pre[:, j, :], scalar=-1.0, in1=pre[:, j, :], op0=ALU.mult, op1=ALU.max).then_inc(s.folded, 1)
                step = Steps(dve, s.step)
                dve.wait_ge(s.logd, 1)
                step(v.scalar_tensor_tensor(out=dt[:, :, :], in0=pre[:, :, :], scalar=0.0, in1=neg[:, :, :], op0=ALU.max, op1=ALU.add))
                step(v.tensor_tensor(dtu[:, :, :], dt[:, :, :], uc[:, :, :], ALU.mult))
                dve.wait_ge(s.a_ready, 1)
                step(v.tensor_scalar(a_log[:, :, :], a_log[:, :, :], -1.0, None, ALU.mult))

        decay, drive, state, seen = t("decay", [P, 2, T]), t("drive", [P, 2, T]), t("state", [P, 2, T]), t("seen", [P, 2, T])
        b_sb = t("b_sb", [P, 2, T])
        y = t("y", [P, 2, T])
        items = 2 * N
        with stage(nc, "l1a_scan", "b_ready c_ready b_copied decayed reset driven scanned seen_ready summed y_step projected") as (block, s):
            @block.tensor
            def _(pe):
                def spread(k):
                    if k >= 2:
                        pe.wait_ge(s.b_copied, k - 1)
                    nc.tensor.matmul(c.bank[k % 2][:, :], c.select[:, k, :], bs[:, :], start=True, stop=True).then_inc(s.b_ready, 1)
                    if k >= 2:
                        pe.wait_ge(s.seen_ready, 2 * k - 2)
                    nc.tensor.matmul(c.bank[2 + k % 2][:, :], c.select[:, k, :], cs[:, :], start=True, stop=True).then_inc(s.c_ready, 1)

                spread(0)
                for k in range(N):
                    if k + 1 < N:
                        spread(k + 1)
                    for j in range(2):
                        n = 2 * k + j
                        pe.wait_ge(s.seen_ready, n + 1)
                        nc.tensor.matmul(c.bank[4 + j][:, :], c.ident[:, :], seen[:, n % 2, :], start=(k == 0), stop=(k == N - 1)).then_inc(s.summed, 1)
                pe.wait_ge(s.y_step, 4)
                for j in range(2):
                    mm = nc.tensor.matmul(c.bank[6][:, :], w_out[:, j, :], y[:, j, :], start=(j == 0), stop=(j == 1))
                mm.then_inc(s.projected, 1)

            @block.scalar
            def _(act):
                for k in range(N):
                    act.wait_ge(s.b_ready, k + 1)
                    if k >= 2:
                        act.wait_ge(s.driven, 2 * k - 2)
                    nc.scalar.activation(b_sb[:, k % 2, :], c.bank[k % 2][:, :], ACT.Copy).then_inc(s.b_copied, 1)
                    for j in range(2):
                        n = 2 * k + j
                        if n >= 2:
                            act.wait_ge(s.scanned, n - 1)
                        nc.scalar.activation(decay[:, n % 2, :], dt[:, j, :], ACT.Exp, scale=a_log[:, j, k:k + 1]).then_inc(s.decayed, 1)

            @block.gpsimd
            def _(pool):
                for k in range(N):
                    for j in range(2):
                        n = 2 * k + j
                        pool.wait_ge(s.decayed, n + 1)
                        nc.gpsimd.memset(decay[:, n % 2, :].rearrange("p (b l) -> p b l", b=B)[:, :, 0:1], 0.0).then_inc(s.reset, 1)
                        pool.wait_ge(s.b_copied, k + 1)
                        if n >= 2:
                            pool.wait_ge(s.scanned, n - 1)
                        nc.gpsimd.tensor_tensor(drive[:, n % 2, :], dtu[:, j, :], b_sb[:, k % 2, :], ALU.mult).then_inc(s.driven, 1)

            @block.vector
            def _(dve):
                v = nc.vector
                for k in range(N):
                    for j in range(2):
                        n = 2 * k + j
                        dve.wait_ge(s.reset, n + 1)
                        dve.wait_ge(s.driven, n + 1)
                        if n >= 2:
                            dve.wait_ge(s.seen_ready, n - 1)
                        v.tensor_tensor_scan(state[:, n % 2, :], decay[:, n % 2, :], drive[:, n % 2, :], 0.0, ALU.mult, ALU.add).then_inc(s.scanned, 1)
                        dve.wait_ge(s.scanned, n + 1)
                        dve.wait_ge(s.c_ready, k + 1)
                        if n >= 2:
                            dve.wait_ge(s.summed, n - 1)
                        v.tensor_tensor(seen[:, n % 2, :], state[:, n % 2, :], c.bank[2 + k % 2][:, :], ALU.mult).then_inc(s.seen_ready, 1)
                for j in range(2):
                    dve.wait_ge(s.summed, items)
                    v.scalar_tensor_tensor(out=y[:, j, :], in0=uc[:, j, :], scalar=cols[:, j, DS:DS + 1], in1=c.bank[4 + j][:, :],
                                           op0=ALU.mult, op1=ALU.add).then_inc(s.y_step, 1)
                    dve.wait_ge(s.y_step, 2 * j + 1)
                    v.tensor_tensor(y[:, j, :], y[:, j, :], z[:, j, :], ALU.mult).then_inc(s.y_step, 1)
                v.tensor_tensor(c.x[:, :], c.x[:, :], c.xn[:, :], ALU.add).then_inc(s.y_step, 1)
                dve.wait_ge(s.y_step, 5)
                dve.wait_ge(s.projected, 1)
                v.tensor_tensor(c.x[:, :], c.x[:, :], c.bank[6][:, :], ALU.add)


def l2_attn(c):
    nc, d = c.nc, c.d
    DEPTH = 6
    layernorm(c, "l2a_ln", c.x[:, :], c.xn[:, :])
    with ExitStack() as st:
        def t(name, shape):
            return scratch(nc, st, f"l2a_{name}", shape, F32)

        y, x2 = t("y", [P, T]), t("x2", [P, T])
        w, wo, cols = t("w", [P, 3 * P]), t("wo", [P, P]), t("cols", [P, 3])
        v_t, q, q_tok, k = t("v_t", [P, T]), t("q", [P, B, P]), t("q_tok", [P, B, P]), t("k", [P, B, P])
        top, total = t("top", [P, 2, B]), t("total", [P, 2, B])
        m, out = t("m", [P, B, P]), t("out", [P, T])
        with stage(nc, "l2a_copy", "copied") as (block, s):
            @block.vector
            def _(dve):
                nc.vector.tensor_copy(y[:, :], c.xn[:, :]).then_inc(s.copied, 1)

        with nc.Fori(0, DEPTH) as layer:
            load(c, "l2a_load", [(w[:, :], d.L2_attn_w_qkv[bass.ds(layer, 1)].rearrange("o p n -> (o p) n")),
                                 (wo[:, :], d.L2_attn_w_out[bass.ds(layer, 1)].rearrange("o p n -> (o p) n")),
                                 (cols[:, :], d.L2_attn_cols[bass.ds(layer, 1)].rearrange("o p n -> (o p) n"))])
            layernorm(c, "l2a_lni", y[:, :], x2[:, :], cols[:, 0:1], cols[:, 1:2])
            with stage(nc, "l2a", "projected v_copied top_ready shifted expd total_ready normed turned turned_copied m_ready m_copied "
                                  "out_ready out_copied added") as (block, s):
                def b3(ap):
                    return ap.rearrange("p (b j) -> p b j", b=B)

                def wide(v):
                    return v.unsqueeze(2).to_broadcast([P, B, P])

                @block.tensor
                def _(pe):
                    nc.tensor.matmul(c.bank[0][:, :], w[:, 0:P], x2[:, :], start=True, stop=True).then_inc(s.projected, 1)
                    for b in range(B):
                        mm = nc.tensor.matmul(c.bank[1][:, b * P:(b + 1) * P], x2[:, b * P:(b + 1) * P], w[:, P:2 * P], start=True, stop=True)
                    mm.then_inc(s.projected, 1)
                    nc.tensor.matmul(c.bank[2][:, :], w[:, 2 * P:], x2[:, :], start=True, stop=True).then_inc(s.projected, 1)
                    pe.wait_ge(s.normed, 1)
                    for b in range(B):
                        mm = nc.tensor.transpose(c.bank[3][:, b * P:(b + 1) * P], q[:, b, :], c.ident[:, :])
                    mm.then_inc(s.turned, 1)
                    pe.wait_ge(s.turned_copied, 1)
                    pe.wait_ge(s.normed, 2)
                    for b in range(B):
                        mm = nc.tensor.matmul(c.bank[4][:, b * P:(b + 1) * P], k[:, b, :], q_tok[:, b, :], start=True, stop=True)
                    mm.then_inc(s.m_ready, 1)
                    pe.wait_ge(s.m_copied, 1)
                    pe.wait_ge(s.v_copied, 1)
                    for b in range(B):
                        mm = nc.tensor.matmul(c.bank[5][:, b * P:(b + 1) * P], m[:, b, :], v_t[:, b * P:(b + 1) * P], start=True, stop=True)
                    mm.then_inc(s.out_ready, 1)
                    pe.wait_ge(s.out_copied, 1)
                    nc.tensor.matmul(c.bank[6][:, :], wo[:, :], out[:, :], start=True, stop=True).then_inc(s.out_ready, 1)

                @block.scalar
                def _(act):
                    for n, dst in enumerate((q, k)):
                        act.wait_ge(s.shifted, n + 1)
                        nc.scalar.activation(dst[:, :, :], dst[:, :, :], ACT.Exp).then_inc(s.expd, 1)
                    act.wait_ge(s.projected, 3)
                    nc.scalar.activation(v_t[:, :], c.bank[2][:, :], ACT.Copy).then_inc(s.v_copied, 1)
                    act.wait_ge(s.turned, 1)
                    nc.scalar.activation(q_tok[:, :, :], b3(c.bank[3][:, :]), ACT.Copy).then_inc(s.turned_copied, 1)
                    act.wait_ge(s.m_ready, 1)
                    nc.scalar.activation(m[:, :, :], b3(c.bank[4][:, :]), ACT.Copy).then_inc(s.m_copied, 1)
                    act.wait_ge(s.out_ready, 1)
                    nc.scalar.activation(out[:, :], c.bank[5][:, :], ACT.Copy).then_inc(s.out_copied, 1)

                @block.vector
                def _(dve):
                    v = nc.vector
                    for n, dst in enumerate((q, k)):
                        ps = b3(c.bank[n][:, :])
                        dve.wait_ge(s.projected, n + 1)
                        v.tensor_reduce(top[:, n, :], ps, X, ALU.max).then_inc(s.top_ready, 1)
                        dve.wait_ge(s.top_ready, n + 1)
                        v.tensor_tensor(dst[:, :, :], ps, wide(top[:, n, :]), ALU.subtract).then_inc(s.shifted, 1)
                    for n, dst in enumerate((q, k)):
                        dve.wait_ge(s.expd, n + 1)
                        v.tensor_reduce(total[:, n, :], dst[:, :, :], X, ALU.add).then_inc(s.total_ready, 1)
                        dve.wait_ge(s.total_ready, 2 * n + 1)
                        v.reciprocal(total[:, n, :], total[:, n, :]).then_inc(s.total_ready, 1)
                        dve.wait_ge(s.total_ready, 2 * n + 2)
                        v.tensor_tensor(dst[:, :, :], dst[:, :, :], wide(total[:, n, :]), ALU.mult).then_inc(s.normed, 1)
                    dve.wait_ge(s.out_ready, 2)
                    v.scalar_tensor_tensor(out=y[:, :], in0=c.bank[6][:, :], scalar=cols[:, 2:3], in1=y[:, :], op0=ALU.add, op1=ALU.add)
        with stage(nc, "l2a_add", "added") as (block, s):
            @block.vector
            def _(dve):
                nc.vector.tensor_tensor(c.x[:, :], c.x[:, :], y[:, :], ALU.add)


def normalize_context(c, z, wk):
    nc, d = c.nc, c.d
    heads, dq = 16, 64
    BLOCKS = B * KEYS // T
    with ExitStack() as st:
        def t(name, shape, dt=F32):
            return scratch(nc, st, f"l2n_{name}", shape, dt)

        raw, sq, std, xn, nat = t("raw", [P, 2, T]), t("sq", [P, 2, T]), t("std", [P, 2, T]), t("xn", [P, 2, T]), t("nat", [P, 2, T])
        ksq = t("ksq", [P, 2, heads * dq])
        block, s = st.enter_context(stage(nc, "l2n", "raw_in0 raw_in1 mean_ready centred squared var_ready std_ready inverted scaled normed stored0 stored1 "
                                                     "turned nat_copied nat_stored0 nat_stored1 keys_ready keys_squared reduced"))
        raw_in, stored, nat_stored = [s.raw_in0, s.raw_in1], [s.stored0, s.stored1], [s.nat_stored0, s.nat_stored1]

        def over_blocks(eng, step, tail):
            with eng.Fori(0, BLOCKS // 2 - 1) as i:
                for k in range(2):
                    step(2 * i + k, k, False)
            step(BLOCKS - 2, 0, False)
            step(BLOCKS - 1, 1, True)
            tail()

        @block.sync
        def _(sp):
            def raw_load(n, k):
                sp.dma_start(raw[:, k, :].rearrange("p (j x) -> p j x", j=4), d.ctxT[:, bass.ds(4 * n, 4), :]).then_inc(raw_in[k], 16)

            def put(n, k, latents, n_of_slot):
                sp.wait_ge(s.normed, n + 1)
                to_t = d.latT if latents else d.ctxnT[:, bass.ds(4 * n, 4), :]
                sp.dma_start(to_t, xn[:, k, :].rearrange("p (j x) -> p j x", j=4)).then_inc(stored[k], 16)
                sp.wait_ge(s.nat_copied, n + 1)
                to_n = d.lat if latents else d.ctxn[:, bass.ds(4 * n, 4), :]
                sp.dma_start(to_n, nat[:, k, :].rearrange("p (j x) -> p j x", j=4)).then_inc(nat_stored[k], 16)

            raw_load(0, 0)
            raw_load(1, 1)
            with sp.Fori(0, BLOCKS // 2 - 1) as i:
                for k in range(2):
                    sp.wait_ge(s.centred, 2 * i + k + 1)
                    raw_load(2 * i + k + 2, k)
                    put(2 * i + k, k, False, i)
            for n in range(BLOCKS - 2, BLOCKS + 1):
                put(n, n % 2, n == BLOCKS, n // 2)
            sp.wait_ge(stored[0], 16 * (BLOCKS // 2 + 1))
            sp.wait_ge(stored[1], 16 * (BLOCKS // 2))
            sp.wait_ge(nat_stored[0], 16 * (BLOCKS // 2 + 1))
            sp.wait_ge(nat_stored[1], 16 * (BLOCKS // 2))

        @block.tensor
        def _(pe):
            def mean(n, k, latents):
                if latents:
                    src = z.latents[:, :]
                else:
                    pe.wait_ge(raw_in[k], 16 * (n // 2 + 1) if isinstance(n, int) else 8 * (n - k) + 16)
                    src = raw[:, k, :]
                nc.tensor.matmul(c.bank[0][:, :], c.mean[:, :], src, start=True, stop=True).then_inc(s.mean_ready, 1)

            def var(n, k):
                pe.wait_ge(s.squared, n + 1)
                nc.tensor.matmul(c.bank[1][:, :], c.mean[:, :], sq[:, k, :], start=True, stop=True).then_inc(s.var_ready, 1)

            def turn(n, k):
                pe.wait_ge(s.normed, n + 1)
                pe.wait_ge(s.nat_copied, n)
                for j in range(4):
                    mm = nc.tensor.transpose(c.bank[2][:, j * P:(j + 1) * P], xn[:, k, j * P:(j + 1) * P], c.ident[:, :])
                mm.then_inc(s.turned, 1)

            def keys(n, k, j):
                pe.wait_ge(s.keys_squared, 4 * n + j + 1)
                for f in range(2):
                    mm = nc.tensor.matmul(c.bank[4 + 2 * (j % 2) + f][:, :], xn[:, k, j * P:(j + 1) * P], wk[:, f * T:(f + 1) * T], start=True, stop=True)
                mm.then_inc(s.keys_ready, 1)

            def step(n, k, latents):
                mean(n + 1, 1 - k, latents)
                keys(n, k, 0)
                keys(n, k, 1)
                var(n + 1, 1 - k)
                keys(n, k, 2)
                keys(n, k, 3)
                turn(n + 1, 1 - k)

            def tail():
                for j in range(4):
                    keys(BLOCKS, 0, j)

            mean(0, 0, False)
            var(0, 0)
            turn(0, 0)
            over_blocks(pe, step, tail)

        @block.scalar
        def _(act):
            def square(n, k):
                act.wait_ge(s.centred, n + 1)
                act.wait_ge(s.var_ready, n)
                nc.scalar.activation(sq[:, k, :], xn[:, k, :], ACT.Square).then_inc(s.squared, 1)

            def root(n, k):
                act.wait_ge(s.var_ready, n + 1)
                nc.scalar.activation(std[:, k, :], c.bank[1][:, :], ACT.Sqrt, bias=c.eps[:, 0:1]).then_inc(s.std_ready, 1)

            def copy(n, k, first):
                act.wait_ge(s.turned, n + 1)
                if not first:
                    act.wait_ge(nat_stored[k], 16 * ((n - k) // 2) if isinstance(n, int) else 8 * (n - k))
                nc.scalar.activation(nat[:, k, :], c.bank[2][:, :], ACT.Copy).then_inc(s.nat_copied, 1)

            def key_squares(n, j):
                act.wait_ge(s.keys_ready, 4 * n + j + 1)
                act.wait_ge(s.reduced, 4 * n + j + 1)
                for f in range(2):
                    i = nc.scalar.activation(ksq[:, j % 2, f * T:(f + 1) * T], c.bank[4 + 2 * (j % 2) + f][:, :], ACT.Square)
                i.then_inc(s.keys_squared, 1)

            def step(n, k, latents):
                square(n + 1, 1 - k)
                key_squares(n, 0)
                key_squares(n, 1)
                root(n + 1, 1 - k)
                key_squares(n, 2)
                key_squares(n, 3)
                copy(n + 1, 1 - k, False)

            def tail():
                for j in range(4):
                    key_squares(BLOCKS, j)

            act.sem_inc(s.keys_squared, 2)
            square(0, 0)
            root(0, 0)
            copy(0, 0, True)
            over_blocks(act, step, tail)

        @block.vector
        def _(dve):
            v = nc.vector

            def centre(n, k, latents):
                dve.wait_ge(s.mean_ready, n + 1)
                dve.wait_ge(s.keys_squared, 4 * n - 2 if isinstance(n, int) else 4 * n - 2)
                dve.wait_ge(stored[k], 16 * ((n - k) // 2) if isinstance(n, int) else 8 * (n - k))
                src = z.latents[:, :] if latents else raw[:, k, :]
                v.tensor_tensor(xn[:, k, :], src, c.bank[0][:, :], ALU.subtract).then_inc(s.centred, 1)

            def norm(n, k, latents):
                g = z.gains[:, 2:4] if latents else z.gains[:, 0:2]
                dve.wait_ge(s.std_ready, n + 1)
                v.reciprocal(std[:, k, :], std[:, k, :]).then_inc(s.inverted, 1)
                dve.wait_ge(s.inverted, n + 1)
                dve.wait_ge(s.squared, n + 1)
                v.tensor_tensor(xn[:, k, :], xn[:, k, :], std[:, k, :], ALU.mult).then_inc(s.scaled, 1)
                dve.wait_ge(s.scaled, n + 1)
                v.tensor_scalar(xn[:, k, :], xn[:, k, :], g[:, 0:1], g[:, 1:2], ALU.mult, ALU.add).then_inc(s.normed, 1)

            def reduce(n, j):
                dve.wait_ge(s.keys_squared, 4 * n + j + 3)
                v.tensor_reduce(z.key_norm[:, bass.ds(4 * n + j, 1), :].rearrange("p o h -> p (o h)"),
                                ksq[:, j % 2, :].rearrange("p (h j) -> p h j", h=heads), X, ALU.add).then_inc(s.reduced, 1)

            def step(n, k, latents):
                centre(n + 1, 1 - k, latents)
                reduce(n, 0)
                reduce(n, 1)
                norm(n + 1, 1 - k, latents)
                reduce(n, 2)
                reduce(n, 3)

            def tail():
                for j in range(4):
                    reduce(BLOCKS, j)

            dve.sem_inc(s.reduced, 2)
            dve.wait_ge(s.mean_ready, 1)
            v.tensor_tensor(xn[:, 0, :], raw[:, 0, :], c.bank[0][:, :], ALU.subtract).then_inc(s.centred, 1)
            norm(0, 0, False)
            over_blocks(dve, step, tail)


def l2_xattn(c):
    nc, d = c.nc, c.d
    heads, dq = 16, 64
    with ExitStack() as st:
        z = Queries(scratch(nc, st, "qp6", [P, B, heads, P], F32))
        z.key_norm = scratch(nc, st, "l2x_key_norm", [P, B * CH + B, heads], F32)
        key_add = scratch(nc, st, "l2x_key_add", [P, B * CH + B], F32)
        layernorm(c, "l2x_ln", c.x[:, :], c.xn[:, :])
        with ExitStack() as st2:
            z.latents = c.xn
            z.gains = scratch(nc, st2, "l2x_gains", [P, 4], F32)
            wk = scratch(nc, st2, "l2x_wk", [P, heads * dq], F32)
            load(c, "l2x_load0", [(z.gains[:, :], d.L2_xattn_gains), (wk[:, :], d.L2_xattn_Wk)])
            normalize_context(c, z, wk)
        with ExitStack() as st2:
            wq = scratch(nc, st2, "l2x_wq", [P, heads, dq], F32)
            wk_t = scratch(nc, st2, "l2x_wkt", [dq, heads, P], F32)
            gains = scratch(nc, st2, "l2x_qk_gains", [dq, 3], F32)
            lg = scratch(nc, st2, "l2x_lat_gains", [P, 4], F32)
            mask = scratch(nc, st2, "l2x_mask", [P, B * CH], U8)
            load(c, "l2x_load1", [(wq[:, :, :], d.L2_xattn_Wq), (wk_t[:, :, :], d.L2_xattn_WkT), (gains[:, 0:2], d.L2_xattn_qk_gains),
                                  (mask[:, :], d.key_mask), (lg[:, :], d.L2_xattn_gains)])
            with stage(nc, "l2x_keys", "step rooted gain") as (block, s):
                @block.scalar
                def _(act):
                    nc.scalar.activation(z.key_norm[:, :, :], z.key_norm[:, :, :], ACT.Sqrt, scale=1.0 / dq).then_inc(s.rooted, 1)

                @block.vector
                def _(dve):
                    v = nc.vector
                    v.tensor_tensor(gains[:, 2:3], gains[:, 0:1], gains[:, 1:2], ALU.mult).then_inc(s.gain, 1)
                    dve.wait_ge(s.gain, 1)
                    v.tensor_scalar(gains[:, 2:3], gains[:, 2:3], dq ** -0.5, None, ALU.mult)
                    v.memset(key_add[:, B * CH:], 0.0)
                    v.tensor_scalar(key_add[:, 0:B * CH], mask[:, :], 0.0, MASKED, ALU.is_equal, ALU.mult)
                    dve.wait_ge(s.rooted, 1)
                    step = Steps(dve, s.step)
                    step(v.tensor_scalar(z.key_norm[:, :, :], z.key_norm[:, :, :], 1e-8, None, ALU.max))
                    step(v.reciprocal(z.key_norm[:, :, :], z.key_norm[:, :, :]))
            layernorm(c, "l2x_ln2", c.xn[:, :], c.xn[:, :], lg[:, 2:3], lg[:, 3:4])
            query_side(c, z, "l2x_q", heads, 1.0, dq, wq, wk_t, gains=gains[:, 2:3])

        def ctx_t(b, a, e):
            return d.latT[:, bass.ds(b, 1), :] if a == CH else d.ctxnT[:, bass.ds(b * CH + a, e - a), :]

        def ctx(b, a, e):
            return d.lat[:, bass.ds(b, 1), :] if a == CH else d.ctxn[:, bass.ds(b * CH + a, e - a), :]

        def at(b, ci):
            return B * CH + b if ci == CH else b * CH + ci

        attend_context(c, z, "l2x", heads, ctx_t, ctx, CH + 1, False,
                       key_scale=(lambda b, ci: key_add[:, bass.ds(at(b, ci), 1)],
                                  lambda b, g, ci: z.key_norm[:, bass.ds(at(b, ci), 1), g * HB:(g + 1) * HB].rearrange("p o h -> p (o h)")))
        with ExitStack() as st2:
            wv = scratch(nc, st2, "l2_wv", [P, heads, dq], F32)
            wo = scratch(nc, st2, "l2_wo", [P, heads // 2, P], F32)
            bo = scratch(nc, st2, "l2_bo", [P, 1], F32)
            load(c, "l2x_load2", [(wv[:, :, :], d.L2_xattn_Wv), (wo[:, :, :], d.L2_xattn_Wout), (bo[:, :], d.L2_xattn_bout)])
            output_side(c, z, "l2x_out", heads, dq, wv, wo, bo[:, 0:1])


def l3_attn(c):
    nc, d = c.nc, c.d
    heads, dq, NB = 16, 64, 10
    NEG = -1e9
    layernorm(c, "l3a_ln", c.x[:, :], c.xn[:, :])
    with ExitStack() as st:
        def t(name, shape, dt=F32):
            return scratch(nc, st, f"l3a_{name}", shape, dt)

        o = t("o", [dq, heads, T])
        wp, bp = t("wp", [dq, heads, P]), t("bp", [P, 1])
        with ExitStack() as st2:
            def t2(name, shape, dt=F32):
                return scratch(nc, st2, f"l3a_{name}", shape, dt)

            q, k = t2("q", [dq, heads, T]), t2("k", [dq, heads, T])
            causal = t2("causal", [P, P])
            v = t2("v", [P, B, heads * dq])
            with ExitStack() as st3:
                def t3(name, shape, dt=F32):
                    return scratch(nc, st3, f"l3a_{name}", shape, dt)

                wq, wk, wv = t3("wq", [P, heads, dq]), t3("wk", [P, heads, dq]), t3("wv", [P, heads * dq])
                wr, bq, br = t3("wr", [P, heads, NB]), t3("bq", [dq, heads]), t3("br", [NB, heads])
                bnd, r, far = t3("bnd", [NB, P]), t3("r", [NB, 2, T]), t3("far", [P, 2, B, P])
                load(c, "l3a_load", [(wq[:, :, :], d.L3_attn_Wq), (wk[:, :, :], d.L3_attn_Wk), (wv[:, :], d.L3_attn_Wv), (wr[:, :, :], d.L3_attn_Wr),
                                     (bq[:, :], d.L3_attn_bq), (br[:, :], d.L3_attn_br), (bnd[:, :], d.L3_attn_b_nd_rev), (wp[:, :, :], d.L3_attn_Wproj),
                                     (bp[:, :], d.L3_attn_bproj), (causal[:, :], d.causal)])
                with stage(nc, "l3a_qkv", "q_ready k_ready v_ready q_copied k_copied v_copied r_ready r_copied far_ready far_copied far_stored0 far_stored1 scaled") as (block, s):
                    stored = [s.far_stored0, s.far_stored1]

                    @block.tensor
                    def _(pe):
                        def bias(h):
                            pe.wait_ge(s.r_copied, h + 1)
                            if h >= 1:
                                pe.wait_ge(s.far_copied, h)
                            for b in range(B):
                                mm = nc.tensor.matmul(c.bank[7][:, b * P:(b + 1) * P], r[:, h % 2, b * P:(b + 1) * P], bnd[:, :], start=True, stop=True)
                            mm.then_inc(s.far_ready, 1)

                        for h in range(heads):
                            if h >= 1:
                                pe.wait_ge(s.r_copied, h)
                            nc.tensor.matmul(c.bank[6][0:NB, :], wr[:, h, :], c.xn[:, :], start=True, stop=True).then_inc(s.r_ready, 1)
                            if h >= 2:
                                pe.wait_ge(s.q_copied, h - 1)
                            nc.tensor.matmul(c.bank[h % 2][0:dq, :], wq[:, h, :], c.xn[:, :], start=True, stop=True).then_inc(s.q_ready, 1)
                            if h >= 2:
                                pe.wait_ge(s.k_copied, h - 1)
                            nc.tensor.matmul(c.bank[2 + h % 2][0:dq, :], wk[:, h, :], c.xn[:, :], start=True, stop=True).then_inc(s.k_ready, 1)
                            if h < 2 * B:
                                b, f = divmod(h, 2)
                                if h >= 2:
                                    pe.wait_ge(s.v_copied, h - 1)
                                nc.tensor.matmul(c.bank[4 + h % 2][:, :], c.xn[:, b * P:(b + 1) * P], wv[:, f * T:(f + 1) * T], start=True, stop=True).then_inc(s.v_ready, 1)
                            bias(h)

                    @block.scalar
                    def _(act):
                        for h in range(heads):
                            act.wait_ge(s.r_ready, h + 1)
                            if h >= 2:
                                act.wait_ge(s.far_ready, h - 1)
                            nc.scalar.activation(r[:, h % 2, :], c.bank[6][0:NB, :], ACT.Identity, bias=br[:, h:h + 1]).then_inc(s.r_copied, 1)
                            act.wait_ge(s.q_ready, h + 1)
                            nc.scalar.activation(q[:, h, :], c.bank[h % 2][0:dq, :], ACT.Identity, bias=bq[:, h:h + 1]).then_inc(s.q_copied, 1)
                            act.wait_ge(s.far_ready, h + 1)
                            if h >= 2:
                                act.wait_ge(stored[h % 2], 16 * (h // 2))
                            nc.scalar.activation(far[:, h % 2, :, :], c.bank[7][:, :].rearrange("p (b j) -> p b j", b=B), ACT.Copy).then_inc(s.far_copied, 1)

                    @block.vector
                    def _(dve):
                        for h in range(heads):
                            dve.wait_ge(s.k_ready, h + 1)
                            nc.vector.tensor_scalar(k[:, h, :], c.bank[2 + h % 2][0:dq, :], dq ** -0.5, None, ALU.mult).then_inc(s.k_copied, 1)
                            if h < 2 * B:
                                b, f = divmod(h, 2)
                                dve.wait_ge(s.v_ready, h + 1)
                                nc.vector.tensor_copy(v[:, b, f * T:(f + 1) * T], c.bank[4 + h % 2][:, :]).then_inc(s.v_copied, 1)

                    @block.sync
                    def _(sp):
                        for h in range(heads):
                            sp.wait_ge(s.far_copied, h + 1)
                            sp.dma_start(d.far[:, h, :].rearrange("b (t j) -> t b j", j=P), far[:, h % 2, :, :]).then_inc(stored[h % 2], 16)
                        sp.wait_ge(s.far_stored0, 16 * heads // 2)
                        sp.wait_ge(s.far_stored1, 16 * heads // 2)

            W = heads * P
            logits, bias_t, p_t = t2("logits", [P, W]), t2("bias_t", [P, W]), t2("p_t", [P, W])
            top, total = t2("top", [P, heads]), t2("total", [P, heads])

            def h3(ap):
                return ap.rearrange("p (h j) -> p h j", h=heads)

            with stage(nc, "l3a", "bias_in bias_masked logits_ready added top_ready shifted expd total_ready normed turned turned_copied out_ready out_copied") as (block, s):
                @block.sync
                def _(sp):
                    for b in range(B):
                        if b:
                            sp.wait_ge(s.added, 4 * b)
                        for h0 in range(0, heads, 4):
                            src = d.far[b, h0:h0 + 4, P - 1:P - 1 + (P - 1) * P + 1]
                            src = bass.AP(tensor=src.tensor, offset=src.offset, ap=[[P - 1, P], [P * P, 4], [1, P]])
                            sp.dma_start(h3(bias_t[:, :])[:, h0:h0 + 4, :], src).then_inc(s.bias_in, 16)

                @block.tensor
                def _(pe):
                    for b in range(B):
                        cols = slice(b * P, (b + 1) * P)
                        if b:
                            pe.wait_ge(s.added, 4 * b)
                        for h in range(heads):
                            mm = nc.tensor.matmul(c.bank[h // 4][:, (h % 4) * P:(h % 4 + 1) * P], q[:, h, cols], k[:, h, cols], start=True, stop=True)
                            if h % 4 == 3:
                                mm.then_inc(s.logits_ready, 1)
                        pe.wait_ge(s.normed, b + 1)
                        for g in range(4):
                            pe.wait_ge(s.turned_copied, 4 * b + g) if b or g else None
                            for h in range(4 * g, 4 * g + 4):
                                mm = nc.tensor.transpose(c.bank[4 + g % 2][:, (h % 4) * P:(h % 4 + 1) * P], logits[:, h * P:(h + 1) * P], c.ident[:, :])
                            mm.then_inc(s.turned, 1)
                        for g in range(4):
                            pe.wait_ge(s.turned_copied, 4 * b + g + 1)
                            n = 4 * b + g
                            if n >= 2:
                                pe.wait_ge(s.out_copied, n - 1)
                            for h in range(4 * g, 4 * g + 4):
                                mm = nc.tensor.matmul(c.bank[6 + g % 2][0:dq, (h % 4) * P:(h % 4 + 1) * P], v[:, b, h * dq:(h + 1) * dq],
                                                      p_t[:, h * P:(h + 1) * P], start=True, stop=True)
                            mm.then_inc(s.out_ready, 1)

                @block.scalar
                def _(act):
                    for b in range(B):
                        act.wait_ge(s.shifted, b + 1)
                        nc.scalar.activation(logits[:, :], logits[:, :], ACT.Exp).then_inc(s.expd, 1)
                        for g in range(4):
                            act.wait_ge(s.turned, 4 * b + g + 1)
                            if b:
                                act.wait_ge(s.out_ready, 4 * b)
                            nc.scalar.activation(p_t[:, g * T:(g + 1) * T], c.bank[4 + g % 2][:, :], ACT.Copy).then_inc(s.turned_copied, 1)
                        for g in range(4):
                            act.wait_ge(s.out_ready, 4 * b + g + 1)
                            nc.scalar.activation(o[:, 4 * g:4 * g + 4, b * P:(b + 1) * P], c.bank[6 + g % 2][0:dq, :].rearrange("p (h j) -> p h j", h=4),
                                                 ACT.Copy).then_inc(s.out_copied, 1)

                @block.vector
                def _(dve):
                    vec = nc.vector
                    for b in range(B):
                        dve.wait_ge(s.bias_in, 64 * (b + 1))
                        vec.tensor_tensor(h3(bias_t[:, :]), h3(bias_t[:, :]), causal[:, :].unsqueeze(1).to_broadcast([P, heads, P]), ALU.add).then_inc(s.bias_masked, 1)
                        dve.wait_ge(s.bias_masked, b + 1)
                        if b:
                            dve.wait_ge(s.turned, 4 * b)
                        for g in range(4):
                            dve.wait_ge(s.logits_ready, 4 * b + g + 1)
                            vec.tensor_tensor(logits[:, g * T:(g + 1) * T], c.bank[g][:, :], bias_t[:, g * T:(g + 1) * T], ALU.add).then_inc(s.added, 1)
                        dve.wait_ge(s.added, 4 * b + 4)
                        vec.tensor_reduce(top[:, :], h3(logits[:, :]), X, ALU.max).then_inc(s.top_ready, 1)
                        dve.wait_ge(s.top_ready, b + 1)
                        vec.tensor_tensor(h3(logits[:, :]), h3(logits[:, :]), top[:, :].unsqueeze(2).to_broadcast([P, heads, P]), ALU.subtract).then_inc(s.shifted, 1)
                        dve.wait_ge(s.expd, b + 1)
                        vec.tensor_reduce(total[:, :], h3(logits[:, :]), X, ALU.add).then_inc(s.total_ready, 1)
                        dve.wait_ge(s.total_ready, 2 * b + 1)
                        vec.reciprocal(total[:, :], total[:, :]).then_inc(s.total_ready, 1)
                        dve.wait_ge(s.total_ready, 2 * b + 2)
                        vec.tensor_tensor(h3(logits[:, :]), h3(logits[:, :]), total[:, :].unsqueeze(2).to_broadcast([P, heads, P]), ALU.mult).then_inc(s.normed, 1)
        with stage(nc, "l3a_out", "projected") as (block, s):
            @block.tensor
            def _(pe):
                for h in range(heads):
                    mm = nc.tensor.matmul(c.bank[0][:, :], wp[:, h, :], o[:, h, :], start=(h == 0), stop=(h == heads - 1))
                mm.then_inc(s.projected, 1)

            @block.vector
            def _(dve):
                dve.wait_ge(s.projected, 1)
                nc.vector.scalar_tensor_tensor(out=c.x[:, :], in0=c.bank[0][:, :], scalar=bp[:, 0:1], in1=c.x[:, :], op0=ALU.add, op1=ALU.add)


def butterflies(c, name, m, coef, swap, order, cols):
    nc = c.nc
    INNER = 7
    with nc.sbuf_tensor(f"{name}_own", [P, 2, 4, cols], F32) as own, nc.sbuf_tensor(f"{name}_swapped", [P, 4, cols], F32) as swapped, \
            stage(nc, name, "swapped owned mixed copied") as (block, s):
        n_in = [0]
        main = cols - cols % P

        @block.tensor
        def _(pe):
            done = 0
            for n, stg in enumerate(order):
                if stg >= INNER:
                    continue
                if n:
                    pe.wait_ge(s.mixed, n)
                for b in range(4):
                    mm = nc.tensor.matmul(c.bank[b][:, 0:cols], swap[:, stg, :], m[:, b, :], start=True, stop=True)
                mm.then_inc(s.swapped, 1)

        @block.vector
        def _(dve):
            inner = 0
            for n, stg in enumerate(order):
                if n:
                    dve.wait_ge(s.mixed, n)
                for b in range(4):
                    i = nc.vector.tensor_scalar(own[:, n % 2, b, :], m[:, b, :], coef[:, stg, b, 0:1], None, ALU.mult)
                i.then_inc(s.owned, 1)
                if stg < INNER:
                    inner += 1
                    dve.wait_ge(s.swapped, inner)
                else:
                    nc.vector.tensor_copy(swapped[:, :, :], m[:, :, :]).then_inc(s.copied, 1)
                    dve.wait_ge(s.copied, n + 1 - inner)
                dve.wait_ge(s.owned, n + 1)
                for b in range(4):
                    other = c.bank[b][:, 0:cols] if stg < INNER else swapped[:, b ^ (1 << (stg - INNER)), :]
                    i = nc.vector.scalar_tensor_tensor(out=m[:, b, :], in0=other, scalar=coef[:, stg, b, 1:2], in1=own[:, n % 2, b, :],
                                                       op0=ALU.mult, op1=ALU.add)
                i.then_inc(s.mixed, 1)


def l3_ffn(c):
    nc, d = c.nc, c.d
    STAGES = 9
    layernorm(c, "l3f_ln", c.x[:, :], c.xn[:, :])
    with ExitStack() as st:
        def t(name, shape, dt=F32):
            return scratch(nc, st, f"l3f_{name}", shape, dt)

        up, down = t("up", [P, 4, P + 1]), t("down", [P, 4, P])
        swap, cu, cd = t("swap", [P, 7, P]), t("cu", [P, STAGES, 4, 2]), t("cd", [P, STAGES, 4, 2])
        ub, bc = t("ub", [P, 4]), t("bc", [P, 3])
        load(c, "l3f_load", [(up[:, :, :], d.L3_ffn_up), (down[:, :, :], d.L3_ffn_W_con), (swap[:, :, :], d.swap), (cu[:, :, :, :], d.L3_ffn_up_coef),
                             (cd[:, :, :, :], d.L3_ffn_down_coef), (ub[:, :], d.L3_ffn_up_bias), (bc[:, 0:2], d.L3_ffn_out_bias)])
        butterflies(c, "l3f_up", up, cu, swap, range(STAGES), P + 1)
        butterflies(c, "l3f_down", down, cd, swap, range(STAGES)[::-1], P)
        up_t, hid = t("up_t", [P, 4, P]), t("hid", [P, 4, T])
        with stage(nc, "l3f", "turned turned_copied biased up_ready waved down_ready") as (block, s):
            @block.tensor
            def _(pe):
                for j in range(4):
                    mm = nc.tensor.transpose(c.bank[0][:, j * P:(j + 1) * P], up[:, j, 0:P], c.ident[:, :])
                mm.then_inc(s.turned, 1)
                pe.wait_ge(s.turned_copied, 1)
                for j in range(4):
                    nc.tensor.matmul(c.bank[1 + j][:, :], up_t[:, j, :], c.xn[:, :], start=True, stop=True).then_inc(s.up_ready, 1)
                for j in range(4):
                    pe.wait_ge(s.waved, j + 1)
                    mm = nc.tensor.matmul(c.bank[5][:, :], down[:, j, :], hid[:, j, :], start=(j == 0), stop=(j == 3))
                mm.then_inc(s.down_ready, 1)

            @block.scalar
            def _(act):
                act.wait_ge(s.turned, 1)
                nc.scalar.activation(up_t[:, :, :], c.bank[0][:, :].rearrange("p (j i) -> p j i", j=4), ACT.Copy).then_inc(s.turned_copied, 1)
                act.wait_ge(s.biased, 1)
                for j in range(4):
                    act.wait_ge(s.up_ready, j + 1)
                    nc.scalar.activation(hid[:, j, :], c.bank[1 + j][:, :], ACT.Gelu, bias=ub[:, j:j + 1]).then_inc(s.waved, 1)

            @block.vector
            def _(dve):
                nc.vector.tensor_tensor(ub[:, :], ub[:, :], up[:, :, P], ALU.add).then_inc(s.biased, 1)
                nc.vector.tensor_tensor(bc[:, 2:3], bc[:, 0:1], bc[:, 1:2], ALU.add).then_inc(s.biased, 1)
                dve.wait_ge(s.biased, 2)
                dve.wait_ge(s.down_ready, 1)
                nc.vector.scalar_tensor_tensor(out=c.x[:, :], in0=c.bank[5][:, :], scalar=bc[:, 2:3], in1=c.x[:, :], op0=ALU.add, op1=ALU.add)


BUILDERS = {6: l2_xattn, 10: l3_attn, 11: l3_ffn, 1: l0_attn, 4: l1_attn, 7: l2_attn, 0: l0_xattn, 2: l0_ffn, 3: l1_xattn, 5: l1_ffn, 8: l2_ffn, 9: l3_xattn}


def program(nc, d):
    c = Chip(nc, d)
    setup(c)
    for k in SUBLAYERS:
        BUILDERS[k](c)
    store(c)



def layout(i):
    a = {k: np.asarray(v) for k, v in i.items()}

    def col(v):
        return v.reshape(-1, P).T

    r = {}
    r["xT"] = a["x"].reshape(T, P).T
    r["ctxT"] = a["ctx_1024"].reshape(B * CH, P, P).transpose(2, 0, 1)
    r["ctx"] = a["ctx_1024"].reshape(B * CH, P, P).transpose(1, 0, 2)
    r["key_pos"] = a["itok_BxS2_1_8191"].reshape(P, B * CH)
    r["mask_t"] = a["mask_BxSxS2_if1"].reshape(B, P, CH, P).transpose(3, 0, 2, 1).reshape(P, B * CH, P)
    r["query_mask"] = a["mask_BxS_ik0"]
    r["L0_xattn_W_qT"] = a["L0_xattn_W_q"].T
    r["L0_xattn_W_k"] = a["L0_xattn_W_k"]
    blocks = np.zeros((P, 16, P), a["L0_xattn_W_v"].dtype)
    for h in range(16):
        blocks[:, h, 8 * h:8 * h + 8] = a["L0_xattn_W_v"].T[:, 8 * h:8 * h + 8]
    r["L0_xattn_W_v_blocks"] = blocks
    r["L0_xattn_W_oT"] = a["L0_xattn_W_o"].T
    wkv = a["L1_xattn_Wkv"]
    r["L1_xattn_Wq"] = a["L1_xattn_Wq"].reshape(P, 16, 64)
    r["L1_xattn_WkT"] = wkv[:, :1024].reshape(P, 16, 64).transpose(2, 1, 0)
    r["L1_xattn_Wv"] = wkv[:, 1024:].reshape(P, 16, 64)
    r["L1_xattn_Wout"] = a["L1_xattn_Wout"].reshape(8, P, P).transpose(1, 0, 2)
    r["L1_xattn_bout"] = col(a["L1_xattn_bout"])
    r["L3_xattn_Wq"] = a["L3_xattn_Wq"].reshape(P, 8, 64)
    r["L3_xattn_WkT"] = a["L3_xattn_Wk"].reshape(P, 8, 64).transpose(2, 1, 0)
    r["L3_xattn_Wv"] = a["L3_xattn_Wv"].reshape(P, 8, 64)
    r["L3_xattn_Wo"] = a["L3_xattn_Wo"].reshape(4, P, P).transpose(1, 0, 2)
    r["L3_xattn_bo"] = col(a["L3_xattn_bo"])
    r["L0_ffn_Wg"] = a["L0_ffn_Wg"]
    r["L0_ffn_bg"] = a["L0_ffn_bg"][None]
    r["L0_ffn_W1"] = a["L0_ffn_W1"].transpose(1, 0, 2)
    r["L0_ffn_b1"] = a["L0_ffn_b1"].reshape(E * 4, P).T
    r["L0_ffn_W2"] = a["L0_ffn_W2"].reshape(E, 4, P, P).transpose(2, 0, 1, 3)
    r["L0_ffn_b2"] = a["L0_ffn_b2"]
    r["L1_ffn_w_gate"] = a["L1_ffn_w_gate"]
    r["L1_ffn_w_g"] = a["L1_ffn_w_g"].transpose(1, 0, 2)
    r["L1_ffn_w_u"] = a["L1_ffn_w_u"].transpose(1, 0, 2)
    r["L1_ffn_w_d"] = a["L1_ffn_w_d"].reshape(E, 2, 88, P).transpose(2, 0, 1, 3)
    r["L2_ffn_gate_w"] = a["L2_ffn_gate_w"].T
    r["L2_ffn_wi_gate"] = a["L2_ffn_wi_gate"].transpose(2, 0, 1)
    r["L2_ffn_wi_up"] = a["L2_ffn_wi_up"].transpose(2, 0, 1)
    r["L2_ffn_wo"] = a["L2_ffn_wo"].transpose(2, 0, 1).reshape(4, P, E, P).transpose(1, 2, 0, 3)
    n = "L0_attn_"
    r["L0_attn_w4"] = np.stack([a[n + w] for w in ("wq", "wk", "wv", "wo")], 1)
    r["L0_attn_bias"] = np.stack([a[n + w] for w in ("bq", "bk", "bo", "ln1_g", "ln1_b", "ln2_g", "ln2_b", "b2")]
                                 + list(a[n + "b1"].reshape(4, P)) + [a[n + "bv"]], 1)
    r["L0_attn_bv"] = a[n + "bv"][None]
    proj = np.zeros((P, 16, P), a[n + "proj_mat"].dtype)
    for h in range(16):
        proj[8 * h:8 * h + 8, h, :] = a[n + "proj_mat"]
    r["L0_attn_proj"] = proj
    r["L0_attn_w1"] = a[n + "w1"]
    r["L0_attn_w2"] = a[n + "w2"].reshape(4, P, P).transpose(1, 0, 2)
    n = "L1_attn_"
    r["L1_attn_ln"] = np.stack([a[n + "ln_g"], a[n + "ln_b"]], 1)
    r["L1_attn_W_in"] = a[n + "W_in"].reshape(P, 4, P)
    r["L1_attn_conv_w"] = a[n + "conv_w"].reshape(2, P, 4).transpose(1, 0, 2)
    r["L1_attn_W_x"] = a[n + "W_x"].reshape(2, P, 40).transpose(1, 0, 2)
    r["L1_attn_W_dt"] = a[n + "W_dt"].reshape(8, 2, P)
    r["L1_attn_cols"] = np.stack([a[n + w].reshape(2, P) for w in ("conv_b", "b_dt", "Dskip")], 2).transpose(1, 0, 2)
    r["L1_attn_A_log"] = a[n + "A_log"].reshape(2, P, 16).transpose(1, 0, 2)
    r["L1_attn_W_out"] = a[n + "W_out"].reshape(2, P, P).transpose(1, 0, 2)
    n = "L2_attn_"
    r["L2_attn_w_qkv"] = a[n + "w_qkv"]
    r["L2_attn_w_out"] = a[n + "w_out"]
    r["L2_attn_cols"] = np.stack([a[n + w] for w in ("gamma", "beta", "b_out")], 2)
    n = "L2_xattn_"
    wkv = a[n + "Wkv"]
    r["L2_xattn_gains"] = np.stack([a[n + w] for w in ("ln_x_g", "ln_x_b", "ln_l_g", "ln_l_b")], 1)
    r["L2_xattn_qk_gains"] = np.stack([a[n + "qn_g"], a[n + "kn_g"]], 1)
    r["L2_xattn_Wk"] = wkv[:, :1024]
    r["L2_xattn_Wq"] = a[n + "Wq"].reshape(P, 16, 64)
    r["L2_xattn_WkT"] = wkv[:, :1024].reshape(P, 16, 64).transpose(2, 1, 0)
    r["L2_xattn_Wv"] = wkv[:, 1024:].reshape(P, 16, 64)
    r["L2_xattn_Wout"] = a[n + "Wout"].reshape(8, P, P).transpose(1, 0, 2)
    r["L2_xattn_bout"] = col(a[n + "bout"])
    r["key_mask"] = a["mask_BxS2_bf1"].view(np.uint8).reshape(B * CH, P).T
    n = "L3_attn_"
    r["L3_attn_Wq"] = a[n + "Wq"].reshape(P, 16, 64)
    r["L3_attn_Wk"] = a[n + "Wk"].reshape(P, 16, 64)
    r["L3_attn_Wv"] = a[n + "Wv"]
    r["L3_attn_Wr"] = a[n + "Wr"].reshape(P, 16, 10)
    r["L3_attn_bq"] = a[n + "bq"].reshape(16, 64).T
    r["L3_attn_br"] = a[n + "br"].reshape(16, 10).T
    r["L3_attn_b_nd_rev"] = a[n + "b_nd"][:, ::-1]
    r["L3_attn_Wproj"] = a[n + "Wproj"].reshape(16, 64, P).transpose(1, 0, 2)
    r["L3_attn_bproj"] = col(a[n + "bproj"])
    n = "L3_ffn_"
    r["L3_ffn_up"] = np.concatenate([a[n + "W_exp"].T, a[n + "b_exp"][:, None]], 1).reshape(4, P, P + 1).transpose(1, 0, 2)
    r["L3_ffn_W_con"] = a[n + "W_con"].reshape(4, P, P).transpose(1, 0, 2)
    hidden = np.arange(512)
    for name, transposed in (("up", False), ("down", True)):
        w = a[n + name + "_weights"]
        coef = np.empty((9, 512, 2), w.dtype)
        for stg in range(9):
            half = 1 << stg
            pair, side = hidden // (2 * half) * half + hidden % half, hidden // half % 2
            coef[stg, :, 0] = w[stg, pair, side, side]
            coef[stg, :, 1] = w[stg, pair, 1 - side, side] if transposed else w[stg, pair, side, 1 - side]
        r[f"L3_ffn_{name}_coef"] = coef.reshape(9, 4, P, 2).transpose(2, 0, 1, 3)
    r["L3_ffn_up_bias"] = a[n + "up_bias"].reshape(4, P).T
    r["L3_ffn_out_bias"] = np.stack([a[n + "b_con"], a[n + "down_bias"]], 1)
    r["causal"] = np.where(np.arange(P)[None, :] <= np.arange(P)[:, None], 0, -1e9).astype(np.float32)
    swap = np.zeros((P, 7, P), np.float32)
    for stg in range(7):
        swap[np.arange(P), stg, np.arange(P) ^ (1 << stg)] = 1
    r["swap"] = swap
    bf = np.dtype("bfloat16")
    sel = np.zeros((16, 16, P), np.float32)
    for e in range(16):
        sel[e, e, :] = 1
    r["select"] = sel
    r["rank"] = np.broadcast_to(np.arange(E, 0, -1, dtype=np.float32), (P, B, E))
    hm = np.zeros((P, 16), np.float32)
    for h in range(16):
        hm[8 * h:8 * h + 8, h] = 1
    r["headmask"] = hm
    ratio = 2.0 ** (-8.0 / 16)
    slope = np.array([ratio ** k for k in range(1, 17)], np.float32)
    parts, left = [], slope
    for _ in range(3):
        parts.append(left.astype(bf))
        left = left - parts[-1].astype(np.float32)
    r["slope_rows"] = np.ascontiguousarray(np.broadcast_to(np.stack(parts * 3)[:, :, None], (9, 16, P)))
    r["ones_rows"] = np.ones((3, CH, P), bf)
    return {k: np.ascontiguousarray(v) for k, v in r.items()}


SCRATCH = {"ctxnT": ([P, B * CH, P], F32), "ctxn": ([P, B * CH, P], F32), "latT": ([P, B, P], F32), "lat": ([P, B, P], F32),
           "far": ([B, 16, P * P], F32),
           "pos_parts": ([3, P, B * CH], BF16), "pos_rows": ([9, B, CH, P], BF16), "mask_parts": ([3, B, P], BF16)}


def kernel(**inputs):
    import concourse.bacc as bacc
    from concourse.bass_utils import run_bass_kernel_spmd

    nc = bacc.Bacc("TRN2", target_bir_lowering=False, num_devices=1)
    arrays = layout(inputs)
    dram = {k: nc.dram_tensor(f"in_{k}", v.shape, mybir.dt.from_np(v.dtype), kind="ExternalInput").ap()
            for k, v in arrays.items()}
    for k, (shape, dt) in SCRATCH.items():
        dram[k] = nc.dram_tensor(f"tmp_{k}", shape, dt, kind="Internal").ap()
    dram["outT"] = nc.dram_tensor("outT", (P, T), F32, kind="ExternalOutput").ap()
    program(nc, namedtuple("Dram", dram)(*dram.values()))
    r = run_bass_kernel_spmd(nc, [{f"in_{k}": v for k, v in arrays.items()}], core_ids=[0])
    return np.ascontiguousarray(r.results[0]["outT"].T).reshape(B, P, P)
```

```python
from collections import namedtuple
from contextlib import ExitStack, contextmanager

import numpy as np

import concourse.bass as bass
from concourse import mybir

SUBLAYERS = range(12)

ALU = mybir.AluOpType
ACT = mybir.ActivationFunctionType
F32 = mybir.dt.float32
BF16 = mybir.dt.bfloat16
I32 = mybir.dt.int32
U8 = mybir.dt.uint8
X = mybir.AxisListType.X

P = 128
B = 4
T = B * P
KEYS = 2048
CH = KEYS // P
HB = 4
E = 8
LN_EPS = 1e-5
MASKED = -1e30


@contextmanager
def stage(nc, prefix, names):
    fields, sems, every = [], [], []
    for entry in names.split():
        field, _, count = entry.partition("*")
        mine = [nc.alloc_semaphore(f"{prefix}_{field}{i}" if count else f"{prefix}_{field}") for i in range(int(count or 1))]
        fields.append(field)
        sems.append(mine if count else mine[0])
        every += mine
    with nc.Block() as block:
        yield block, namedtuple("Semaphores", fields)(*sems)
    for s in every:
        nc.gpsimd.sem_clear(s)
    for s in every:
        nc.release_semaphore(s)


class Chip:

    def __init__(self, nc, d):
        self.nc, self.d = nc, d
        self.x = nc.alloc_sbuf_tensor("x", [P, T], F32)
        self.xn = nc.alloc_sbuf_tensor("xn", [P, T], F32)
        self.ident = nc.alloc_sbuf_tensor("ident", [P, P], F32)
        self.ident_bf = nc.alloc_sbuf_tensor("ident_bf", [P, P], BF16)
        self.ones = nc.alloc_sbuf_tensor("ones", [P, P], F32)
        self.ones_bf = nc.alloc_sbuf_tensor("ones_bf", [P, P], BF16)
        self.mean = nc.alloc_sbuf_tensor("mean", [P, P], F32)
        self.eps = nc.alloc_sbuf_tensor("eps", [P, 1], F32)
        self.half_pi = nc.alloc_sbuf_tensor("half_pi", [P, 1], F32)
        self.select = nc.alloc_sbuf_tensor("select", [16, 16, P], F32)
        self.rank = nc.alloc_sbuf_tensor("rank", [P, B, E], F32)
        self.bank = [nc.alloc_psum_tensor(f"bank{i}", [P, T], F32) for i in range(8)]


class Queries:

    def __init__(self, qp):
        self.qp, self.latents, self.gains, self.key_norm = qp, None, None, None


def scratch(nc, frees, name, shape, dt):
    return frees.enter_context(nc.sbuf_tensor(name, shape, dt))


def setup(c):
    nc = c.nc
    with stage(nc, "setup", "loaded zeroed made") as (block, s):
        @block.sync
        def _(sp):
            sp.dma_start(c.x[:, :], c.d.xT).then_inc(s.loaded, 16)
            sp.dma_start(c.select[:, :, :], c.d.select).then_inc(s.loaded, 16)
            sp.dma_start(c.rank[:, :, :], c.d.rank).then_inc(s.loaded, 16)
            sp.wait_ge(s.loaded, 48)

        @block.gpsimd
        def _(pool):
            nc.gpsimd.memset(c.ident[:, :], 0.0).then_inc(s.zeroed, 1)
            nc.gpsimd.memset(c.ones[:, :], 1.0)
            nc.gpsimd.memset(c.ones_bf[:, :], 1.0)
            nc.gpsimd.memset(c.mean[:, :], 1.0 / P)
            nc.gpsimd.memset(c.eps[:, :], LN_EPS)
            nc.gpsimd.memset(c.half_pi[:, :], float(np.float32(np.pi / 2)))
            pool.wait_ge(s.zeroed, 1)
            nc.gpsimd.affine_select(out=c.ident[:, :], in_=c.ident[:, :], compare_op=ALU.not_equal, fill=1.0,
                                    base=0, pattern=[[-1, P]], channel_multiplier=1).then_inc(s.made, 1)
            pool.wait_ge(s.made, 1)
            nc.gpsimd.tensor_copy(c.ident_bf[:, :], c.ident[:, :])


def store(c):
    nc = c.nc
    with stage(nc, "store", "stored") as (block, s):
        @block.sync
        def _(sp):
            sp.dma_start(c.d.outT, c.x[:, :]).then_inc(s.stored, 16)
            sp.wait_ge(s.stored, 16)


def layernorm(c, name, src, out, gain=None, shift=None, also=None):
    nc = c.nc
    n = src.shape[-1]
    with nc.sbuf_tensor(f"{name}_xc", [P, n], F32) as xc, nc.sbuf_tensor(f"{name}_sq", [P, n], F32) as sq, \
            nc.sbuf_tensor(f"{name}_std", [P, n], F32) as std, \
            stage(nc, name, "mean_done centred squared var_done std_done inverted normed") as (block, s):
        mean_ps, var_ps = c.bank[0][:, 0:n], c.bank[1][:, 0:n]

        @block.tensor
        def _(pe):
            nc.tensor.matmul(mean_ps, c.mean[:, :], src, start=True, stop=True).then_inc(s.mean_done, 1)
            pe.wait_ge(s.squared, 1)
            nc.tensor.matmul(var_ps, c.mean[:, :], sq[:, :], start=True, stop=True).then_inc(s.var_done, 1)

        @block.scalar
        def _(act):
            act.wait_ge(s.centred, 1)
            nc.scalar.activation(sq[:, :], xc[:, :], ACT.Square).then_inc(s.squared, 1)
            act.wait_ge(s.var_done, 1)
            nc.scalar.activation(std[:, :], var_ps, ACT.Sqrt, bias=c.eps[:, 0:1]).then_inc(s.std_done, 1)

        @block.vector
        def _(dve):
            dve.wait_ge(s.mean_done, 1)
            nc.vector.tensor_tensor(xc[:, :], src, mean_ps, ALU.subtract).then_inc(s.centred, 1)
            dve.wait_ge(s.std_done, 1)
            nc.vector.reciprocal(std[:, :], std[:, :]).then_inc(s.inverted, 1)
            dve.wait_ge(s.inverted, 1)
            nc.vector.tensor_tensor(out, xc[:, :], std[:, :], ALU.mult).then_inc(s.normed, 1)
            if gain is not None:
                dve.wait_ge(s.normed, 1)
                nc.vector.tensor_scalar(out, out, gain, shift, ALU.mult, ALU.add)



def query_side(c, z, name, heads, scale, dq, wq, wk_t, gains=None):
    nc = c.nc
    pairs = heads // 2
    W = 2 * dq
    with nc.sbuf_tensor(f"{name}_q", [W, 2, T], F32) as q, nc.sbuf_tensor(f"{name}_sq", [W, 2, T], F32) as sq, \
            nc.sbuf_tensor(f"{name}_rms", [W, 2, T], F32) as rms, nc.sbuf_tensor(f"{name}_both", [W, 2, dq], F32) as own_ones, \
            stage(nc, name, "q_ready q_copied carried carried_copied squared sum_ready rms_ready rms_kept inverted scaled zeroed ones_ready") as (block, s):
        q_ps, carried_ps, sum_ps = c.bank[0:2], c.bank[2:6], c.bank[6:8]

        @block.tensor
        def _(pe):
            def project(j):
                if j >= 2:
                    pe.wait_ge(s.q_copied, j - 1)
                nc.tensor.matmul(q_ps[j % 2][0:W, :], wq[:, j, :], c.xn[:, :], start=True, stop=True).then_inc(s.q_ready, 1)

            def norm(j):
                pe.wait_ge(s.squared, j + 1)
                if j == 0:
                    pe.wait_ge(s.ones_ready, 2)
                if j >= 2:
                    pe.wait_ge(s.rms_ready, j - 1)
                nc.tensor.matmul(sum_ps[j % 2][0:W, :], own_ones[:, :, :].rearrange("p h k -> p (h k)"), sq[:, j % 2, :],
                                 start=True, stop=True).then_inc(s.sum_ready, 1)

            def carry(j):
                pe.wait_ge(s.scaled if gains is not None else s.q_copied, j + 1)
                for k in range(2):
                    if j >= 2:
                        pe.wait_ge(s.carried_copied, 2 * j + k - 3)
                    rows = slice(k * dq, (k + 1) * dq)
                    nc.tensor.matmul(carried_ps[(2 * j + k) % 4][:, :], wk_t[rows, j, :], q[rows, j % 2, :], start=True, stop=True).then_inc(s.carried, 1)

            project(0)
            for j in range(pairs):
                if gains is not None:
                    norm(j)
                if j + 1 < pairs:
                    project(j + 1)
                carry(j)

        @block.scalar
        def _(act):
            for j in range(pairs):
                act.wait_ge(s.q_ready, j + 1)
                if j >= 2:
                    act.wait_ge(s.carried, 2 * j - 2)
                nc.scalar.activation(q[:, j % 2, :], q_ps[j % 2][0:W, :], ACT.Copy, scale=scale).then_inc(s.q_copied, 1)
                if gains is not None:
                    act.wait_ge(s.q_copied, j + 1)
                    nc.scalar.activation(sq[:, j % 2, :], q[:, j % 2, :], ACT.Square).then_inc(s.squared, 1)
                    act.wait_ge(s.sum_ready, j + 1)
                    if j >= 2:
                        act.wait_ge(s.scaled, j - 1)
                    nc.scalar.activation(rms[:, j % 2, :], sum_ps[j % 2][0:W, :], ACT.Sqrt, scale=1.0 / dq).then_inc(s.rms_ready, 1)

        @block.vector
        def _(dve):
            if gains is not None:
                nc.vector.memset(own_ones[:, :, :], 0.0).then_inc(s.zeroed, 1)
                dve.wait_ge(s.zeroed, 1)
                for k in range(2):
                    nc.vector.memset(own_ones[k * dq:(k + 1) * dq, k, :], 1.0).then_inc(s.ones_ready, 1)
            for j in range(pairs):
                if gains is not None:
                    dve.wait_ge(s.rms_ready, j + 1)
                    nc.vector.tensor_scalar(rms[:, j % 2, :], rms[:, j % 2, :], 1e-8, None, ALU.max).then_inc(s.rms_kept, 1)
                    dve.wait_ge(s.rms_kept, j + 1)
                    nc.vector.reciprocal(rms[:, j % 2, :], rms[:, j % 2, :]).then_inc(s.inverted, 1)
                    dve.wait_ge(s.inverted, j + 1)
                    nc.vector.scalar_tensor_tensor(out=q[:, j % 2, :], in0=q[:, j % 2, :], scalar=gains, in1=rms[:, j % 2, :],
                                                   op0=ALU.mult, op1=ALU.mult).then_inc(s.scaled, 1)
                for h in range(2 * j, 2 * j + 2):
                    dve.wait_ge(s.carried, h + 1)
                    nc.vector.tensor_copy(z.qp[:, :, h, :], carried_ps[h % 4][:, :].rearrange("p (b q) -> p b q", b=B)).then_inc(s.carried_copied, 1)


def attend_context(c, z, name, heads, ctx_t, ctx, chunks, one_more, rows=None, row_bias=None, mask=None, key_scale=None):
    nc = c.nc
    groups = heads // HB
    steps = B * groups
    PIECE = 4
    pieces = [(a, min(a + PIECE, chunks)) for a in range(0, chunks, PIECE)]
    NP = len(pieces)
    R = rows[1] if rows is not None else 0
    with ExitStack() as st:
        kt = scratch(nc, st, f"{name}_kt", [P, chunks, P], F32)
        kn = scratch(nc, st, f"{name}_kn", [P, chunks, P], F32)
        sc = scratch(nc, st, f"{name}_scores", [P, 2, chunks, HB * P], F32)
        part = scratch(nc, st, f"{name}_part", [P, NP, HB * P], F32)
        cmax = scratch(nc, st, f"{name}_cmax", [P, HB * P], F32)
        m = scratch(nc, st, f"{name}_m", [P, HB], F32)
        diag = scratch(nc, st, f"{name}_diag", [P, HB, P], F32)
        psum_rows = scratch(nc, st, f"{name}_rowsum", [P, HB * P], F32)
        den = scratch(nc, st, f"{name}_den", [P, HB], F32)
        rec = scratch(nc, st, f"{name}_rec", [P, HB], F32)
        rdiag = scratch(nc, st, f"{name}_rdiag", [P, HB, P], F32)
        spread = scratch(nc, st, f"{name}_spread", [P, HB * P], F32)
        if rows is not None:
            rt = scratch(nc, st, f"{name}_rows", [R, chunks, P], BF16)
        if mask is not None:
            mi = scratch(nc, st, f"{name}_mask", [P, chunks, P], I32)
            mb = scratch(nc, st, f"{name}_maskbias", [P, chunks, P], BF16)
        names = "scores_ready act_copied dve_copied part_max col_max turned row_max diag_ready max_ready " \
                "shifted exps sum_step den_ready den_copied inverted rdiag_ready spread_ready spread_copied mean_ready stored mask_in mask_ready " 
        names += f" kt_in*{NP} kn_in*{NP} rows_in*{NP}"
        block, s = st.enter_context(stage(nc, name, names))
        score_ps, turn_ps, max_ps, out_ps, den_ps = c.bank[0:4], c.bank[4], c.bank[5], c.bank[6], c.bank[7]
        order = [(ci, pi) for pi, (a, b_) in enumerate(pieces) for ci in range(a, b_)]

        def over_batches(eng, body):
            with eng.Fori(0, B - 1) as b:
                body(b, False)
            body(B - 1, True)

        def first(n):
            return isinstance(n, int) and n == 0

        def more(last, g):
            return not last or g + 1 < groups, not last or g + 2 < groups

        by_act = [ci for ci in range(chunks) if key_scale is None or ci % 2]
        by_dve = [ci for ci in range(chunks) if ci not in by_act]

        def wait_copied(eng, n, ci):
            if ci in by_act:
                eng.wait_ge(s.act_copied, n * len(by_act) + by_act.index(ci) + 1)
            else:
                eng.wait_ge(s.dve_copied, n * len(by_dve) + by_dve.index(ci) + 1)

        def successor(b, g):
            return (b, g + 1) if g + 1 < groups else (b + 1, 0)

        @block.sync
        def _(sp):
            def load(b, first):
                for p, (a, e) in enumerate(pieces):
                    if not first:
                        sp.wait_ge(s.scores_ready, (b * groups - 1) * chunks + e)
                    sp.dma_start(kt[:, a:e, :], ctx_t(b, a, e)).then_inc(s.kt_in[p], 16)
                    if rows is not None:
                        sp.dma_start(rt[:, a:e, :], rows[0](b, a, e)).then_inc(s.rows_in[p], 16)
                    if mask is not None and p == 0:
                        if not first:
                            sp.wait_ge(s.mask_ready, NP * b)
                        sp.dma_start(mi[:, :, :], mask(b)).then_inc(s.mask_in, 16)
                if not first:
                    sp.wait_ge(s.mean_ready, b * groups + 1)
                for p, (a, e) in enumerate(pieces):
                    sp.dma_start(kn[:, a:e, :], ctx(b, a, e)).then_inc(s.kn_in[p], 16)

            load(0, True)
            with sp.Fori(1, B) as b:
                load(b, False)

        @block.tensor
        def _(pe):
            def scores(b, g, p):
                for ci in range(*pieces[p]):
                    n = b * groups + g
                    if g == 0 and ci == pieces[p][0]:
                        pe.wait_ge(s.kt_in[p], 16 * b + 16)
                        if rows is not None:
                            pe.wait_ge(s.rows_in[p], 16 * b + 16)
                        if mask is not None:
                            pe.wait_ge(s.mask_ready, NP * b + p + 1)
                    if ci >= 4:
                        wait_copied(pe, n, ci - 4)
                    elif not first(n):
                        wait_copied(pe, n - 1, chunks + ci - 4)
                    ps = score_ps[(g * chunks + ci) % 4]
                    more = (rows is not None) + (mask is not None)
                    mm = nc.tensor.matmul(ps[:, :].rearrange("p (h q) -> p h q", h=HB), kt[:, ci, :], z.qp[:, b, g * HB:(g + 1) * HB, :],
                                          start=True, stop=not more)
                    if mask is not None:
                        more -= 1
                        mm = nc.tensor.matmul(ps[:, :].rearrange("p (h q) -> p h q", h=HB), c.ident_bf[:, :],
                                              mb[:, ci, :].unsqueeze(1).to_broadcast([P, HB, P]), start=False, stop=not more)
                    if rows is not None:
                        mm = nc.tensor.matmul(ps[:, :].rearrange("p (h q) -> p h q", h=HB), rt[:, ci, :], row_bias(b, g), start=False, stop=True)
                    mm.then_inc(s.scores_ready, 1)

            def weighted_sum(b, g, p):
                n = b * groups + g
                if p == 0:
                    pe.wait_ge(s.stored, n + 2)
                pe.wait_ge(s.exps, n * NP + p + 1)
                if g == 0:
                    pe.wait_ge(s.kn_in[p], 16 * b + 16)
                for ci in range(*pieces[p]):
                    mm = nc.tensor.matmul(out_ps[:, :], kn[:, ci, :], sc[:, g % 2, ci, :], start=(ci == 0), stop=(ci == chunks - 1))
                if p == NP - 1:
                    mm.then_inc(s.mean_ready, 1)

            def turn(b, g):
                n = b * groups + g
                pe.wait_ge(s.col_max, n + 1)
                pe.wait_ge(s.row_max, n + 1)
                for h in range(HB):
                    mm = nc.tensor.transpose(turn_ps[:, h * P:(h + 1) * P], cmax[:, h * P:(h + 1) * P], c.ident[:, :])
                mm.then_inc(s.turned, 1)

            def denominators(b, g):
                n = b * groups + g
                pe.wait_ge(s.sum_step, (n + 2) * (chunks - 1))
                pe.wait_ge(s.spread_copied, n + 1)
                for h in range(HB):
                    mm = nc.tensor.matmul(den_ps[:, h:h + 1], psum_rows[:, h * P:(h + 1) * P], c.ones[:, 0:1], start=True, stop=True)
                mm.then_inc(s.den_ready, 1)

            def spread_inverses(b, g):
                n = b * groups + g
                pe.wait_ge(s.rdiag_ready, n + 1)
                nc.tensor.matmul(den_ps[:, :].rearrange("p (h q) -> p h q", h=HB), c.ones[:, :], rdiag[:, :, :],
                                 start=True, stop=True).then_inc(s.spread_ready, 1)

            def spread_max(b, g):
                n = b * groups + g
                pe.wait_ge(s.diag_ready, n + 1)
                pe.wait_ge(s.shifted, n * NP + 1)
                nc.tensor.matmul(max_ps[:, :].rearrange("p (h q) -> p h q", h=HB), c.ones[:, :], diag[:, :, :],
                                 start=True, stop=True).then_inc(s.max_ready, 1)

            for p in range(NP):
                scores(0, 0, p)
            turn(0, 0)
            scores(0, 1, 0)
            spread_max(0, 0)

            def body(b, last):
                for g in range(groups):
                    one, two = more(last, g)
                    for p in range(NP):
                        if one and p + 1 < NP:
                            scores(*successor(b, g), p + 1)
                        if key_scale is not None:
                            weighted_sum(b, g, p)
                    if key_scale is None:
                        for p in range(NP):
                            weighted_sum(b, g, p)
                    if one:
                        turn(*successor(b, g))
                    if two:
                        scores(*successor(*successor(b, g)), 0)
                    denominators(b, g)
                    if one:
                        spread_max(*successor(b, g))
                    spread_inverses(b, g)

            over_batches(pe, body)

        @block.scalar
        def _(act):
            def copy(b, g, ci):
                n = (b * groups + g) * chunks + ci
                act.wait_ge(s.scores_ready, n + 1)
                ps = score_ps[(g * chunks + ci) % 4]
                if key_scale is None:
                    nc.scalar.activation(sc[:, g % 2, ci, :], ps[:, :], ACT.Copy).then_inc(s.act_copied, 1)
                    return
                for h in range(HB):
                    of_head = slice(h * P, (h + 1) * P)
                    i = nc.scalar.activation(sc[:, g % 2, ci, of_head], ps[:, of_head], ACT.Identity,
                                             scale=key_scale[1](b, g, ci)[:, h:h + 1], bias=key_scale[2](b, g, ci)[:, h:h + 1])
                i.then_inc(s.act_copied, 1)

            def exps(b, g, p):
                n = b * groups + g
                a, e = pieces[p]
                act.wait_ge(s.shifted, n * NP + p + 2)
                nc.scalar.activation(sc[:, g % 2, a:e, :], sc[:, g % 2, a:e, :], ACT.Exp).then_inc(s.exps, 1)

            def copies(b, g, p, at_first=False, halves=(0, 1)):
                n = b * groups + g
                mine = [ci for ci in range(*pieces[p]) if ci in by_act]
                for half in halves:
                    if half == 0 and mine and not at_first:
                        act.wait_ge(s.mean_ready, n)
                        act.wait_ge(s.sum_step, (n - 1) * (chunks - 1) + pieces[p][1] - 1)
                    for ci in (mine[:len(mine) // 2], mine[len(mine) // 2:])[half]:
                        copy(b, g, ci)

            for p in range(NP):
                copies(0, 0, p, True)
            copies(0, 1, 0, True)

            def body(b, last):
                for g in range(groups):
                    one, two = more(last, g)
                    for p in range(NP):
                        if one and p + 1 < NP:
                            copies(*successor(b, g), p + 1, False, [0])
                        exps(b, g, p)
                        if one and p + 1 < NP:
                            copies(*successor(b, g), p + 1, True, [1])
                    if two:
                        copies(*successor(*successor(b, g)), 0)

            over_batches(act, body)

        @block.vector
        def _(dve):
            def scale_keys(b, g, ci, at_first):
                n = (b * groups + g) * chunks + ci
                if ci % PIECE == 0 and not at_first:
                    dve.wait_ge(s.mean_ready, b * groups + g)
                    dve.wait_ge(s.sum_step, (b * groups + g - 1) * (chunks - 1) + min(ci + PIECE, chunks) - 1)
                dve.wait_ge(s.scores_ready, n + 1)
                add, factor, _ = key_scale
                nc.vector.scalar_tensor_tensor(
                    out=sc[:, g % 2, ci, :].rearrange("p (h q) -> p h q", h=HB),
                    in0=score_ps[(g * chunks + ci) % 4][:, :].rearrange("p (h q) -> p h q", h=HB), scalar=add(b, ci),
                    in1=factor(b, g, ci).unsqueeze(2).to_broadcast([P, HB, P]),
                    op0=ALU.add, op1=ALU.mult).then_inc(s.dve_copied, 1)

            def scale_piece(b, g, p, at_first=False):
                for ci in range(*pieces[p]):
                    if ci in by_dve:
                        scale_keys(b, g, ci, at_first)

            def part_max(b, g, p):
                n = b * groups + g
                a, e = pieces[p]
                for ci in range(max(a, e - 2), e):
                    wait_copied(dve, n, ci)
                if p == 0 and not first(n):
                    dve.wait_ge(s.col_max, n)
                nc.vector.tensor_reduce(part[:, p, :], sc[:, g % 2, a:e, :].rearrange("p c f -> p f c"), X, ALU.max).then_inc(s.part_max, 1)

            def col_max(b, g):
                n = b * groups + g
                dve.wait_ge(s.part_max, (n + 1) * NP)
                if not first(n):
                    dve.wait_ge(s.turned, n)
                nc.vector.tensor_reduce(cmax[:, :], part[:, :, :].rearrange("p c f -> p f c"), X, ALU.max).then_inc(s.col_max, 1)

            def row_max(b, g):
                n = b * groups + g
                dve.wait_ge(s.turned, n + 1)
                nc.vector.tensor_reduce(m[:, :], turn_ps[:, :].rearrange("p (h k) -> p h k", h=HB), X, ALU.max).then_inc(s.row_max, 1)
                dve.wait_ge(s.row_max, n + 2)
                dve.wait_ge(s.max_ready, n + 1)
                nc.vector.tensor_tensor(diag[:, :, :], c.ident[:, :].unsqueeze(1).to_broadcast([P, HB, P]),
                                        m[:, :].unsqueeze(2).to_broadcast([P, HB, P]), ALU.mult).then_inc(s.diag_ready, 1)

            def shift(b, g, p):
                n = b * groups + g
                a, e = pieces[p]
                dve.wait_ge(s.max_ready, n + 2)
                if p == 0:
                    dve.wait_ge(s.part_max, (n + 1) * NP)
                nc.vector.tensor_tensor(sc[:, g % 2, a:e, :], sc[:, g % 2, a:e, :], max_ps[:, :].unsqueeze(1).to_broadcast([P, e - a, HB * P]),
                                        ALU.subtract).then_inc(s.shifted, 1)

            def invert(b, g):
                n = b * groups + g
                dve.wait_ge(s.den_ready, n + 2)
                nc.vector.tensor_scalar(den[:, :], den_ps[:, 0:HB], 1.0 if one_more else 0.0, None, ALU.add).then_inc(s.den_copied, 1)
                dve.wait_ge(s.den_copied, n + 1)
                nc.vector.reciprocal(rec[:, :], den[:, :]).then_inc(s.inverted, 1)
                dve.wait_ge(s.inverted, n + 1)
                dve.wait_ge(s.spread_ready, n + 1)
                nc.vector.tensor_tensor(rdiag[:, :, :], c.ident[:, :].unsqueeze(1).to_broadcast([P, HB, P]),
                                        rec[:, :].unsqueeze(2).to_broadcast([P, HB, P]), ALU.mult).then_inc(s.rdiag_ready, 1)

            def divide(b, g):
                n = b * groups + g
                dve.wait_ge(s.spread_ready, n + 2)
                dve.wait_ge(s.stored, n + 2)
                nc.vector.tensor_copy(spread[:, :], den_ps[:, :]).then_inc(s.spread_copied, 1)
                dve.wait_ge(s.spread_copied, n + 2)
                dve.wait_ge(s.mean_ready, n + 2)
                nc.vector.tensor_tensor(z.qp[:, b, g * HB:(g + 1) * HB, :], out_ps[:, :].rearrange("p (h q) -> p h q", h=HB),
                                        spread[:, :].rearrange("p (h q) -> p h q", h=HB), ALU.mult).then_inc(s.stored, 1)

            def convert_mask(b, p, at_first=False):
                a, e = pieces[p]
                if p == 0:
                    dve.wait_ge(s.mask_in, 16 * b + 16)
                if not at_first:
                    dve.wait_ge(s.scores_ready, (b * groups - 1) * chunks + e)
                nc.vector.tensor_scalar(mb[:, a:e, :], mi[:, a:e, :], 0.0, MASKED, ALU.is_equal, ALU.mult).then_inc(s.mask_ready, 1)

            dve.sem_inc(s.sum_step, chunks - 1)
            dve.sem_inc(s.mean_ready, 1)
            dve.sem_inc(s.max_ready, 1)
            dve.sem_inc(s.den_ready, 1)
            dve.sem_inc(s.stored, 2)
            dve.sem_inc(s.row_max, 1)
            dve.sem_inc(s.spread_copied, 1)
            dve.sem_inc(s.spread_ready, 1)
            dve.sem_inc(s.shifted, 1)
            if mask is not None:
                for p in range(NP):
                    convert_mask(0, p, True)
            for p in range(NP):
                scale_piece(0, 0, p, True)
                part_max(0, 0, p)
            col_max(0, 0)
            row_max(0, 0)
            scale_piece(0, 1, 0, True)

            def body(b, last):
                for g in range(groups):
                    one, two = more(last, g)
                    for p in range(NP):
                        shift(b, g, p)
                        if one and key_scale is not None:
                            if p:
                                scale_piece(*successor(b, g), p)
                            part_max(*successor(b, g), p)
                    for p in range(NP):
                        if one and key_scale is None:
                            part_max(*successor(b, g), p)
                        if mask is not None and g == groups - 2 and not last:
                            convert_mask(b + 1, p)
                    if one:
                        col_max(*successor(b, g))
                        row_max(*successor(b, g))
                    if two:
                        scale_piece(*successor(*successor(b, g)), 0)
                    invert(b, g)
                    divide(b, g)

            over_batches(dve, body)

        @block.gpsimd
        def _(pool):
            def sums(b, g):
                n = b * groups + g
                pool.wait_ge(s.den_ready, n + 1)
                for k, (ci, p) in enumerate(order):
                    if ci == pieces[p][0] and ci:
                        pool.wait_ge(s.exps, n * NP + p + 1)
                    if ci == 1:
                        pool.wait_ge(s.exps, n * NP + 1)
                        nc.gpsimd.tensor_tensor(psum_rows[:, :], sc[:, g % 2, 0, :], sc[:, g % 2, 1, :], ALU.add).then_inc(s.sum_step, 1)
                    elif ci > 1:
                        pool.wait_ge(s.sum_step, (n + 1) * (chunks - 1) + ci - 1)
                        nc.gpsimd.tensor_tensor(psum_rows[:, :], psum_rows[:, :], sc[:, g % 2, ci, :], ALU.add).then_inc(s.sum_step, 1)

            def body(b, last):
                for g in range(groups):
                    sums(b, g)

            over_batches(pool, body)


def output_side(c, z, name, heads, dq, wv, wout, bout=None):
    nc = c.nc
    pairs = heads // 2
    with nc.sbuf_tensor(f"{name}_o", [P, 2, T], F32) as o, stage(nc, name, "values_ready values_copied projected") as (block, s):
        @block.tensor
        def _(pe):
            def values(j):
                if j >= 2:
                    pe.wait_ge(s.values_copied, j - 1)
                for k in range(2):
                    mm = nc.tensor.matmul(c.bank[j % 2][k * dq:(k + 1) * dq, :].rearrange("p (b q) -> p b q", b=B), wv[:, 2 * j + k, :],
                                          z.qp[:, :, 2 * j + k, :], start=True, stop=True)
                mm.then_inc(s.values_ready, 1)

            values(0)
            for j in range(pairs):
                if j + 1 < pairs:
                    values(j + 1)
                pe.wait_ge(s.values_copied, j + 1)
                mm = nc.tensor.matmul(c.bank[2][:, :], wout[:, j, :], o[:, j % 2, :], start=(j == 0), stop=(j == pairs - 1))
                mm.then_inc(s.projected, 1)

        @block.scalar
        def _(act):
            for j in range(pairs):
                act.wait_ge(s.values_ready, j + 1)
                if j >= 2:
                    act.wait_ge(s.projected, j - 1)
                nc.scalar.activation(o[:, j % 2, :], c.bank[j % 2][:, :], ACT.Copy).then_inc(s.values_copied, 1)

        @block.vector
        def _(dve):
            dve.wait_ge(s.projected, pairs)
            nc.vector.scalar_tensor_tensor(out=c.x[:, :], in0=c.bank[2][:, :], scalar=bout if bout is not None else 0.0, in1=c.x[:, :],
                                           op0=ALU.add, op1=ALU.add)


def load(c, name, pairs):
    nc = c.nc
    with stage(nc, name, "loaded") as (block, s):
        @block.sync
        def _(sp):
            for dst, src in pairs:
                sp.dma_start(dst, src).then_inc(s.loaded, 16)
            sp.wait_ge(s.loaded, 16 * len(pairs))


def split_to_dram(c, name, src, dst):
    nc = c.nc
    m, n = src.shape
    with nc.sbuf_tensor(f"{name}_parts", [m, 3, n], BF16) as parts, nc.sbuf_tensor(f"{name}_rest", [m, 2, n], F32) as rest, \
            stage(nc, name, "step stored") as (block, s):
        @block.vector
        def _(dve):
            left = src
            for i in range(3):
                nc.vector.tensor_copy(parts[:, i, :], left).then_inc(s.step, 1)
                dve.wait_ge(s.step, 2 * i + 1)
                if i < 2:
                    nc.vector.tensor_tensor(rest[:, i, :], left, parts[:, i, :], ALU.subtract).then_inc(s.step, 1)
                    dve.wait_ge(s.step, 2 * i + 2)
                    left = rest[:, i, :]

        @block.sync
        def _(sp):
            sp.wait_ge(s.step, 5)
            for i in range(3):
                sp.dma_start(dst[i], parts[:, i, :]).then_inc(s.stored, 16)
            sp.wait_ge(s.stored, 48)


def context_views(d):
    def ctx_t(b, a, e):
        return d.ctxT[:, bass.ds(b * CH + a, e - a) if not isinstance(b, int) else slice(b * CH + a, b * CH + e), :]

    def ctx(b, a, e):
        return d.ctx[:, bass.ds(b * CH + a, e - a) if not isinstance(b, int) else slice(b * CH + a, b * CH + e), :]

    return ctx_t, ctx


def l0_xattn(c):
    nc, d = c.nc, c.d
    with ExitStack() as st:
        heads, dh = 16, 8
        z = Queries(scratch(nc, st, "qp0", [P, B, heads, P], F32))
        rb = scratch(nc, st, "l0_slopes", [9, heads, P], BF16)
        layernorm(c, "l0x_ln", c.x[:, :], c.xn[:, :])
        with ExitStack() as st2:
            wq = scratch(nc, st2, "l0_wq", [P, P], F32)
            wk = scratch(nc, st2, "l0_wk", [P, P], F32)
            hm = scratch(nc, st2, "l0_headmask", [P, heads], F32)
            pos_i = scratch(nc, st2, "l0_pos_i", [P, B * CH], I32)
            pos = scratch(nc, st2, "l0_pos", [P, B * CH], F32)
            q = scratch(nc, st2, "l0_q", [P, T], F32)
            qm = scratch(nc, st2, "l0_qm", [P, 2, T], F32)
            load(c, "l0x_load", [(wq[:, :], d.L0_xattn_W_qT), (wk[:, :], d.L0_xattn_W_k), (hm[:, :], d.headmask),
                                 (pos_i[:, :], d.key_pos), (rb[:, :, :], d.slope_rows)])
            with stage(nc, "l0x_q", "q_ready q_scaled masked carried copied cast") as (block, s):
                @block.tensor
                def _(pe):
                    nc.tensor.matmul(c.bank[0][:, :], wq[:, :], c.xn[:, :], start=True, stop=True).then_inc(s.q_ready, 1)
                    for h in range(heads):
                        pe.wait_ge(s.masked, h + 1)
                        if h >= 2:
                            pe.wait_ge(s.copied, h - 1)
                        nc.tensor.matmul(c.bank[1 + h % 2][:, :], wk[:, :], qm[:, h % 2, :], start=True, stop=True).then_inc(s.carried, 1)

                @block.scalar
                def _(act):
                    act.wait_ge(s.q_ready, 1)
                    nc.scalar.activation(q[:, :], c.bank[0][:, :], ACT.Copy, scale=dh ** -0.5).then_inc(s.q_scaled, 1)
                    act.wait_ge(s.q_scaled, 1)
                    for h in range(heads):
                        if h >= 2:
                            act.wait_ge(s.carried, h - 1)
                        nc.scalar.activation(qm[:, h % 2, :], q[:, :], ACT.Copy, scale=hm[:, h:h + 1]).then_inc(s.masked, 1)

                @block.vector
                def _(dve):
                    nc.vector.tensor_copy(pos[:, :], pos_i[:, :]).then_inc(s.cast, 1)
                    for h in range(heads):
                        dve.wait_ge(s.carried, h + 1)
                        nc.vector.tensor_copy(z.qp[:, :, h, :], c.bank[1 + h % 2][:, :].rearrange("p (b q) -> p b q", b=B)).then_inc(s.copied, 1)

            split_to_dram(c, "l0x_pos", pos[:, :], [d.pos_parts[i] for i in range(3)])

        rows_dram = d.pos_parts.rearrange("i p n -> i (p n)").rearrange("i (b c k) -> i b c k", b=B, k=P)
        with stage(nc, "l0x_rows", "spread") as (block, s):
            @block.sync
            def _(sp):
                for i in range(3):
                    sp.dma_start(d.pos_rows[3 * i:3 * i + 3], rows_dram[i:i + 1].to_broadcast([3, B, CH, P])).then_inc(s.spread, 16)
                sp.wait_ge(s.spread, 48)
        ctx_t, ctx = context_views(d)
        attend_context(c, z, "l0x", heads, ctx_t, ctx, CH, True,
                       rows=(lambda b, a, e: d.pos_rows[:, bass.ds(b, 1), a:e, :].rearrange("r b c k -> r (b c) k"), 9),
                       row_bias=lambda b, g: rb[:, g * HB:(g + 1) * HB, :],
                       mask=lambda b: d.mask_t[:, bass.ds(b * CH, CH), :])
        with ExitStack() as st2:
            wv = scratch(nc, st2, "l0_wv", [P, heads, P], F32)
            wo = scratch(nc, st2, "l0_wo", [P, P], F32)
            o = scratch(nc, st2, "l0_o", [P, T], F32)
            load(c, "l0x_load2", [(wv[:, :, :], d.L0_xattn_W_v_blocks), (wo[:, :], d.L0_xattn_W_oT)])
            with stage(nc, "l0x_out", "values_ready values_copied projected") as (block, s):
                @block.tensor
                def _(pe):
                    for h in range(heads):
                        mm = nc.tensor.matmul(c.bank[0][:, :].rearrange("p (b q) -> p b q", b=B), wv[:, h, :], z.qp[:, :, h, :],
                                              start=(h == 0), stop=(h == heads - 1))
                    mm.then_inc(s.values_ready, 1)
                    pe.wait_ge(s.values_copied, 1)
                    nc.tensor.matmul(c.bank[1][:, :], wo[:, :], o[:, :], start=True, stop=True).then_inc(s.projected, 1)

                @block.scalar
                def _(act):
                    act.wait_ge(s.values_ready, 1)
                    nc.scalar.activation(o[:, :], c.bank[0][:, :], ACT.Copy).then_inc(s.values_copied, 1)

                @block.vector
                def _(dve):
                    dve.wait_ge(s.projected, 1)
                    nc.vector.tensor_tensor(c.x[:, :], c.x[:, :], c.bank[1][:, :], ALU.add)


def l3_xattn(c):
    nc, d = c.nc, c.d
    with ExitStack() as st:
        heads, dq = 8, 64
        z = Queries(scratch(nc, st, "qp9", [P, B, heads, P], F32))
        layernorm(c, "l3x_ln", c.x[:, :], c.xn[:, :])
        with ExitStack() as st2:
            wq = scratch(nc, st2, "l3_wq", [P, heads // 2, 2 * dq], F32)
            wk = scratch(nc, st2, "l3_wk", [2 * dq, heads // 2, P], F32)
            load(c, "l3x_load", [(wq[:, :, :], d.L3_xattn_Wq), (wk[:, :, :], d.L3_xattn_WkT)])
            query_side(c, z, "l3x_q", heads, dq ** -0.5, dq, wq, wk)
        ctx_t, ctx = context_views(d)
        attend_context(c, z, "l3x", heads, ctx_t, ctx, CH, False)
        with ExitStack() as st2:
            wv = scratch(nc, st2, "l3_wv", [P, heads, dq], F32)
            wo = scratch(nc, st2, "l3_wo", [P, heads // 2, P], F32)
            bo = scratch(nc, st2, "l3_bo", [P, 1], F32)
            load(c, "l3x_load2", [(wv[:, :, :], d.L3_xattn_Wv), (wo[:, :, :], d.L3_xattn_Wo), (bo[:, :], d.L3_xattn_bo)])
            output_side(c, z, "l3x_out", heads, dq, wv, wo, bo[:, 0:1])


def l1_xattn(c):
    nc, d = c.nc, c.d
    with ExitStack() as st:
        heads, dq = 16, 64
        z = Queries(scratch(nc, st, "qp3", [P, B, heads, P], F32))
        mrows = scratch(nc, st, "l1_mask_rows", [3, B, P], BF16)
        layernorm(c, "l1x_ln", c.x[:, :], c.xn[:, :])
        with ExitStack() as st2:
            wq = scratch(nc, st2, "l1_wq", [P, heads // 2, 2 * dq], F32)
            wk = scratch(nc, st2, "l1_wk", [2 * dq, heads // 2, P], F32)
            mi = scratch(nc, st2, "l1_mi", [B, P], I32)
            mf = scratch(nc, st2, "l1_mf", [B, P], F32)
            load(c, "l1x_load", [(wq[:, :, :], d.L1_xattn_Wq), (wk[:, :, :], d.L1_xattn_WkT), (mi[:, :], d.query_mask)])
            query_side(c, z, "l1x_q", heads, dq ** -0.5, dq, wq, wk)
            with stage(nc, "l1x_mask", "made") as (block, s):
                @block.vector
                def _(dve):
                    nc.vector.tensor_scalar(mf[:, :], mi[:, :], 1.0, 1e6, ALU.subtract, ALU.mult).then_inc(s.made, 1)
            split_to_dram(c, "l1x_parts", mf[:, :], [d.mask_parts[i] for i in range(3)])
            load(c, "l1x_load_rows", [(mrows[:, :, :], d.mask_parts)])
        ctx_t, ctx = context_views(d)
        attend_context(c, z, "l1x", heads, ctx_t, ctx, CH, False,
                       rows=(lambda b, a, e: d.ones_rows[:, a:e, :], 3),
                       row_bias=lambda b, g: mrows[:, bass.ds(b, 1), :].to_broadcast([3, HB, P]))
        with ExitStack() as st2:
            wv = scratch(nc, st2, "l1_wv", [P, heads, dq], F32)
            wo = scratch(nc, st2, "l1_wo", [P, heads // 2, P], F32)
            bo = scratch(nc, st2, "l1_bo", [P, 1], F32)
            load(c, "l1x_load2", [(wv[:, :, :], d.L1_xattn_Wv), (wo[:, :, :], d.L1_xattn_Wout), (bo[:, :], d.L1_xattn_bout)])
            output_side(c, z, "l1x_out", heads, dq, wv, wo, bo[:, 0:1])



class Steps:

    def __init__(self, eng, sem):
        self.eng, self.sem, self.n = eng, sem, 0

    def __call__(self, instruction):
        self.n += 1
        instruction.then_inc(self.sem, 1)
        self.eng.wait_ge(self.sem, self.n)


def route(c, name, wg, bg, w_t, top, capacity=None):
    nc = c.nc
    with ExitStack() as st:
        def t3(n):
            return scratch(nc, st, f"{name}_{n}", [P, B, E], F32)

        def t2(n):
            return scratch(nc, st, f"{name}_{n}", [P, B], F32)

        score, eq, second, expd = t3("score"), t3("eq"), t3("second"), t3("expd")
        chosen = [t3("chosen0"), t3("chosen1")]
        weighed = [t3("weighed0"), t3("weighed1")]
        top_v = [t2("top0"), t2("top1")]
        rank_top, total, e2 = t2("rank_top"), t2("total"), t2("e2")
        turned_sb = scratch(nc, st, f"{name}_turned", [E, 4, T], F32)
        count = scratch(nc, st, f"{name}_count", [E, 2, T], F32)
        ones_row = scratch(nc, st, f"{name}_ones", [E, T], F32)
        block, s = st.enter_context(stage(nc, name, "scored step to_exp exp_done ready turned out_step"))

        def over_e(v):
            return v[:, :].unsqueeze(2).to_broadcast([P, B, E])

        sources = [weighed[0]] if capacity is None else [chosen[0], chosen[1], weighed[0], weighed[1]]

        @block.tensor
        def _(pe):
            for b in range(B):
                mm = nc.tensor.matmul(c.bank[0][:, b * E:(b + 1) * E], c.xn[:, b * P:(b + 1) * P], wg, start=True, stop=True)
            mm.then_inc(s.scored, 1)
            pe.wait_ge(s.ready, 1)
            for k, src in enumerate(sources):
                for b in range(B):
                    mm = nc.tensor.transpose(c.bank[1 + k][0:E, b * P:(b + 1) * P], src[:, b, :], c.ident[:, :])
            mm.then_inc(s.turned, 1)

        @block.scalar
        def _(act):
            if top == 1:
                return
            act.wait_ge(s.to_exp, 1)
            if capacity is None:
                nc.scalar.activation(e2[:, :], e2[:, :], ACT.Exp).then_inc(s.exp_done, 1)
            else:
                nc.scalar.activation(expd[:, :, :], expd[:, :, :], ACT.Exp).then_inc(s.exp_done, 1)

        @block.vector
        def _(dve):
            step = Steps(dve, s.step)
            v = nc.vector

            def choose(src, k):
                step(v.tensor_reduce(top_v[k][:, :], src[:, :, :], X, ALU.max))
                step(v.tensor_tensor(eq[:, :, :], src[:, :, :], over_e(top_v[k]), ALU.is_equal))
                step(v.tensor_tensor(eq[:, :, :], eq[:, :, :], c.rank[:, :, :], ALU.mult))
                step(v.tensor_reduce(rank_top[:, :], eq[:, :, :], X, ALU.max))
                step(v.tensor_tensor(chosen[k][:, :, :], eq[:, :, :], over_e(rank_top), ALU.is_equal))

            def without_first(src):
                step(v.scalar_tensor_tensor(out=second[:, :, :], in0=chosen[0][:, :, :], scalar=MASKED, in1=src[:, :, :],
                                            op0=ALU.mult, op1=ALU.add))

            dve.wait_ge(s.scored, 1)
            ps = c.bank[0][:, 0:B * E].rearrange("p (b e) -> p b e", b=B)
            if bg is not None:
                step(v.tensor_tensor(score[:, :, :], ps, bg.unsqueeze(1).to_broadcast([P, B, E]), ALU.add))
            else:
                step(v.tensor_copy(score[:, :, :], ps))
            if capacity is not None:
                step(v.tensor_reduce(total[:, :], score[:, :, :], X, ALU.max))
                v.tensor_tensor(expd[:, :, :], score[:, :, :], over_e(total), ALU.subtract).then_inc(s.to_exp, 1)
                dve.wait_ge(s.exp_done, 1)
                step(v.tensor_reduce(total[:, :], expd[:, :, :], X, ALU.add))
                step(v.reciprocal(total[:, :], total[:, :]))
                step(v.tensor_tensor(score[:, :, :], expd[:, :, :], over_e(total), ALU.mult))
            choose(score, 0)
            if top == 2:
                without_first(score)
                choose(second, 1)
                if capacity is None:
                    v.tensor_tensor(e2[:, :], top_v[1][:, :], top_v[0][:, :], ALU.subtract).then_inc(s.to_exp, 1)
                    dve.wait_ge(s.exp_done, 1)
                    step(v.tensor_scalar(total[:, :], e2[:, :], 1.0, None, ALU.add))
                    step(v.reciprocal(top_v[0][:, :], total[:, :]))
                    step(v.tensor_tensor(top_v[1][:, :], e2[:, :], top_v[0][:, :], ALU.mult))
                else:
                    step(v.tensor_tensor(total[:, :], top_v[0][:, :], top_v[1][:, :], ALU.add))
                    step(v.reciprocal(total[:, :], total[:, :]))
                    step(v.tensor_tensor(top_v[0][:, :], top_v[0][:, :], total[:, :], ALU.mult))
                    step(v.tensor_tensor(top_v[1][:, :], top_v[1][:, :], total[:, :], ALU.mult))
                step(v.tensor_tensor(weighed[0][:, :, :], chosen[0][:, :, :], over_e(top_v[0]), ALU.mult))
                if capacity is None:
                    step(v.tensor_tensor(weighed[1][:, :, :], chosen[1][:, :, :], over_e(top_v[1]), ALU.mult))
                    v.tensor_tensor(weighed[0][:, :, :], weighed[0][:, :, :], weighed[1][:, :, :], ALU.add).then_inc(s.ready, 1)
                else:
                    v.tensor_tensor(weighed[1][:, :, :], chosen[1][:, :, :], over_e(top_v[1]), ALU.mult).then_inc(s.ready, 1)
            else:
                v.tensor_copy(weighed[0][:, :, :], chosen[0][:, :, :]).then_inc(s.ready, 1)
            if capacity is None:
                dve.wait_ge(s.turned, 1)
                step(v.tensor_copy(w_t[:, :], c.bank[1][0:E, :]))
                return
            step(v.memset(ones_row[:, :], 1.0))
            dve.wait_ge(s.turned, 1)
            for k in range(4):
                step(v.tensor_copy(turned_sb[:, k, :], c.bank[1 + k][0:E, :]))
            for k in range(2):
                step(v.tensor_tensor_scan(count[:, k, :], ones_row[:, :], turned_sb[:, k, :], 0.0, ALU.mult, ALU.add))
                step(v.scalar_tensor_tensor(out=turned_sb[:, 2 + k, :], in0=count[:, k, :], scalar=float(capacity), in1=turned_sb[:, 2 + k, :],
                                            op0=ALU.is_le, op1=ALU.mult))
            step(v.tensor_tensor(w_t[:, :], turned_sb[:, 2, :], turned_sb[:, 3, :], ALU.add))


def experts(c, name, w_t, up, gate, down, blocks, width, b1=None, b2=None):
    nc = c.nc
    F = blocks * width
    glu = gate is not None
    RING = 4
    with ExitStack() as st:
        wu = scratch(nc, st, f"{name}_wu", [P, 2, F], F32)
        wg = scratch(nc, st, f"{name}_wg", [P, 2, F], F32) if glu else None
        wd = scratch(nc, st, f"{name}_wd", [width, 2, blocks, P], F32)
        spread = scratch(nc, st, f"{name}_spread", [P, E, T], F32)
        act_out = scratch(nc, st, f"{name}_act", [width, RING, T], F32)
        prod = scratch(nc, st, f"{name}_prod", [width, RING, T], F32) if glu else None
        hidden = scratch(nc, st, f"{name}_hidden", [width, RING, T], F32)
        block, s = st.enter_context(stage(nc, name, "w_in0 w_in1 up_used down_used spread_ready spread_copied "
                                                    "up_ready activated multiplied weighed accumulated"))
        w_in = [s.w_in0, s.w_in1]
        acc = c.bank[7]
        banks = 2 if glu else RING
        up_ps, gate_ps = c.bank[0:banks], c.bank[2:4]
        spread_ps = c.bank[5:7]
        per = 2 * blocks
        LAG = 2
        loads = 48 if glu else 32

        @block.sync
        def _(sp):
            with sp.Fori(0, E // 2) as i:
                for k in range(2):
                    sp.wait_ge(s.up_used, 2 * i + k + 1)
                    sp.dma_start(wu[:, k, :], up[:, bass.ds(2 * i + k, 1), :].rearrange("p o f -> p (o f)")).then_inc(w_in[k], 16)
                    if glu:
                        sp.dma_start(wg[:, k, :], gate[:, bass.ds(2 * i + k, 1), :].rearrange("p o f -> p (o f)")).then_inc(w_in[k], 16)
                    sp.wait_ge(s.down_used, 2 * i + k + 1)
                    sp.dma_start(wd[:, k, :, :], down[:, bass.ds(2 * i + k, 1), :, :].rearrange("p o j d -> p (o j) d")).then_inc(w_in[k], 16)

        @block.tensor
        def _(pe):
            pe.sem_inc(s.up_used, 2)
            pe.sem_inc(s.down_used, 2)
            pe.sem_inc(s.accumulated, RING)
            for e in range(E):
                if e >= 2:
                    pe.wait_ge(s.spread_copied, e - 1)
                nc.tensor.matmul(spread_ps[e % 2][:, :], c.select[0:E, e, :], w_t[:, :], start=True, stop=True).then_inc(s.spread_ready, 1)
            nc.tensor.matmul(acc[:, :], c.ident[:, :], c.x[:, :], start=True, stop=False, skip_group_check=True)
            if b2 is not None:
                nc.tensor.matmul(acc[:, :], b2, w_t[:, :], start=False, stop=False, skip_group_check=True)

            def first(i, k):
                slot, j = divmod(k, blocks)
                n = i * per + k
                if j == 0:
                    pe.wait_ge(w_in[slot], loads * i + loads)
                pe.wait_ge(s.multiplied if glu else s.activated, n + 1 + RING - banks)
                if glu:
                    nc.tensor.matmul(gate_ps[k % banks][0:width, :], wg[:, slot, j * width:(j + 1) * width], c.xn[:, :], start=True, stop=True)
                nc.tensor.matmul(up_ps[k % banks][0:width, :], wu[:, slot, j * width:(j + 1) * width], c.xn[:, :],
                                 start=True, stop=True).then_inc(s.up_ready, 1)
                if j == blocks - 1:
                    pe.wait_ge(s.up_ready, n + 1)
                    pe.sem_inc(s.up_used, 1)

            def second(i, k, end):
                slot, j = divmod(k, blocks)
                n = i * per + k
                pe.wait_ge(s.weighed, n + 1 + RING)
                nc.tensor.matmul(acc[:, :], wd[:, slot, j, :], hidden[:, k % RING, :], start=False, stop=end,
                                 skip_group_check=True).then_inc(s.accumulated, 1)
                if j == blocks - 1:
                    pe.wait_ge(s.accumulated, n + 1 + RING)
                    pe.sem_inc(s.down_used, 1)

            for k in range(LAG):
                first(0, k)
            with pe.Fori(0, E // 2 - 1) as i:
                for k in range(per):
                    first(*((i, k + LAG) if k + LAG < per else (i + 1, k + LAG - per)))
                    second(i, k, False)
            for k in range(per):
                if k + LAG < per:
                    first(E // 2 - 1, k + LAG)
                second(E // 2 - 1, k, k == per - 1)

        @block.scalar
        def _(act):
            if not glu:
                act.sem_inc(s.activated, RING)
            for e in range(E):
                act.wait_ge(s.spread_ready, e + 1)
                nc.scalar.activation(spread[:, e, :], spread_ps[e % 2][:, :], ACT.Copy).then_inc(s.spread_copied, 1)
            with act.Fori(0, E // 2) as i:
                for k in range(per):
                    slot, j = divmod(k, blocks)
                    n = i * per + k
                    act.wait_ge(s.up_ready, n + 1)
                    act.wait_ge(s.multiplied if glu else s.weighed, n + 1)
                    if glu:
                        nc.scalar.activation(act_out[:, k % RING, :], gate_ps[k % banks][0:width, :], ACT.Silu).then_inc(s.activated, 1)
                    else:
                        nc.scalar.activation(act_out[:, k % RING, :], up_ps[k % banks][0:width, :], ACT.Relu,
                                             bias=b1[:, bass.ds((2 * i + slot) * blocks + j, 1)]).then_inc(s.activated, 1)

        @block.vector
        def _(dve):
            dve.sem_inc(s.weighed, RING)
            if glu:
                dve.sem_inc(s.multiplied, RING)
            dve.wait_ge(s.spread_copied, E)
            with dve.Fori(0, E // 2) as i:
                for k in range(per):
                    slot = k // blocks
                    n = i * per + k
                    src = act_out
                    if glu:
                        dve.wait_ge(s.activated, n + 1)
                        dve.wait_ge(s.weighed, n + 1)
                        nc.vector.tensor_tensor(prod[:, k % RING, :], act_out[:, k % RING, :], up_ps[k % banks][0:width, :],
                                                ALU.mult).then_inc(s.multiplied, 1)
                        src = prod
                        dve.wait_ge(s.multiplied, n + 1 + RING)
                    else:
                        dve.wait_ge(s.activated, n + 1 + RING)
                    dve.wait_ge(s.accumulated, n + 1)
                    nc.vector.tensor_tensor(hidden[:, k % RING, :], src[:, k % RING, :],
                                            spread[0:width, bass.ds(2 * i + slot, 1), :].rearrange("p o t -> p (o t)"),
                                            ALU.mult).then_inc(s.weighed, 1)
            dve.wait_ge(s.accumulated, E * blocks + RING)
            nc.vector.tensor_copy(c.x[:, :], acc[:, :])


def l0_ffn(c):
    nc, d = c.nc, c.d
    layernorm(c, "l0f_ln", c.x[:, :], c.xn[:, :])
    with ExitStack() as st:
        w_t = scratch(nc, st, "l0f_w_t", [E, T], F32)
        wg = scratch(nc, st, "l0f_router", [P, E], F32)
        bg = scratch(nc, st, "l0f_bg", [P, E], F32)
        b1 = scratch(nc, st, "l0f_b1", [P, E * 4], F32)
        b2 = scratch(nc, st, "l0f_b2", [E, P], F32)
        load(c, "l0f_load", [(wg[:, :], d.L0_ffn_Wg), (bg[:, :], d.L0_ffn_bg.to_broadcast([P, E])), (b1[:, :], d.L0_ffn_b1), (b2[:, :], d.L0_ffn_b2)])
        route(c, "l0f_route", wg[:, :], bg[:, :], w_t, 1)
        experts(c, "l0f", w_t, d.L0_ffn_W1, None, d.L0_ffn_W2, 4, P, b1, b2[:, :])


def l1_ffn(c):
    nc, d = c.nc, c.d
    layernorm(c, "l1f_ln", c.x[:, :], c.xn[:, :])
    with ExitStack() as st:
        w_t = scratch(nc, st, "l1f_w_t", [E, T], F32)
        wg = scratch(nc, st, "l1f_router", [P, E], F32)
        load(c, "l1f_load", [(wg[:, :], d.L1_ffn_w_gate)])
        route(c, "l1f_route", wg[:, :], None, w_t, 2)
        experts(c, "l1f", w_t, d.L1_ffn_w_u, d.L1_ffn_w_g, d.L1_ffn_w_d, 2, 88)


def l2_ffn(c):
    nc, d = c.nc, c.d
    layernorm(c, "l2f_ln", c.x[:, :], c.xn[:, :])
    with ExitStack() as st:
        w_t = scratch(nc, st, "l2f_w_t", [E, T], F32)
        wg = scratch(nc, st, "l2f_router", [P, E], F32)
        load(c, "l2f_load", [(wg[:, :], d.L2_ffn_gate_w)])
        route(c, "l2f_route", wg[:, :], None, w_t, 2, capacity=max(int(T / E * 1.25), 1))
        experts(c, "l2f", w_t, d.L2_ffn_wi_up, d.L2_ffn_wi_gate, d.L2_ffn_wo, 4, P)




def l0_attn(c):
    nc, d = c.nc, c.d
    heads, dh = 16, 8
    ROUND = 1.5 * 2.0 ** 23
    TURN = -6.283185
    layernorm(c, "l0a_ln", c.x[:, :], c.xn[:, :])
    with ExitStack() as st:
        def t(name, shape):
            return scratch(nc, st, f"l0a_{name}", shape, F32)

        x2, x1, q, k, v = t("x2", [P, T]), t("x1", [P, T]), t("q", [P, T]), t("k", [P, T]), t("v", [P, B, P])
        bias, bv = t("bias", [P, 13]), t("bv", [P, P])
        w4 = t("w4", [P, 4, P])
        load(c, "l0a_load", [(w4[:, :, :], d.L0_attn_w4), (bias[:, :], d.L0_attn_bias), (bv[:, :], d.L0_attn_bv.to_broadcast([P, P]))])
        BQ, BK, BO, G1, S1, G2, S2, B2, B1 = range(9)

        def col(i):
            return bias[:, i:i + 1]

        layernorm(c, "l0a_ln1", c.xn[:, :], x2[:, :], col(G1), col(S1))
        with stage(nc, "l0a_qkv", "projected") as (block, s):
            @block.tensor
            def _(pe):
                nc.tensor.matmul(c.bank[0][:, :], w4[:, 0, :], x2[:, :], start=True, stop=True).then_inc(s.projected, 1)
                nc.tensor.matmul(c.bank[1][:, :], w4[:, 1, :], x2[:, :], start=True, stop=True).then_inc(s.projected, 1)
                for b in range(B):
                    mm = nc.tensor.matmul(c.bank[2][:, b * P:(b + 1) * P], x2[:, b * P:(b + 1) * P], w4[:, 2, :], start=True, stop=True)
                mm.then_inc(s.projected, 1)

            @block.scalar
            def _(act):
                act.wait_ge(s.projected, 1)
                nc.scalar.activation(q[:, :], c.bank[0][:, :], ACT.Identity, bias=col(BQ))
                act.wait_ge(s.projected, 2)
                nc.scalar.activation(k[:, :], c.bank[1][:, :], ACT.Identity, bias=col(BK))

            @block.vector
            def _(dve):
                dve.wait_ge(s.projected, 3)
                nc.vector.tensor_tensor(v[:, :, :], c.bank[2][:, :].rearrange("p (b j) -> p b j", b=B),
                                        bv[:, :].unsqueeze(1).to_broadcast([P, B, P]), ALU.add)

        with ExitStack() as st2:
            def t2(name, shape):
                return scratch(nc, st2, f"l0a_{name}", shape, F32)

            proj = t2("proj", [P, heads, P])
            fq = t2("fq", [P, 2, heads, T])
            fk = t2("fk", [P, 2, B, heads * P])
            turns, whole, fold = t2("turns", [P, 3, T]), t2("whole", [P, 3, 2, T]), t2("fold", [P, 3, 2, T])
            kv, out, out_t = t2("kv", [P, 2, T]), t2("out", [P, B, P]), t2("out_t", [P, T])
            load(c, "l0a_load2", [(proj[:, :, :], d.L0_attn_proj)])
            n_items = heads + B * heads // HB
            with stage(nc, "l0a_feat", "angle_ready turns_ready whole_ready dve_whole_ready folded waved kv_ready kv_copied out_ready out_copied "
                                       "turned turned_copied") as (block, s):
                @block.tensor
                def _(pe):
                    for i in range(n_items):
                        if i >= 3:
                            pe.wait_ge(s.turns_ready, i - 2)
                        if i < heads:
                            mm = nc.tensor.matmul(c.bank[i % 3][:, :], proj[:, i, :], q[:, :], start=True, stop=True)
                        else:
                            b, g = divmod(i - heads, heads // HB)
                            mm = nc.tensor.matmul(c.bank[i % 3][:, :].rearrange("p (h m) -> p h m", h=HB), k[:, b * P:(b + 1) * P],
                                                  proj[:, g * HB:(g + 1) * HB, :], start=True, stop=True)
                        mm.then_inc(s.angle_ready, 1)
                    pe.wait_ge(s.waved, n_items)
                    for f in range(2):
                        for b in range(B):
                            for h in range(heads):
                                at = slice(b * P + h * dh, b * P + (h + 1) * dh)
                                mm = nc.tensor.matmul(c.bank[3 + f][:, at], fk[:, f, b, h * P:(h + 1) * P], v[:, b, h * dh:(h + 1) * dh],
                                                      start=True, stop=True)
                        mm.then_inc(s.kv_ready, 1)
                    pe.wait_ge(s.kv_copied, 2)
                    for b in range(B):
                        for h in range(heads):
                            at = slice(b * P + h * dh, b * P + (h + 1) * dh)
                            for f in range(2):
                                mm = nc.tensor.matmul(c.bank[5][:, at], fq[:, f, h, b * P:(b + 1) * P], kv[:, f, at], start=(f == 0), stop=(f == 1))
                    mm.then_inc(s.out_ready, 1)
                    pe.wait_ge(s.out_copied, 1)
                    for b in range(B):
                        mm = nc.tensor.transpose(c.bank[6][:, b * P:(b + 1) * P], out[:, b, :], c.ident[:, :])
                    mm.then_inc(s.turned, 1)
                    pe.wait_ge(s.turned_copied, 1)
                    nc.tensor.matmul(c.bank[7][:, :], w4[:, 3, :], out_t[:, :], start=True, stop=True).then_inc(s.out_ready, 1)

                @block.scalar
                def _(act):
                    def waves(i):
                        act.wait_ge(s.folded, i + 1)
                        if i < heads:
                            cos, sin = fq[:, 0, i, :], fq[:, 1, i, :]
                        else:
                            b, g = divmod(i - heads, heads // HB)
                            cos, sin = fk[:, 0, b, g * T:(g + 1) * T], fk[:, 1, b, g * T:(g + 1) * T]
                        nc.scalar.activation(sin, fold[:, i % 3, 0, :], ACT.Sin, scale=TURN)
                        nc.scalar.activation(cos, fold[:, i % 3, 1, :], ACT.Sin, scale=TURN, bias=c.half_pi[:, 0:1]).then_inc(s.waved, 1)

                    for i in range(n_items):
                        act.wait_ge(s.angle_ready, i + 1)
                        if i >= 3:
                            act.wait_ge(s.folded, i - 2)
                        nc.scalar.activation(turns[:, i % 3, :], c.bank[i % 3][:, :], ACT.Copy,
                                             scale=float(dh ** -0.5 / (2 * np.pi))).then_inc(s.turns_ready, 1)
                        if i >= 2:
                            waves(i - 2)
                    waves(n_items - 2)
                    waves(n_items - 1)
                    for f in range(2):
                        act.wait_ge(s.kv_ready, f + 1)
                        nc.scalar.activation(kv[:, f, :], c.bank[3 + f][:, :], ACT.Copy).then_inc(s.kv_copied, 1)
                    act.wait_ge(s.out_ready, 1)
                    nc.scalar.activation(out[:, :, :], c.bank[5][:, :].rearrange("p (b j) -> p b j", b=B), ACT.Copy, scale=1.0 / P).then_inc(s.out_copied, 1)
                    act.wait_ge(s.turned, 1)
                    nc.scalar.activation(out_t[:, :], c.bank[6][:, :], ACT.Copy).then_inc(s.turned_copied, 1)

                @block.gpsimd
                def _(pool):
                    for i in range(0, n_items, 2):
                        pool.wait_ge(s.turns_ready, i + 1)
                        if i >= 3:
                            pool.wait_ge(s.folded, i - 2)
                        nc.gpsimd.tensor_scalar(whole[:, i % 3, 0, :], turns[:, i % 3, :], ROUND, None, ALU.add).then_inc(s.whole_ready, 1)

                @block.vector
                def _(dve):
                    for i in range(n_items):
                        dve.wait_ge(s.turns_ready, i + 1)
                        nc.vector.tensor_scalar(whole[:, i % 3, 1, :], turns[:, i % 3, :], 0.25, ROUND, ALU.add, ALU.add).then_inc(s.dve_whole_ready, 1)
                        if i % 2:
                            nc.vector.tensor_scalar(whole[:, i % 3, 0, :], turns[:, i % 3, :], ROUND, None, ALU.add).then_inc(s.dve_whole_ready, 1)
                        else:
                            dve.wait_ge(s.whole_ready, i // 2 + 1)
                        dve.wait_ge(s.dve_whole_ready, i + 1 + (i + 1) // 2)
                        if i >= 3:
                            dve.wait_ge(s.waved, i - 2)
                        for f in range(2):
                            mm = nc.vector.scalar_tensor_tensor(out=fold[:, i % 3, f, :], in0=whole[:, i % 3, f, :], scalar=ROUND,
                                                                in1=turns[:, i % 3, :], op0=ALU.subtract, op1=ALU.subtract)
                        mm.then_inc(s.folded, 1)
                    dve.wait_ge(s.out_ready, 2)
                    nc.vector.scalar_tensor_tensor(out=x1[:, :], in0=c.bank[7][:, :], scalar=col(BO), in1=c.xn[:, :], op0=ALU.add, op1=ALU.add)
        layernorm(c, "l0a_ln2", x1[:, :], x2[:, :], col(G2), col(S2))
        w1, w2, hid = t("w1", [P, T]), t("w2", [P, 4, P]), t("hid", [P, 4, T])
        load(c, "l0a_load3", [(w1[:, :], d.L0_attn_w1), (w2[:, :, :], d.L0_attn_w2)])
        with stage(nc, "l0a_ffn", "up_ready relued down_ready added") as (block, s):
            @block.tensor
            def _(pe):
                for j in range(4):
                    nc.tensor.matmul(c.bank[j][:, :], w1[:, j * P:(j + 1) * P], x2[:, :], start=True, stop=True).then_inc(s.up_ready, 1)
                for j in range(4):
                    pe.wait_ge(s.relued, j + 1)
                    mm = nc.tensor.matmul(c.bank[4][:, :], w2[:, j, :], hid[:, j, :], start=(j == 0), stop=(j == 3))
                mm.then_inc(s.down_ready, 1)

            @block.scalar
            def _(act):
                for j in range(4):
                    act.wait_ge(s.up_ready, j + 1)
                    nc.scalar.activation(hid[:, j, :], c.bank[j][:, :], ACT.Relu, bias=col(B1 + j)).then_inc(s.relued, 1)

            @block.vector
            def _(dve):
                nc.vector.tensor_tensor(c.x[:, :], c.x[:, :], x1[:, :], ALU.add).then_inc(s.added, 1)
                dve.wait_ge(s.down_ready, 1)
                dve.wait_ge(s.added, 1)
                nc.vector.scalar_tensor_tensor(out=c.x[:, :], in0=c.bank[4][:, :], scalar=col(B2), in1=c.x[:, :], op0=ALU.add, op1=ALU.add)


def l1_attn(c):
    nc, d = c.nc, c.d
    N, DR, CONV = 16, 8, 4
    layernorm(c, "l1a_ln", c.x[:, :], c.xn[:, :])
    with ExitStack() as st:
        def t(name, shape):
            return scratch(nc, st, f"l1a_{name}", shape, F32)

        x2 = t("x2", [P, T])
        gs = t("gs", [P, 2])
        w_in, conv, w_x, w_dt = t("w_in", [P, 4, P]), t("conv", [P, 2, CONV]), t("w_x", [P, 2, DR + 2 * N]), t("w_dt", [DR, 2, P])
        cols, a_log, w_out = t("cols", [P, 2, 3]), t("a_log", [P, 2, N]), t("w_out", [P, 2, P])
        load(c, "l1a_load", [(gs[:, :], d.L1_attn_ln), (w_in[:, :, :], d.L1_attn_W_in), (conv[:, :, :], d.L1_attn_conv_w),
                             (w_x[:, :, :], d.L1_attn_W_x), (w_dt[:, :, :], d.L1_attn_W_dt), (cols[:, :, :], d.L1_attn_cols),
                             (a_log[:, :, :], d.L1_attn_A_log), (w_out[:, :, :], d.L1_attn_W_out)])
        CB, BDT, DS = range(3)
        layernorm(c, "l1a_ln1", c.xn[:, :], x2[:, :], gs[:, 0:1], gs[:, 1:2])
        PAD = CONV - 1
        u = t("u", [P, 2, B, PAD + P])
        conved, uc, z = t("conved", [P, 2, B, P]), t("uc", [P, 2, T]), t("z", [P, 2, T])
        dt_r, bs, cs = t("dt_r", [DR, T]), t("bs", [N, T]), t("cs", [N, T])
        pre, neg, dt, dtu = t("pre", [P, 2, T]), t("neg", [P, 2, T]), t("dt", [P, 2, T]), t("dtu", [P, 2, T])
        with stage(nc, "l1a_conv", "padded in_ready in_copied conv_step uc_ready x_ready x_copied dt_ready pre_ready folded "
                                   "expd logd step a_ready") as (block, s):
            @block.tensor
            def _(pe):
                for j in range(4):
                    nc.tensor.matmul(c.bank[j][:, :], w_in[:, j, :], x2[:, :], start=True, stop=True).then_inc(s.in_ready, 1)
                pe.wait_ge(s.uc_ready, 2)
                for k, (lo, hi) in enumerate(((0, DR), (DR, DR + N), (DR + N, DR + 2 * N))):
                    for j in range(2):
                        mm = nc.tensor.matmul(c.bank[4 + k][0:hi - lo, :], w_x[:, j, lo:hi], uc[:, j, :], start=(j == 0), stop=(j == 1))
                    mm.then_inc(s.x_ready, 1)
                pe.wait_ge(s.x_copied, 1)
                pe.wait_ge(s.in_copied, 4)
                for j in range(2):
                    nc.tensor.matmul(c.bank[j][:, :], w_dt[:, j, :], dt_r[:, :], start=True, stop=True).then_inc(s.dt_ready, 1)

            @block.gpsimd
            def _(pool):
                nc.gpsimd.memset(u[:, :, :, 0:PAD], 0.0).then_inc(s.padded, 1)

            @block.scalar
            def _(act):
                for j in range(2):
                    act.wait_ge(s.in_ready, j + 1)
                    nc.scalar.activation(u[:, j, :, PAD:], c.bank[j][:, :].rearrange("p (b l) -> p b l", b=B), ACT.Copy).then_inc(s.in_copied, 1)
                for j in range(2):
                    act.wait_ge(s.in_ready, j + 3)
                    nc.scalar.activation(z[:, j, :], c.bank[2 + j][:, :], ACT.Silu).then_inc(s.in_copied, 1)
                for j in range(2):
                    act.wait_ge(s.conv_step, CONV * (j + 1))
                    nc.scalar.activation(uc[:, j, :], conved[:, j, :, :].rearrange("p b l -> p (b l)"), ACT.Silu,
                                         bias=cols[:, j, CB:CB + 1]).then_inc(s.uc_ready, 1)
                for k, dst in enumerate((dt_r, bs, cs)):
                    act.wait_ge(s.x_ready, k + 1)
                    nc.scalar.activation(dst[:, :], c.bank[4 + k][0:dst.shape[0], :], ACT.Copy).then_inc(s.x_copied, 1)
                act.wait_ge(s.folded, 2)
                nc.scalar.activation(neg[:, :, :], neg[:, :, :], ACT.Exp, scale=-1.0).then_inc(s.expd, 1)
                nc.scalar.activation(a_log[:, :, :], a_log[:, :, :], ACT.Exp).then_inc(s.a_ready, 1)
                act.wait_ge(s.expd, 1)
                nc.scalar.activation(neg[:, :, :], neg[:, :, :], ACT.Ln, bias=1.0).then_inc(s.logd, 1)

            @block.vector
            def _(dve):
                v = nc.vector
                dve.wait_ge(s.padded, 1)
                for j in range(2):
                    dve.wait_ge(s.in_copied, j + 1)
                    for k in range(CONV):
                        src = u[:, j, :, k:k + P]
                        if k == 0:
                            v.tensor_scalar(conved[:, j, :, :], src, conv[:, j, 0:1], None, ALU.mult).then_inc(s.conv_step, 1)
                        else:
                            dve.wait_ge(s.conv_step, CONV * j + k)
                            v.scalar_tensor_tensor(out=conved[:, j, :, :], in0=src, scalar=conv[:, j, k:k + 1], in1=conved[:, j, :, :],
                                                   op0=ALU.mult, op1=ALU.add).then_inc(s.conv_step, 1)
                for j in range(2):
                    dve.wait_ge(s.dt_ready, j + 1)
                    v.tensor_scalar(pre[:, j, :], c.bank[j][:, :], cols[:, j, BDT:BDT + 1], None, ALU.add).then_inc(s.pre_ready, 1)
                    dve.wait_ge(s.pre_ready, j + 1)
                    v.scalar_tensor_tensor(out=neg[:, j, :], in0=pre[:, j, :], scalar=-1.0, in1=pre[:, j, :], op0=ALU.mult, op1=ALU.max).then_inc(s.folded, 1)
                step = Steps(dve, s.step)
                dve.wait_ge(s.logd, 1)
                step(v.scalar_tensor_tensor(out=dt[:, :, :], in0=pre[:, :, :], scalar=0.0, in1=neg[:, :, :], op0=ALU.max, op1=ALU.add))
                step(v.tensor_tensor(dtu[:, :, :], dt[:, :, :], uc[:, :, :], ALU.mult))
                dve.wait_ge(s.a_ready, 1)
                step(v.tensor_scalar(a_log[:, :, :], a_log[:, :, :], -1.0, None, ALU.mult))

        decay, drive, state, seen = t("decay", [P, 2, T]), t("drive", [P, 2, T]), t("state", [P, 2, T]), t("seen", [P, 2, T])
        b_sb = t("b_sb", [P, 2, T])
        y = t("y", [P, 2, T])
        items = 2 * N
        with stage(nc, "l1a_scan", "b_ready c_ready b_copied decayed reset driven scanned seen_ready summed y_step projected") as (block, s):
            @block.tensor
            def _(pe):
                def spread(k):
                    if k >= 2:
                        pe.wait_ge(s.b_copied, k - 1)
                    nc.tensor.matmul(c.bank[k % 2][:, :], c.select[:, k, :], bs[:, :], start=True, stop=True).then_inc(s.b_ready, 1)
                    if k >= 2:
                        pe.wait_ge(s.seen_ready, 2 * k - 2)
                    nc.tensor.matmul(c.bank[2 + k % 2][:, :], c.select[:, k, :], cs[:, :], start=True, stop=True).then_inc(s.c_ready, 1)

                spread(0)
                for k in range(N):
                    if k + 1 < N:
                        spread(k + 1)
                    for j in range(2):
                        n = 2 * k + j
                        pe.wait_ge(s.seen_ready, n + 1)
                        nc.tensor.matmul(c.bank[4 + j][:, :], c.ident[:, :], seen[:, n % 2, :], start=(k == 0), stop=(k == N - 1)).then_inc(s.summed, 1)
                pe.wait_ge(s.y_step, 4)
                for j in range(2):
                    mm = nc.tensor.matmul(c.bank[6][:, :], w_out[:, j, :], y[:, j, :], start=(j == 0), stop=(j == 1))
                mm.then_inc(s.projected, 1)

            @block.scalar
            def _(act):
                for k in range(N):
                    act.wait_ge(s.b_ready, k + 1)
                    if k >= 2:
                        act.wait_ge(s.driven, 2 * k - 2)
                    nc.scalar.activation(b_sb[:, k % 2, :], c.bank[k % 2][:, :], ACT.Copy).then_inc(s.b_copied, 1)
                    for j in range(2):
                        n = 2 * k + j
                        if n >= 2:
                            act.wait_ge(s.scanned, n - 1)
                        nc.scalar.activation(decay[:, n % 2, :], dt[:, j, :], ACT.Exp, scale=a_log[:, j, k:k + 1]).then_inc(s.decayed, 1)

            @block.gpsimd
            def _(pool):
                for k in range(N):
                    for j in range(2):
                        n = 2 * k + j
                        pool.wait_ge(s.decayed, n + 1)
                        nc.gpsimd.memset(decay[:, n % 2, :].rearrange("p (b l) -> p b l", b=B)[:, :, 0:1], 0.0).then_inc(s.reset, 1)
                        pool.wait_ge(s.b_copied, k + 1)
                        if n >= 2:
                            pool.wait_ge(s.scanned, n - 1)
                        nc.gpsimd.tensor_tensor(drive[:, n % 2, :], dtu[:, j, :], b_sb[:, k % 2, :], ALU.mult).then_inc(s.driven, 1)

            @block.vector
            def _(dve):
                v = nc.vector
                for k in range(N):
                    for j in range(2):
                        n = 2 * k + j
                        dve.wait_ge(s.reset, n + 1)
                        dve.wait_ge(s.driven, n + 1)
                        if n >= 2:
                            dve.wait_ge(s.seen_ready, n - 1)
                        v.tensor_tensor_scan(state[:, n % 2, :], decay[:, n % 2, :], drive[:, n % 2, :], 0.0, ALU.mult, ALU.add).then_inc(s.scanned, 1)
                        dve.wait_ge(s.scanned, n + 1)
                        dve.wait_ge(s.c_ready, k + 1)
                        if n >= 2:
                            dve.wait_ge(s.summed, n - 1)
                        v.tensor_tensor(seen[:, n % 2, :], state[:, n % 2, :], c.bank[2 + k % 2][:, :], ALU.mult).then_inc(s.seen_ready, 1)
                for j in range(2):
                    dve.wait_ge(s.summed, items)
                    v.scalar_tensor_tensor(out=y[:, j, :], in0=uc[:, j, :], scalar=cols[:, j, DS:DS + 1], in1=c.bank[4 + j][:, :],
                                           op0=ALU.mult, op1=ALU.add).then_inc(s.y_step, 1)
                    dve.wait_ge(s.y_step, 2 * j + 1)
                    v.tensor_tensor(y[:, j, :], y[:, j, :], z[:, j, :], ALU.mult).then_inc(s.y_step, 1)
                v.tensor_tensor(c.x[:, :], c.x[:, :], c.xn[:, :], ALU.add).then_inc(s.y_step, 1)
                dve.wait_ge(s.y_step, 5)
                dve.wait_ge(s.projected, 1)
                v.tensor_tensor(c.x[:, :], c.x[:, :], c.bank[6][:, :], ALU.add)


def l2_attn(c):
    nc, d = c.nc, c.d
    DEPTH = 6
    layernorm(c, "l2a_ln", c.x[:, :], c.xn[:, :])
    with ExitStack() as st:
        def t(name, shape):
            return scratch(nc, st, f"l2a_{name}", shape, F32)

        y, x2 = t("y", [P, T]), t("x2", [P, T])
        w, wo, cols = t("w", [P, 3 * P]), t("wo", [P, P]), t("cols", [P, 3])
        v_t, q, q_tok, k = t("v_t", [P, T]), t("q", [P, B, P]), t("q_tok", [P, B, P]), t("k", [P, B, P])
        top, total = t("top", [P, 2, B]), t("total", [P, 2, B])
        m, out = t("m", [P, B, P]), t("out", [P, T])
        with stage(nc, "l2a_copy", "copied") as (block, s):
            @block.vector
            def _(dve):
                nc.vector.tensor_copy(y[:, :], c.xn[:, :]).then_inc(s.copied, 1)

        with nc.Fori(0, DEPTH) as layer:
            load(c, "l2a_load", [(w[:, :], d.L2_attn_w_qkv[bass.ds(layer, 1)].rearrange("o p n -> (o p) n")),
                                 (wo[:, :], d.L2_attn_w_out[bass.ds(layer, 1)].rearrange("o p n -> (o p) n")),
                                 (cols[:, :], d.L2_attn_cols[bass.ds(layer, 1)].rearrange("o p n -> (o p) n"))])
            layernorm(c, "l2a_lni", y[:, :], x2[:, :], cols[:, 0:1], cols[:, 1:2])
            with stage(nc, "l2a", "projected v_copied top_ready shifted expd total_ready normed turned turned_copied m_ready m_copied "
                                  "out_ready out_copied added") as (block, s):
                def b3(ap):
                    return ap.rearrange("p (b j) -> p b j", b=B)

                def wide(v):
                    return v.unsqueeze(2).to_broadcast([P, B, P])

                @block.tensor
                def _(pe):
                    nc.tensor.matmul(c.bank[0][:, :], w[:, 0:P], x2[:, :], start=True, stop=True).then_inc(s.projected, 1)
                    for b in range(B):
                        mm = nc.tensor.matmul(c.bank[1][:, b * P:(b + 1) * P], x2[:, b * P:(b + 1) * P], w[:, P:2 * P], start=True, stop=True)
                    mm.then_inc(s.projected, 1)
                    nc.tensor.matmul(c.bank[2][:, :], w[:, 2 * P:], x2[:, :], start=True, stop=True).then_inc(s.projected, 1)
                    pe.wait_ge(s.normed, 1)
                    for b in range(B):
                        mm = nc.tensor.transpose(c.bank[3][:, b * P:(b + 1) * P], q[:, b, :], c.ident[:, :])
                    mm.then_inc(s.turned, 1)
                    pe.wait_ge(s.turned_copied, 1)
                    pe.wait_ge(s.normed, 2)
                    for b in range(B):
                        mm = nc.tensor.matmul(c.bank[4][:, b * P:(b + 1) * P], k[:, b, :], q_tok[:, b, :], start=True, stop=True)
                    mm.then_inc(s.m_ready, 1)
                    pe.wait_ge(s.m_copied, 1)
                    pe.wait_ge(s.v_copied, 1)
                    for b in range(B):
                        mm = nc.tensor.matmul(c.bank[5][:, b * P:(b + 1) * P], m[:, b, :], v_t[:, b * P:(b + 1) * P], start=True, stop=True)
                    mm.then_inc(s.out_ready, 1)
                    pe.wait_ge(s.out_copied, 1)
                    nc.tensor.matmul(c.bank[6][:, :], wo[:, :], out[:, :], start=True, stop=True).then_inc(s.out_ready, 1)

                @block.scalar
                def _(act):
                    for n, dst in enumerate((q, k)):
                        act.wait_ge(s.shifted, n + 1)
                        nc.scalar.activation(dst[:, :, :], dst[:, :, :], ACT.Exp).then_inc(s.expd, 1)
                    act.wait_ge(s.projected, 3)
                    nc.scalar.activation(v_t[:, :], c.bank[2][:, :], ACT.Copy).then_inc(s.v_copied, 1)
                    act.wait_ge(s.turned, 1)
                    nc.scalar.activation(q_tok[:, :, :], b3(c.bank[3][:, :]), ACT.Copy).then_inc(s.turned_copied, 1)
                    act.wait_ge(s.m_ready, 1)
                    nc.scalar.activation(m[:, :, :], b3(c.bank[4][:, :]), ACT.Copy).then_inc(s.m_copied, 1)
                    act.wait_ge(s.out_ready, 1)
                    nc.scalar.activation(out[:, :], c.bank[5][:, :], ACT.Copy).then_inc(s.out_copied, 1)

                @block.vector
                def _(dve):
                    v = nc.vector
                    for n, dst in enumerate((q, k)):
                        ps = b3(c.bank[n][:, :])
                        dve.wait_ge(s.projected, n + 1)
                        v.tensor_reduce(top[:, n, :], ps, X, ALU.max).then_inc(s.top_ready, 1)
                        dve.wait_ge(s.top_ready, n + 1)
                        v.tensor_tensor(dst[:, :, :], ps, wide(top[:, n, :]), ALU.subtract).then_inc(s.shifted, 1)
                    for n, dst in enumerate((q, k)):
                        dve.wait_ge(s.expd, n + 1)
                        v.tensor_reduce(total[:, n, :], dst[:, :, :], X, ALU.add).then_inc(s.total_ready, 1)
                        dve.wait_ge(s.total_ready, 2 * n + 1)
                        v.reciprocal(total[:, n, :], total[:, n, :]).then_inc(s.total_ready, 1)
                        dve.wait_ge(s.total_ready, 2 * n + 2)
                        v.tensor_tensor(dst[:, :, :], dst[:, :, :], wide(total[:, n, :]), ALU.mult).then_inc(s.normed, 1)
                    dve.wait_ge(s.out_ready, 2)
                    v.scalar_tensor_tensor(out=y[:, :], in0=c.bank[6][:, :], scalar=cols[:, 2:3], in1=y[:, :], op0=ALU.add, op1=ALU.add)
        with stage(nc, "l2a_add", "added") as (block, s):
            @block.vector
            def _(dve):
                nc.vector.tensor_tensor(c.x[:, :], c.x[:, :], y[:, :], ALU.add)


def normalize_context(c, z, wk):
    nc, d = c.nc, c.d
    heads, dq = 16, 64
    BLOCKS = B * KEYS // T
    with ExitStack() as st:
        def t(name, shape, dt=F32):
            return scratch(nc, st, f"l2n_{name}", shape, dt)

        raw, sq, std, xn, nat = t("raw", [P, 2, T]), t("sq", [P, 2, T]), t("std", [P, 2, T]), t("xn", [P, 2, T]), t("nat", [P, 2, T])
        ksq = t("ksq", [P, 2, heads * dq])
        block, s = st.enter_context(stage(nc, "l2n", "raw_in0 raw_in1 mean_ready centred squared var_ready std_ready inverted scaled normed stored0 stored1 "
                                                     "turned nat_copied nat_stored0 nat_stored1 keys_ready keys_squared reduced"))
        raw_in, stored, nat_stored = [s.raw_in0, s.raw_in1], [s.stored0, s.stored1], [s.nat_stored0, s.nat_stored1]

        def over_blocks(eng, step, tail):
            with eng.Fori(0, BLOCKS // 2 - 1) as i:
                for k in range(2):
                    step(2 * i + k, k, False)
            step(BLOCKS - 2, 0, False)
            step(BLOCKS - 1, 1, True)
            tail()

        @block.sync
        def _(sp):
            def raw_load(n, k):
                sp.dma_start(raw[:, k, :].rearrange("p (j x) -> p j x", j=4), d.ctxT[:, bass.ds(4 * n, 4), :]).then_inc(raw_in[k], 16)

            def put(n, k, latents):
                sp.wait_ge(s.normed, n + 1)
                to_t = d.latT if latents else d.ctxnT[:, bass.ds(4 * n, 4), :]
                sp.dma_start(to_t, xn[:, k, :].rearrange("p (j x) -> p j x", j=4)).then_inc(stored[k], 16)
                sp.wait_ge(s.nat_copied, n + 1)
                to_n = d.lat if latents else d.ctxn[:, bass.ds(4 * n, 4), :]
                sp.dma_start(to_n, nat[:, k, :].rearrange("p (j x) -> p j x", j=4)).then_inc(nat_stored[k], 16)

            raw_load(0, 0)
            raw_load(1, 1)
            with sp.Fori(0, BLOCKS // 2 - 1) as i:
                for k in range(2):
                    sp.wait_ge(s.centred, 2 * i + k + 1)
                    raw_load(2 * i + k + 2, k)
                    put(2 * i + k, k, False)
            for n in range(BLOCKS - 2, BLOCKS + 1):
                put(n, n % 2, n == BLOCKS)
            for sem in (stored, nat_stored):
                sp.wait_ge(sem[0], 16 * (BLOCKS // 2 + 1) + 16)
                sp.wait_ge(sem[1], 16 * (BLOCKS // 2) + 16)

        @block.tensor
        def _(pe):
            def mean(n, k, latents):
                if latents:
                    src = z.latents[:, :]
                else:
                    pe.wait_ge(raw_in[k], 16 * (n // 2 + 1) if isinstance(n, int) else 8 * (n - k) + 16)
                    src = raw[:, k, :]
                nc.tensor.matmul(c.bank[0][:, :], c.mean[:, :], src, start=True, stop=True).then_inc(s.mean_ready, 1)

            def var(n, k):
                pe.wait_ge(s.squared, n + 1)
                nc.tensor.matmul(c.bank[1][:, :], c.mean[:, :], sq[:, k, :], start=True, stop=True).then_inc(s.var_ready, 1)

            def turn(n, k):
                pe.wait_ge(s.normed, n + 1)
                pe.wait_ge(s.nat_copied, n)
                for j in range(4):
                    mm = nc.tensor.transpose(c.bank[2][:, j * P:(j + 1) * P], xn[:, k, j * P:(j + 1) * P], c.ident[:, :])
                mm.then_inc(s.turned, 1)

            def keys(n, k, j):
                pe.wait_ge(s.keys_squared, 4 * n + j + 1)
                for f in range(2):
                    mm = nc.tensor.matmul(c.bank[4 + 2 * (j % 2) + f][:, :], xn[:, k, j * P:(j + 1) * P], wk[:, f * T:(f + 1) * T], start=True, stop=True)
                mm.then_inc(s.keys_ready, 1)

            def step(n, k, latents):
                mean(n + 1, 1 - k, latents)
                keys(n, k, 0)
                keys(n, k, 1)
                var(n + 1, 1 - k)
                keys(n, k, 2)
                keys(n, k, 3)
                turn(n + 1, 1 - k)

            def tail():
                for j in range(4):
                    keys(BLOCKS, 0, j)

            mean(0, 0, False)
            var(0, 0)
            turn(0, 0)
            over_blocks(pe, step, tail)

        @block.scalar
        def _(act):
            def square(n, k):
                act.wait_ge(s.centred, n + 1)
                act.wait_ge(s.var_ready, n)
                nc.scalar.activation(sq[:, k, :], xn[:, k, :], ACT.Square).then_inc(s.squared, 1)

            def root(n, k):
                act.wait_ge(s.var_ready, n + 1)
                nc.scalar.activation(std[:, k, :], c.bank[1][:, :], ACT.Sqrt, bias=c.eps[:, 0:1]).then_inc(s.std_ready, 1)

            def copy(n, k, first):
                act.wait_ge(s.turned, n + 1)
                if not first:
                    act.wait_ge(nat_stored[k], 16 * ((n - k) // 2) + 16 if isinstance(n, int) else 8 * (n - k) + 16)
                nc.scalar.activation(nat[:, k, :], c.bank[2][:, :], ACT.Copy).then_inc(s.nat_copied, 1)

            def key_squares(n, j):
                act.wait_ge(s.keys_ready, 4 * n + j + 1)
                act.wait_ge(s.reduced, 4 * n + j + 1)
                for f in range(2):
                    i = nc.scalar.activation(ksq[:, j % 2, f * T:(f + 1) * T], c.bank[4 + 2 * (j % 2) + f][:, :], ACT.Square)
                i.then_inc(s.keys_squared, 1)

            def step(n, k, latents):
                square(n + 1, 1 - k)
                key_squares(n, 0)
                key_squares(n, 1)
                root(n + 1, 1 - k)
                key_squares(n, 2)
                key_squares(n, 3)
                copy(n + 1, 1 - k, False)

            def tail():
                for j in range(4):
                    key_squares(BLOCKS, j)

            act.sem_inc(s.keys_squared, 2)
            for k in range(2):
                act.sem_inc(stored[k], 16)
                act.sem_inc(nat_stored[k], 16)
            square(0, 0)
            root(0, 0)
            copy(0, 0, True)
            over_blocks(act, step, tail)

        @block.vector
        def _(dve):
            v = nc.vector

            def centre(n, k, latents):
                dve.wait_ge(s.mean_ready, n + 1)
                dve.wait_ge(s.keys_squared, 4 * n - 2 if isinstance(n, int) else 4 * n - 2)
                dve.wait_ge(stored[k], 16 * ((n - k) // 2) + 16 if isinstance(n, int) else 8 * (n - k) + 16)
                src = z.latents[:, :] if latents else raw[:, k, :]
                v.tensor_tensor(xn[:, k, :], src, c.bank[0][:, :], ALU.subtract).then_inc(s.centred, 1)

            def norm(n, k, latents):
                g = z.gains[:, 2:4] if latents else z.gains[:, 0:2]
                dve.wait_ge(s.std_ready, n + 1)
                v.reciprocal(std[:, k, :], std[:, k, :]).then_inc(s.inverted, 1)
                dve.wait_ge(s.inverted, n + 1)
                dve.wait_ge(s.squared, n + 1)
                v.tensor_tensor(xn[:, k, :], xn[:, k, :], std[:, k, :], ALU.mult).then_inc(s.scaled, 1)
                dve.wait_ge(s.scaled, n + 1)
                v.tensor_scalar(xn[:, k, :], xn[:, k, :], g[:, 0:1], g[:, 1:2], ALU.mult, ALU.add).then_inc(s.normed, 1)

            def reduce(n, j):
                dve.wait_ge(s.keys_squared, 4 * n + j + 3)
                v.tensor_reduce(z.key_norm[:, bass.ds(4 * n + j, 1), :].rearrange("p o h -> p (o h)"),
                                ksq[:, j % 2, :].rearrange("p (h j) -> p h j", h=heads), X, ALU.add).then_inc(s.reduced, 1)

            def step(n, k, latents):
                centre(n + 1, 1 - k, latents)
                reduce(n, 0)
                reduce(n, 1)
                norm(n + 1, 1 - k, latents)
                reduce(n, 2)
                reduce(n, 3)

            def tail():
                for j in range(4):
                    reduce(BLOCKS, j)

            dve.sem_inc(s.reduced, 2)
            dve.wait_ge(s.mean_ready, 1)
            v.tensor_tensor(xn[:, 0, :], raw[:, 0, :], c.bank[0][:, :], ALU.subtract).then_inc(s.centred, 1)
            norm(0, 0, False)
            over_blocks(dve, step, tail)


def l2_xattn(c):
    nc, d = c.nc, c.d
    heads, dq = 16, 64
    with ExitStack() as st:
        z = Queries(scratch(nc, st, "qp6", [P, B, heads, P], F32))
        z.key_norm = scratch(nc, st, "l2x_key_norm", [P, B * CH + B, heads], F32)
        key_add = scratch(nc, st, "l2x_key_add", [P, B * CH + B], F32)
        key_shift = scratch(nc, st, "l2x_key_shift", [P, B * CH + B, heads], F32)
        layernorm(c, "l2x_ln", c.x[:, :], c.xn[:, :])
        with ExitStack() as st2:
            z.latents = c.xn
            z.gains = scratch(nc, st2, "l2x_gains", [P, 4], F32)
            wk = scratch(nc, st2, "l2x_wk", [P, heads * dq], F32)
            load(c, "l2x_load0", [(z.gains[:, :], d.L2_xattn_gains), (wk[:, :], d.L2_xattn_Wk)])
            normalize_context(c, z, wk)
        with ExitStack() as st2:
            wq = scratch(nc, st2, "l2x_wq", [P, heads // 2, 2 * dq], F32)
            wk_t = scratch(nc, st2, "l2x_wkt", [2 * dq, heads // 2, P], F32)
            gains = scratch(nc, st2, "l2x_qk_gains", [2 * dq, 3], F32)
            lg = scratch(nc, st2, "l2x_lat_gains", [P, 4], F32)
            mask = scratch(nc, st2, "l2x_mask", [P, B * CH], U8)
            load(c, "l2x_load1", [(wq[:, :, :], d.L2_xattn_Wq), (wk_t[:, :, :], d.L2_xattn_WkT), (gains[:, 0:2], d.L2_xattn_qk_gains),
                                  (mask[:, :], d.key_mask), (lg[:, :], d.L2_xattn_gains)])
            with stage(nc, "l2x_keys", "step rooted gain key_add_made") as (block, s):
                @block.scalar
                def _(act):
                    nc.scalar.activation(z.key_norm[:, :, :], z.key_norm[:, :, :], ACT.Sqrt, scale=1.0 / dq).then_inc(s.rooted, 1)

                @block.vector
                def _(dve):
                    v = nc.vector
                    v.tensor_tensor(gains[:, 2:3], gains[:, 0:1], gains[:, 1:2], ALU.mult).then_inc(s.gain, 1)
                    dve.wait_ge(s.gain, 1)
                    v.tensor_scalar(gains[:, 2:3], gains[:, 2:3], dq ** -0.5, None, ALU.mult)
                    v.memset(key_add[:, B * CH:], 0.0).then_inc(s.key_add_made, 1)
                    v.tensor_scalar(key_add[:, 0:B * CH], mask[:, :], 0.0, MASKED, ALU.is_equal, ALU.mult).then_inc(s.key_add_made, 1)
                    dve.wait_ge(s.key_add_made, 2)
                    dve.wait_ge(s.rooted, 1)
                    step = Steps(dve, s.step)
                    step(v.tensor_scalar(z.key_norm[:, :, :], z.key_norm[:, :, :], 1e-8, None, ALU.max))
                    step(v.reciprocal(z.key_norm[:, :, :], z.key_norm[:, :, :]))
                    step(v.tensor_tensor(key_shift[:, :, :], z.key_norm[:, :, :],
                                         key_add[:, :].unsqueeze(2).to_broadcast([P, B * CH + B, heads]), ALU.mult))
            layernorm(c, "l2x_ln2", c.xn[:, :], c.xn[:, :], lg[:, 2:3], lg[:, 3:4])
            query_side(c, z, "l2x_q", heads, 1.0, dq, wq, wk_t, gains=gains[:, 2:3])

        def ctx_t(b, a, e):
            return d.latT[:, bass.ds(b, 1), :] if a == CH else d.ctxnT[:, bass.ds(b * CH + a, e - a), :]

        def ctx(b, a, e):
            return d.lat[:, bass.ds(b, 1), :] if a == CH else d.ctxn[:, bass.ds(b * CH + a, e - a), :]

        def at(b, ci):
            return B * CH + b if ci == CH else b * CH + ci

        def of_group(per_key, b, g, ci):
            return per_key[:, bass.ds(at(b, ci), 1), g * HB:(g + 1) * HB].rearrange("p o h -> p (o h)")

        attend_context(c, z, "l2x", heads, ctx_t, ctx, CH + 1, False,
                       key_scale=(lambda b, ci: key_add[:, bass.ds(at(b, ci), 1)],
                                  lambda b, g, ci: of_group(z.key_norm, b, g, ci), lambda b, g, ci: of_group(key_shift, b, g, ci)))
        with ExitStack() as st2:
            wv = scratch(nc, st2, "l2_wv", [P, heads, dq], F32)
            wo = scratch(nc, st2, "l2_wo", [P, heads // 2, P], F32)
            bo = scratch(nc, st2, "l2_bo", [P, 1], F32)
            load(c, "l2x_load2", [(wv[:, :, :], d.L2_xattn_Wv), (wo[:, :, :], d.L2_xattn_Wout), (bo[:, :], d.L2_xattn_bout)])
            output_side(c, z, "l2x_out", heads, dq, wv, wo, bo[:, 0:1])


def l3_attn(c):
    nc, d = c.nc, c.d
    heads, dq, NB = 16, 64, 10
    NEG = -1e9
    layernorm(c, "l3a_ln", c.x[:, :], c.xn[:, :])
    with ExitStack() as st:
        def t(name, shape, dt=F32):
            return scratch(nc, st, f"l3a_{name}", shape, dt)

        o = t("o", [dq, heads, T])
        wp, bp = t("wp", [dq, heads, P]), t("bp", [P, 1])
        with ExitStack() as st2:
            def t2(name, shape, dt=F32):
                return scratch(nc, st2, f"l3a_{name}", shape, dt)

            q, k = t2("q", [dq, heads, T]), t2("k", [dq, heads, T])
            causal = t2("causal", [P, P])
            v = t2("v", [P, B, heads * dq])
            with ExitStack() as st3:
                def t3(name, shape, dt=F32):
                    return scratch(nc, st3, f"l3a_{name}", shape, dt)

                wq, wk, wv = t3("wq", [P, heads, dq]), t3("wk", [P, heads, dq]), t3("wv", [P, heads * dq])
                wr, bq, br = t3("wr", [P, heads, NB]), t3("bq", [dq, heads]), t3("br", [NB, heads])
                bnd, r, far = t3("bnd", [NB, P]), t3("r", [NB, 2, T]), t3("far", [P, 2, B, P])
                load(c, "l3a_load", [(wq[:, :, :], d.L3_attn_Wq), (wk[:, :, :], d.L3_attn_Wk), (wv[:, :], d.L3_attn_Wv), (wr[:, :, :], d.L3_attn_Wr),
                                     (bq[:, :], d.L3_attn_bq), (br[:, :], d.L3_attn_br), (bnd[:, :], d.L3_attn_b_nd_rev), (wp[:, :, :], d.L3_attn_Wproj),
                                     (bp[:, :], d.L3_attn_bproj), (causal[:, :], d.causal)])
                with stage(nc, "l3a_qkv", "q_ready k_ready v_ready q_copied k_copied v_copied r_ready r_copied far_ready far_copied far_stored0 far_stored1 scaled") as (block, s):
                    stored = [s.far_stored0, s.far_stored1]

                    @block.tensor
                    def _(pe):
                        def bias(h):
                            pe.wait_ge(s.r_copied, h + 1)
                            if h >= 1:
                                pe.wait_ge(s.far_copied, h)
                            for b in range(B):
                                mm = nc.tensor.matmul(c.bank[7][:, b * P:(b + 1) * P], r[:, h % 2, b * P:(b + 1) * P], bnd[:, :], start=True, stop=True)
                            mm.then_inc(s.far_ready, 1)

                        for h in range(heads):
                            if h >= 1:
                                pe.wait_ge(s.r_copied, h)
                            nc.tensor.matmul(c.bank[6][0:NB, :], wr[:, h, :], c.xn[:, :], start=True, stop=True).then_inc(s.r_ready, 1)
                            if h >= 2:
                                pe.wait_ge(s.q_copied, h - 1)
                            nc.tensor.matmul(c.bank[h % 2][0:dq, :], wq[:, h, :], c.xn[:, :], start=True, stop=True).then_inc(s.q_ready, 1)
                            if h >= 2:
                                pe.wait_ge(s.k_copied, h - 1)
                            nc.tensor.matmul(c.bank[2 + h % 2][0:dq, :], wk[:, h, :], c.xn[:, :], start=True, stop=True).then_inc(s.k_ready, 1)
                            if h < 2 * B:
                                b, f = divmod(h, 2)
                                if h >= 2:
                                    pe.wait_ge(s.v_copied, h - 1)
                                nc.tensor.matmul(c.bank[4 + h % 2][:, :], c.xn[:, b * P:(b + 1) * P], wv[:, f * T:(f + 1) * T], start=True, stop=True).then_inc(s.v_ready, 1)
                            bias(h)

                    @block.scalar
                    def _(act):
                        for h in range(heads):
                            act.wait_ge(s.r_ready, h + 1)
                            if h >= 2:
                                act.wait_ge(s.far_ready, h - 1)
                            nc.scalar.activation(r[:, h % 2, :], c.bank[6][0:NB, :], ACT.Identity, bias=br[:, h:h + 1]).then_inc(s.r_copied, 1)
                            act.wait_ge(s.q_ready, h + 1)
                            nc.scalar.activation(q[:, h, :], c.bank[h % 2][0:dq, :], ACT.Identity, bias=bq[:, h:h + 1]).then_inc(s.q_copied, 1)
                            act.wait_ge(s.far_ready, h + 1)
                            if h >= 2:
                                act.wait_ge(stored[h % 2], 16 * (h // 2))
                            nc.scalar.activation(far[:, h % 2, :, :], c.bank[7][:, :].rearrange("p (b j) -> p b j", b=B), ACT.Copy).then_inc(s.far_copied, 1)

                    @block.vector
                    def _(dve):
                        for h in range(heads):
                            dve.wait_ge(s.k_ready, h + 1)
                            nc.vector.tensor_scalar(k[:, h, :], c.bank[2 + h % 2][0:dq, :], dq ** -0.5, None, ALU.mult).then_inc(s.k_copied, 1)
                            if h < 2 * B:
                                b, f = divmod(h, 2)
                                dve.wait_ge(s.v_ready, h + 1)
                                nc.vector.tensor_copy(v[:, b, f * T:(f + 1) * T], c.bank[4 + h % 2][:, :]).then_inc(s.v_copied, 1)

                    @block.sync
                    def _(sp):
                        for h in range(heads):
                            sp.wait_ge(s.far_copied, h + 1)
                            sp.dma_start(d.far[:, h, :].rearrange("b (t j) -> t b j", j=P), far[:, h % 2, :, :]).then_inc(stored[h % 2], 16)
                        sp.wait_ge(s.far_stored0, 16 * heads // 2)
                        sp.wait_ge(s.far_stored1, 16 * heads // 2)

            W = heads * P
            logits, bias_t, p_t = t2("logits", [P, W]), t2("bias_t", [P, W]), t2("p_t", [P, W])
            top, total = t2("top", [P, heads]), t2("total", [P, heads])

            def h3(ap):
                return ap.rearrange("p (h j) -> p h j", h=heads)

            with stage(nc, "l3a", "bias_in bias_masked logits_ready added top_ready shifted expd total_ready normed turned turned_copied out_ready out_copied") as (block, s):
                @block.sync
                def _(sp):
                    for b in range(B):
                        if b:
                            sp.wait_ge(s.added, 4 * b)
                        for h0 in range(0, heads, 4):
                            src = d.far[b, h0:h0 + 4, P - 1:P - 1 + (P - 1) * P + 1]
                            src = bass.AP(tensor=src.tensor, offset=src.offset, ap=[[P - 1, P], [P * P, 4], [1, P]])
                            sp.dma_start(h3(bias_t[:, :])[:, h0:h0 + 4, :], src).then_inc(s.bias_in, 16)

                @block.tensor
                def _(pe):
                    for b in range(B):
                        cols = slice(b * P, (b + 1) * P)
                        if b:
                            pe.wait_ge(s.added, 4 * b)
                        for h in range(heads):
                            mm = nc.tensor.matmul(c.bank[h // 4][:, (h % 4) * P:(h % 4 + 1) * P], q[:, h, cols], k[:, h, cols], start=True, stop=True)
                            if h % 4 == 3:
                                mm.then_inc(s.logits_ready, 1)
                        pe.wait_ge(s.normed, b + 1)
                        for g in range(4):
                            pe.wait_ge(s.turned_copied, 4 * b + g) if b or g else None
                            for h in range(4 * g, 4 * g + 4):
                                mm = nc.tensor.transpose(c.bank[4 + g % 2][:, (h % 4) * P:(h % 4 + 1) * P], logits[:, h * P:(h + 1) * P], c.ident[:, :])
                            mm.then_inc(s.turned, 1)
                        for g in range(4):
                            pe.wait_ge(s.turned_copied, 4 * b + g + 1)
                            n = 4 * b + g
                            if n >= 2:
                                pe.wait_ge(s.out_copied, n - 1)
                            for h in range(4 * g, 4 * g + 4):
                                mm = nc.tensor.matmul(c.bank[6 + g % 2][0:dq, (h % 4) * P:(h % 4 + 1) * P], v[:, b, h * dq:(h + 1) * dq],
                                                      p_t[:, h * P:(h + 1) * P], start=True, stop=True)
                            mm.then_inc(s.out_ready, 1)

                @block.scalar
                def _(act):
                    for b in range(B):
                        act.wait_ge(s.shifted, b + 1)
                        nc.scalar.activation(logits[:, :], logits[:, :], ACT.Exp).then_inc(s.expd, 1)
                        for g in range(4):
                            act.wait_ge(s.turned, 4 * b + g + 1)
                            if b:
                                act.wait_ge(s.out_ready, 4 * b)
                            nc.scalar.activation(p_t[:, g * T:(g + 1) * T], c.bank[4 + g % 2][:, :], ACT.Copy).then_inc(s.turned_copied, 1)
                        for g in range(4):
                            act.wait_ge(s.out_ready, 4 * b + g + 1)
                            nc.scalar.activation(o[:, 4 * g:4 * g + 4, b * P:(b + 1) * P], c.bank[6 + g % 2][0:dq, :].rearrange("p (h j) -> p h j", h=4),
                                                 ACT.Copy).then_inc(s.out_copied, 1)

                @block.vector
                def _(dve):
                    vec = nc.vector
                    for b in range(B):
                        dve.wait_ge(s.bias_in, 64 * (b + 1))
                        vec.tensor_tensor(h3(bias_t[:, :]), h3(bias_t[:, :]), causal[:, :].unsqueeze(1).to_broadcast([P, heads, P]), ALU.add).then_inc(s.bias_masked, 1)
                        dve.wait_ge(s.bias_masked, b + 1)
                        if b:
                            dve.wait_ge(s.turned, 4 * b)
                        for g in range(4):
                            dve.wait_ge(s.logits_ready, 4 * b + g + 1)
                            vec.tensor_tensor(logits[:, g * T:(g + 1) * T], c.bank[g][:, :], bias_t[:, g * T:(g + 1) * T], ALU.add).then_inc(s.added, 1)
                        dve.wait_ge(s.added, 4 * b + 4)
                        vec.tensor_reduce(top[:, :], h3(logits[:, :]), X, ALU.max).then_inc(s.top_ready, 1)
                        dve.wait_ge(s.top_ready, b + 1)
                        vec.tensor_tensor(h3(logits[:, :]), h3(logits[:, :]), top[:, :].unsqueeze(2).to_broadcast([P, heads, P]), ALU.subtract).then_inc(s.shifted, 1)
                        dve.wait_ge(s.expd, b + 1)
                        vec.tensor_reduce(total[:, :], h3(logits[:, :]), X, ALU.add).then_inc(s.total_ready, 1)
                        dve.wait_ge(s.total_ready, 2 * b + 1)
                        vec.reciprocal(total[:, :], total[:, :]).then_inc(s.total_ready, 1)
                        dve.wait_ge(s.total_ready, 2 * b + 2)
                        vec.tensor_tensor(h3(logits[:, :]), h3(logits[:, :]), total[:, :].unsqueeze(2).to_broadcast([P, heads, P]), ALU.mult).then_inc(s.normed, 1)
        with stage(nc, "l3a_out", "projected") as (block, s):
            @block.tensor
            def _(pe):
                for h in range(heads):
                    mm = nc.tensor.matmul(c.bank[0][:, :], wp[:, h, :], o[:, h, :], start=(h == 0), stop=(h == heads - 1))
                mm.then_inc(s.projected, 1)

            @block.vector
            def _(dve):
                dve.wait_ge(s.projected, 1)
                nc.vector.scalar_tensor_tensor(out=c.x[:, :], in0=c.bank[0][:, :], scalar=bp[:, 0:1], in1=c.x[:, :], op0=ALU.add, op1=ALU.add)


def butterflies(c, name, m, coef, swap, order, cols):
    nc = c.nc
    INNER = 7
    with nc.sbuf_tensor(f"{name}_own", [P, 2, 4, cols], F32) as own, nc.sbuf_tensor(f"{name}_swapped", [P, 4, cols], F32) as swapped, \
            stage(nc, name, "swapped owned mixed copied") as (block, s):
        n_in = [0]
        main = cols - cols % P

        @block.tensor
        def _(pe):
            done = 0
            for n, stg in enumerate(order):
                if stg >= INNER:
                    continue
                if n:
                    pe.wait_ge(s.mixed, n)
                for b in range(4):
                    mm = nc.tensor.matmul(c.bank[b][:, 0:cols], swap[:, stg, :], m[:, b, :], start=True, stop=True)
                mm.then_inc(s.swapped, 1)

        @block.vector
        def _(dve):
            inner = 0
            for n, stg in enumerate(order):
                if n:
                    dve.wait_ge(s.mixed, n)
                for b in range(4):
                    i = nc.vector.tensor_scalar(own[:, n % 2, b, :], m[:, b, :], coef[:, stg, b, 0:1], None, ALU.mult)
                i.then_inc(s.owned, 1)
                if stg < INNER:
                    inner += 1
                    dve.wait_ge(s.swapped, inner)
                else:
                    nc.vector.tensor_copy(swapped[:, :, :], m[:, :, :]).then_inc(s.copied, 1)
                    dve.wait_ge(s.copied, n + 1 - inner)
                dve.wait_ge(s.owned, n + 1)
                for b in range(4):
                    other = c.bank[b][:, 0:cols] if stg < INNER else swapped[:, b ^ (1 << (stg - INNER)), :]
                    i = nc.vector.scalar_tensor_tensor(out=m[:, b, :], in0=other, scalar=coef[:, stg, b, 1:2], in1=own[:, n % 2, b, :],
                                                       op0=ALU.mult, op1=ALU.add)
                i.then_inc(s.mixed, 1)


def l3_ffn(c):
    nc, d = c.nc, c.d
    STAGES = 9
    layernorm(c, "l3f_ln", c.x[:, :], c.xn[:, :])
    with ExitStack() as st:
        def t(name, shape, dt=F32):
            return scratch(nc, st, f"l3f_{name}", shape, dt)

        up, down = t("up", [P, 4, P + 1]), t("down", [P, 4, P])
        swap, cu, cd = t("swap", [P, 7, P]), t("cu", [P, STAGES, 4, 2]), t("cd", [P, STAGES, 4, 2])
        ub, bc = t("ub", [P, 4]), t("bc", [P, 3])
        load(c, "l3f_load", [(up[:, :, :], d.L3_ffn_up), (down[:, :, :], d.L3_ffn_W_con), (swap[:, :, :], d.swap), (cu[:, :, :, :], d.L3_ffn_up_coef),
                             (cd[:, :, :, :], d.L3_ffn_down_coef), (ub[:, :], d.L3_ffn_up_bias), (bc[:, 0:2], d.L3_ffn_out_bias)])
        butterflies(c, "l3f_up", up, cu, swap, range(STAGES), P + 1)
        butterflies(c, "l3f_down", down, cd, swap, range(STAGES)[::-1], P)
        up_t, hid = t("up_t", [P, 4, P]), t("hid", [P, 4, T])
        with stage(nc, "l3f", "turned turned_copied biased up_ready waved down_ready") as (block, s):
            @block.tensor
            def _(pe):
                for j in range(4):
                    mm = nc.tensor.transpose(c.bank[0][:, j * P:(j + 1) * P], up[:, j, 0:P], c.ident[:, :])
                mm.then_inc(s.turned, 1)
                pe.wait_ge(s.turned_copied, 1)
                for j in range(4):
                    nc.tensor.matmul(c.bank[1 + j][:, :], up_t[:, j, :], c.xn[:, :], start=True, stop=True).then_inc(s.up_ready, 1)
                for j in range(4):
                    pe.wait_ge(s.waved, j + 1)
                    mm = nc.tensor.matmul(c.bank[5][:, :], down[:, j, :], hid[:, j, :], start=(j == 0), stop=(j == 3))
                mm.then_inc(s.down_ready, 1)

            @block.scalar
            def _(act):
                act.wait_ge(s.turned, 1)
                nc.scalar.activation(up_t[:, :, :], c.bank[0][:, :].rearrange("p (j i) -> p j i", j=4), ACT.Copy).then_inc(s.turned_copied, 1)
                act.wait_ge(s.biased, 1)
                for j in range(4):
                    act.wait_ge(s.up_ready, j + 1)
                    nc.scalar.activation(hid[:, j, :], c.bank[1 + j][:, :], ACT.Gelu, bias=ub[:, j:j + 1]).then_inc(s.waved, 1)

            @block.vector
            def _(dve):
                nc.vector.tensor_tensor(ub[:, :], ub[:, :], up[:, :, P], ALU.add).then_inc(s.biased, 1)
                nc.vector.tensor_tensor(bc[:, 2:3], bc[:, 0:1], bc[:, 1:2], ALU.add).then_inc(s.biased, 1)
                dve.wait_ge(s.biased, 2)
                dve.wait_ge(s.down_ready, 1)
                nc.vector.scalar_tensor_tensor(out=c.x[:, :], in0=c.bank[5][:, :], scalar=bc[:, 2:3], in1=c.x[:, :], op0=ALU.add, op1=ALU.add)


BUILDERS = {6: l2_xattn, 10: l3_attn, 11: l3_ffn, 1: l0_attn, 4: l1_attn, 7: l2_attn, 0: l0_xattn, 2: l0_ffn, 3: l1_xattn, 5: l1_ffn, 8: l2_ffn, 9: l3_xattn}


def program(nc, d):
    c = Chip(nc, d)
    setup(c)
    for k in SUBLAYERS:
        BUILDERS[k](c)
    store(c)



def layout(i):
    a = {k: np.asarray(v) for k, v in i.items()}

    def col(v):
        return v.reshape(-1, P).T

    r = {}
    r["xT"] = a["x"].reshape(T, P).T
    r["ctxT"] = a["ctx_1024"].reshape(B * CH, P, P).transpose(2, 0, 1)
    r["ctx"] = a["ctx_1024"].reshape(B * CH, P, P).transpose(1, 0, 2)
    r["key_pos"] = a["itok_BxS2_1_8191"].reshape(P, B * CH)
    r["mask_t"] = a["mask_BxSxS2_if1"].reshape(B, P, CH, P).transpose(3, 0, 2, 1).reshape(P, B * CH, P)
    r["query_mask"] = a["mask_BxS_ik0"]
    r["L0_xattn_W_qT"] = a["L0_xattn_W_q"].T
    r["L0_xattn_W_k"] = a["L0_xattn_W_k"]
    blocks = np.zeros((P, 16, P), a["L0_xattn_W_v"].dtype)
    for h in range(16):
        blocks[:, h, 8 * h:8 * h + 8] = a["L0_xattn_W_v"].T[:, 8 * h:8 * h + 8]
    r["L0_xattn_W_v_blocks"] = blocks
    r["L0_xattn_W_oT"] = a["L0_xattn_W_o"].T
    wkv = a["L1_xattn_Wkv"]
    r["L1_xattn_Wq"] = a["L1_xattn_Wq"].reshape(P, 8, P)
    r["L1_xattn_WkT"] = wkv[:, :1024].reshape(P, 8, P).transpose(2, 1, 0)
    r["L1_xattn_Wv"] = wkv[:, 1024:].reshape(P, 16, 64)
    r["L1_xattn_Wout"] = a["L1_xattn_Wout"].reshape(8, P, P).transpose(1, 0, 2)
    r["L1_xattn_bout"] = col(a["L1_xattn_bout"])
    r["L3_xattn_Wq"] = a["L3_xattn_Wq"].reshape(P, 4, P)
    r["L3_xattn_WkT"] = a["L3_xattn_Wk"].reshape(P, 4, P).transpose(2, 1, 0)
    r["L3_xattn_Wv"] = a["L3_xattn_Wv"].reshape(P, 8, 64)
    r["L3_xattn_Wo"] = a["L3_xattn_Wo"].reshape(4, P, P).transpose(1, 0, 2)
    r["L3_xattn_bo"] = col(a["L3_xattn_bo"])
    r["L0_ffn_Wg"] = a["L0_ffn_Wg"]
    r["L0_ffn_bg"] = a["L0_ffn_bg"][None]
    r["L0_ffn_W1"] = a["L0_ffn_W1"].transpose(1, 0, 2)
    r["L0_ffn_b1"] = a["L0_ffn_b1"].reshape(E * 4, P).T
    r["L0_ffn_W2"] = a["L0_ffn_W2"].reshape(E, 4, P, P).transpose(2, 0, 1, 3)
    r["L0_ffn_b2"] = a["L0_ffn_b2"]
    r["L1_ffn_w_gate"] = a["L1_ffn_w_gate"]
    r["L1_ffn_w_g"] = a["L1_ffn_w_g"].transpose(1, 0, 2)
    r["L1_ffn_w_u"] = a["L1_ffn_w_u"].transpose(1, 0, 2)
    r["L1_ffn_w_d"] = a["L1_ffn_w_d"].reshape(E, 2, 88, P).transpose(2, 0, 1, 3)
    r["L2_ffn_gate_w"] = a["L2_ffn_gate_w"].T
    r["L2_ffn_wi_gate"] = a["L2_ffn_wi_gate"].transpose(2, 0, 1)
    r["L2_ffn_wi_up"] = a["L2_ffn_wi_up"].transpose(2, 0, 1)
    r["L2_ffn_wo"] = a["L2_ffn_wo"].transpose(2, 0, 1).reshape(4, P, E, P).transpose(1, 2, 0, 3)
    n = "L0_attn_"
    r["L0_attn_w4"] = np.stack([a[n + w] for w in ("wq", "wk", "wv", "wo")], 1)
    r["L0_attn_bias"] = np.stack([a[n + w] for w in ("bq", "bk", "bo", "ln1_g", "ln1_b", "ln2_g", "ln2_b", "b2")]
                                 + list(a[n + "b1"].reshape(4, P)) + [a[n + "bv"]], 1)
    r["L0_attn_bv"] = a[n + "bv"][None]
    proj = np.zeros((P, 16, P), a[n + "proj_mat"].dtype)
    for h in range(16):
        proj[8 * h:8 * h + 8, h, :] = a[n + "proj_mat"]
    r["L0_attn_proj"] = proj
    r["L0_attn_w1"] = a[n + "w1"]
    r["L0_attn_w2"] = a[n + "w2"].reshape(4, P, P).transpose(1, 0, 2)
    n = "L1_attn_"
    r["L1_attn_ln"] = np.stack([a[n + "ln_g"], a[n + "ln_b"]], 1)
    r["L1_attn_W_in"] = a[n + "W_in"].reshape(P, 4, P)
    r["L1_attn_conv_w"] = a[n + "conv_w"].reshape(2, P, 4).transpose(1, 0, 2)
    r["L1_attn_W_x"] = a[n + "W_x"].reshape(2, P, 40).transpose(1, 0, 2)
    r["L1_attn_W_dt"] = a[n + "W_dt"].reshape(8, 2, P)
    r["L1_attn_cols"] = np.stack([a[n + w].reshape(2, P) for w in ("conv_b", "b_dt", "Dskip")], 2).transpose(1, 0, 2)
    r["L1_attn_A_log"] = a[n + "A_log"].reshape(2, P, 16).transpose(1, 0, 2)
    r["L1_attn_W_out"] = a[n + "W_out"].reshape(2, P, P).transpose(1, 0, 2)
    n = "L2_attn_"
    r["L2_attn_w_qkv"] = a[n + "w_qkv"]
    r["L2_attn_w_out"] = a[n + "w_out"]
    r["L2_attn_cols"] = np.stack([a[n + w] for w in ("gamma", "beta", "b_out")], 2)
    n = "L2_xattn_"
    wkv = a[n + "Wkv"]
    r["L2_xattn_gains"] = np.stack([a[n + w] for w in ("ln_x_g", "ln_x_b", "ln_l_g", "ln_l_b")], 1)
    r["L2_xattn_qk_gains"] = np.tile(np.stack([a[n + "qn_g"], a[n + "kn_g"]], 1), (2, 1))
    r["L2_xattn_Wk"] = wkv[:, :1024]
    r["L2_xattn_Wq"] = a["L2_xattn_Wq"].reshape(P, 8, P)
    r["L2_xattn_WkT"] = wkv[:, :1024].reshape(P, 8, P).transpose(2, 1, 0)
    r["L2_xattn_Wv"] = wkv[:, 1024:].reshape(P, 16, 64)
    r["L2_xattn_Wout"] = a[n + "Wout"].reshape(8, P, P).transpose(1, 0, 2)
    r["L2_xattn_bout"] = col(a[n + "bout"])
    r["key_mask"] = a["mask_BxS2_bf1"].view(np.uint8).reshape(B * CH, P).T
    n = "L3_attn_"
    r["L3_attn_Wq"] = a[n + "Wq"].reshape(P, 16, 64)
    r["L3_attn_Wk"] = a[n + "Wk"].reshape(P, 16, 64)
    r["L3_attn_Wv"] = a[n + "Wv"]
    r["L3_attn_Wr"] = a[n + "Wr"].reshape(P, 16, 10)
    r["L3_attn_bq"] = a[n + "bq"].reshape(16, 64).T
    r["L3_attn_br"] = a[n + "br"].reshape(16, 10).T
    r["L3_attn_b_nd_rev"] = a[n + "b_nd"][:, ::-1]
    r["L3_attn_Wproj"] = a[n + "Wproj"].reshape(16, 64, P).transpose(1, 0, 2)
    r["L3_attn_bproj"] = col(a[n + "bproj"])
    n = "L3_ffn_"
    r["L3_ffn_up"] = np.concatenate([a[n + "W_exp"].T, a[n + "b_exp"][:, None]], 1).reshape(4, P, P + 1).transpose(1, 0, 2)
    r["L3_ffn_W_con"] = a[n + "W_con"].reshape(4, P, P).transpose(1, 0, 2)
    hidden = np.arange(512)
    for name, transposed in (("up", False), ("down", True)):
        w = a[n + name + "_weights"]
        coef = np.empty((9, 512, 2), w.dtype)
        for stg in range(9):
            half = 1 << stg
            pair, side = hidden // (2 * half) * half + hidden % half, hidden // half % 2
            coef[stg, :, 0] = w[stg, pair, side, side]
            coef[stg, :, 1] = w[stg, pair, 1 - side, side] if transposed else w[stg, pair, side, 1 - side]
        r[f"L3_ffn_{name}_coef"] = coef.reshape(9, 4, P, 2).transpose(2, 0, 1, 3)
    r["L3_ffn_up_bias"] = a[n + "up_bias"].reshape(4, P).T
    r["L3_ffn_out_bias"] = np.stack([a[n + "b_con"], a[n + "down_bias"]], 1)
    r["causal"] = np.where(np.arange(P)[None, :] <= np.arange(P)[:, None], 0, -1e9).astype(np.float32)
    swap = np.zeros((P, 7, P), np.float32)
    for stg in range(7):
        swap[np.arange(P), stg, np.arange(P) ^ (1 << stg)] = 1
    r["swap"] = swap
    bf = np.dtype("bfloat16")
    sel = np.zeros((16, 16, P), np.float32)
    for e in range(16):
        sel[e, e, :] = 1
    r["select"] = sel
    r["rank"] = np.broadcast_to(np.arange(E, 0, -1, dtype=np.float32), (P, B, E))
    hm = np.zeros((P, 16), np.float32)
    for h in range(16):
        hm[8 * h:8 * h + 8, h] = 1
    r["headmask"] = hm
    ratio = 2.0 ** (-8.0 / 16)
    slope = np.array([ratio ** k for k in range(1, 17)], np.float32)
    parts, left = [], slope
    for _ in range(3):
        parts.append(left.astype(bf))
        left = left - parts[-1].astype(np.float32)
    r["slope_rows"] = np.ascontiguousarray(np.broadcast_to(np.stack(parts * 3)[:, :, None], (9, 16, P)))
    r["ones_rows"] = np.ones((3, CH, P), bf)
    return {k: np.ascontiguousarray(v) for k, v in r.items()}


SCRATCH = {"ctxnT": ([P, B * CH, P], F32), "ctxn": ([P, B * CH, P], F32), "latT": ([P, B, P], F32), "lat": ([P, B, P], F32),
           "far": ([B, 16, P * P], F32),
           "pos_parts": ([3, P, B * CH], BF16), "pos_rows": ([9, B, CH, P], BF16), "mask_parts": ([3, B, P], BF16)}


def kernel(**inputs):
    import concourse.bacc as bacc
    from concourse.bass_utils import run_bass_kernel_spmd

    nc = bacc.Bacc("TRN2", target_bir_lowering=False, num_devices=1)
    arrays = layout(inputs)
    dram = {k: nc.dram_tensor(f"in_{k}", v.shape, mybir.dt.from_np(v.dtype), kind="ExternalInput").ap()
            for k, v in arrays.items()}
    for k, (shape, dt) in SCRATCH.items():
        dram[k] = nc.dram_tensor(f"tmp_{k}", shape, dt, kind="Internal").ap()
    dram["outT"] = nc.dram_tensor("outT", (P, T), F32, kind="ExternalOutput").ap()
    program(nc, namedtuple("Dram", dram)(*dram.values()))
    r = run_bass_kernel_spmd(nc, [{f"in_{k}": v for k, v in arrays.items()}], core_ids=[0])
    return np.ascontiguousarray(r.results[0]["outT"].T).reshape(B, P, P)
```
